# Optimizing a Trainium2 kernel written in Bass

```python
import numpy as np
import jax
import jax.numpy as jnp

def _softmax(x, axis=-1):
    return jax.nn.softmax(x, axis=axis)

def _gelu(x):
    return jax.nn.gelu(x, approximate=True)

def _silu(x):
    return jax.nn.silu(x)

def _sigmoid(x):
    return jax.nn.sigmoid(x)

def _layernorm(x, axis=-1, eps=1e-05):
    m = jnp.mean(x, axis=axis, keepdims=True)
    v = jnp.var(x, axis=axis, keepdims=True)
    return (x - m) / jnp.sqrt(v + eps)

def _scatter_add(tgt, idx, src, axis=0):
    return tgt.at[idx].add(src)

def _segment_sum(src, seg, n):
    return jax.ops.segment_sum(src, seg, n)
kernel_name = 'mk_cond_resid_d4_seqx_r8_14c954'

def setup_inputs(seed: int=0):
    np.random.seed(seed)
    _w = jnp.asarray

    def _rec_inputs():
        import jax
        import jax.numpy as jnp
        _rk = jax.random.key(seed)
        x = -0.0005207 + 1.001 * jax.random.normal(jax.random.fold_in(_rk, 1), (32, 32, 512), jnp.float32)
        _lenS = 32 - jax.random.randint(jax.random.fold_in(_rk, 7), (32,), 0, max(1, 32 // 4) + 1, jnp.int32)
        _lenS2 = 32 - jax.random.randint(jax.random.fold_in(_rk, 8), (32,), 0, max(1, 32 // 4) + 1, jnp.int32)
        itok_Bx16_0_63 = jax.random.randint(jax.random.fold_in(_rk, 11), (32, 16), 0, 64, jnp.int32)
        itok_B_207_1644 = jax.random.randint(jax.random.fold_in(_rk, 12), (32,), 207, 1645, jnp.int32)
        itok_B_2_6 = jax.random.randint(jax.random.fold_in(_rk, 13), (32,), 2, 7, jnp.int32)
        itok_B_0_23 = jax.random.randint(jax.random.fold_in(_rk, 14), (32,), 0, 24, jnp.int32)
        itok_B_0_7 = jax.random.randint(jax.random.fold_in(_rk, 15), (32,), 0, 8, jnp.int32)
        return (x, itok_Bx16_0_63, itok_B_207_1644, itok_B_2_6, itok_B_0_23, itok_B_0_7)
    x, itok_Bx16_0_63, itok_B_207_1644, itok_B_2_6, itok_B_0_23, itok_B_0_7 = _rec_inputs()

    def _L0_cond_setup():
        import jax, jax.numpy as jnp
        import numpy as np
        B, S, HID = (4, 128, 512)
        D, HQ, HK = (128, 32, 8)
        PAGES, PSIZE, NPP = (64, 32, 16)
        THETA = 10000.0
        EPS = 1e-06
        SCALE = 1.0 / float(np.sqrt(D))

        def _rmsnorm(t, w):
            var = jnp.mean(t * t, axis=-1, keepdims=True)
            return t * jax.lax.rsqrt(var + EPS) * w

        def _rope(t, pos):
            inv_freq = 1.0 / THETA ** (jnp.arange(0, D, 2, dtype=jnp.float32) / D)
            freqs = pos[..., None].astype(jnp.float32) * inv_freq
            cos = jnp.cos(freqs)[:, :, None, :]
            sin = jnp.sin(freqs)[:, :, None, :]
            t1, t2 = (t[..., :D // 2], t[..., D // 2:])
            return jnp.concatenate([t1 * cos - t2 * sin, t2 * cos + t1 * sin], axis=-1)
        key = jax.random.key(seed)
        ks = jax.random.split(key, 10)
        x = jax.random.normal(ks[0], (B, S, HID), jnp.float32)
        Wq = jax.random.normal(ks[1], (HQ * D, HID), jnp.float32) * 0.02
        Wk = jax.random.normal(ks[2], (HK * D, HID), jnp.float32) * 0.02
        Wv = jax.random.normal(ks[3], (HK * D, HID), jnp.float32) * 0.02
        Wo = jax.random.normal(ks[4], (HID, HQ * D), jnp.float32) * 0.02
        q_norm_w = jax.random.uniform(ks[5], (D,), jnp.float32)
        k_norm_w = jax.random.uniform(ks[6], (D,), jnp.float32)
        k_cache = jax.random.normal(ks[7], (PAGES, PSIZE, HK, D), jnp.float32)
        v_cache = jax.random.normal(ks[8], (PAGES, PSIZE, HK, D), jnp.float32)
        block_table = jnp.arange(B * NPP, dtype=jnp.int32).reshape(B, NPP)
        cache_seqlens = jax.random.randint(ks[9], (B,), 0, 475).astype(jnp.int32)
        return dict(x=x, Wq=Wq, Wk=Wk, Wv=Wv, Wo=Wo, q_norm_w=q_norm_w, k_norm_w=k_norm_w, k_cache=k_cache, v_cache=v_cache, block_table=block_table, cache_seqlens=cache_seqlens)
    _L0_cond_all = _L0_cond_setup()
    _L0_cond_in = {k: v for k, v in _L0_cond_all.items() if k in ('Wq', 'Wk', 'Wv', 'Wo', 'q_norm_w', 'k_norm_w', 'k_cache', 'v_cache')}
    del _L0_cond_all

    def _L1_cond_setup():
        import jax, jax.numpy as jnp
        import numpy as np
        B, N, H, F = (4, 64, 512, 1376)
        L, R, RANK = (1, 16, 16)
        SCALE = 0.5
        key = jax.random.key(seed)
        ks = jax.random.split(key, 12)
        nrm = lambda k, shape, fan: jax.random.normal(k, shape, jnp.float32) * fan ** (-0.5)
        inp = {'x': jax.random.normal(ks[0], (B, N, H), jnp.float32), 'W_gate': nrm(ks[1], (F, H), H), 'W_up': nrm(ks[2], (F, H), H), 'W_down': nrm(ks[3], (H, F), F), 'A_gate': nrm(ks[4], (L, R, RANK, H), H), 'B_gate': nrm(ks[5], (L, R, F, RANK), RANK), 'A_up': nrm(ks[6], (L, R, RANK, H), H), 'B_up': nrm(ks[7], (L, R, F, RANK), RANK), 'A_down': nrm(ks[8], (L, R, RANK, F), F), 'B_down': nrm(ks[9], (L, R, H, RANK), RANK), 'lora_indices': jax.random.randint(ks[10], (B,), 0, R), 'layer_idx': 0}
        return inp
    _L1_cond_all = _L1_cond_setup()
    _L1_cond_in = {k: v for k, v in _L1_cond_all.items() if k in ('W_gate', 'W_up', 'W_down', 'A_gate', 'B_gate', 'A_up', 'B_up', 'A_down', 'B_down')}
    del _L1_cond_all

    def _L2_cond_setup():
        import jax, jax.numpy as jnp
        import numpy as np
        R = 16
        ALPHA = 32
        SCALING = ALPHA / R
        SLOTS = 32
        IN_F = 512
        OUT_F = 512
        B, T = (8, 128)
        key = jax.random.key(seed)
        k1, k2, k3, k4, k5, k6 = jax.random.split(key, 6)
        x = jax.random.normal(k1, (B, T, IN_F), dtype=jnp.float32)
        adapter_mapping = jax.random.randint(k2, (B,), 0, SLOTS, dtype=jnp.int32)
        W = jax.random.normal(k3, (OUT_F, IN_F), dtype=jnp.float32) * 0.02
        b = jax.random.normal(k4, (OUT_F,), dtype=jnp.float32) * 0.02
        lora_As = jax.random.normal(k5, (SLOTS, IN_F, R), dtype=jnp.float32) * 0.02
        lora_Bs = jax.random.normal(k6, (SLOTS, R, OUT_F), dtype=jnp.float32) * 0.02
        return {'x': x, 'adapter_mapping': adapter_mapping, 'W': W, 'b': b, 'lora_As': lora_As, 'lora_Bs': lora_Bs}
    _L2_cond_all = _L2_cond_setup()
    _L2_cond_in = {k: v for k, v in _L2_cond_all.items() if k in ('W', 'b', 'lora_As', 'lora_Bs')}
    del _L2_cond_all

    def _L3_cond_setup():
        import jax, jax.numpy as jnp
        import numpy as np
        TOP_K = 2
        LANG_BIAS = 5.0
        SCALING = 32.0 / 16.0
        LANGUAGE_PAD_ID = -1
        key = jax.random.key(seed)
        ks = jax.random.split(key, 6)
        B, T, D, O, E, R = (4, 256, 512, 512, 8, 16)
        x = jax.random.normal(ks[0], (B, T, D), dtype=jnp.float32)
        language_ids = jax.random.randint(ks[1], (B,), 0, E).astype(jnp.int64)
        W = jax.random.normal(ks[2], (O, D), dtype=jnp.float32) * (1.0 / np.sqrt(D))
        Wr = jax.random.normal(ks[3], (E, D), dtype=jnp.float32) * (1.0 / np.sqrt(D))
        A = jax.random.normal(ks[4], (E, R, D), dtype=jnp.float32) * (1.0 / np.sqrt(D))
        Bm = jax.random.normal(ks[5], (O, R), dtype=jnp.float32) * 0.0
        Bm = jnp.broadcast_to(Bm, (E, O, R)) + jax.random.normal(ks[5], (E, O, R), dtype=jnp.float32) * 0.02
        return {'x': x, 'language_ids': language_ids, 'W': W, 'Wr': Wr, 'A': A, 'B': Bm}
    _L3_cond_all = _L3_cond_setup()
    _L3_cond_in = {k: v for k, v in _L3_cond_all.items() if k in ('W', 'Wr', 'A', 'B')}
    del _L3_cond_all
    return {'x': x, 'itok_Bx16_0_63': itok_Bx16_0_63, 'itok_B_207_1644': itok_B_207_1644, 'itok_B_2_6': itok_B_2_6, 'itok_B_0_23': itok_B_0_23, 'itok_B_0_7': itok_B_0_7, 'L0_cond_Wq': _L0_cond_in['Wq'], 'L0_cond_Wk': _L0_cond_in['Wk'], 'L0_cond_Wv': _L0_cond_in['Wv'], 'L0_cond_Wo': _L0_cond_in['Wo'], 'L0_cond_q_norm_w': _L0_cond_in['q_norm_w'], 'L0_cond_k_norm_w': _L0_cond_in['k_norm_w'], 'L0_cond_k_cache': _L0_cond_in['k_cache'], 'L0_cond_v_cache': _L0_cond_in['v_cache'], 'L1_cond_W_gate': _L1_cond_in['W_gate'], 'L1_cond_W_up': _L1_cond_in['W_up'], 'L1_cond_W_down': _L1_cond_in['W_down'], 'L1_cond_A_gate': _L1_cond_in['A_gate'], 'L1_cond_B_gate': _L1_cond_in['B_gate'], 'L1_cond_A_up': _L1_cond_in['A_up'], 'L1_cond_B_up': _L1_cond_in['B_up'], 'L1_cond_A_down': _L1_cond_in['A_down'], 'L1_cond_B_down': _L1_cond_in['B_down'], 'L2_cond_W': _L2_cond_in['W'], 'L2_cond_b': _L2_cond_in['b'], 'L2_cond_lora_As': _L2_cond_in['lora_As'], 'L2_cond_lora_Bs': _L2_cond_in['lora_Bs'], 'L3_cond_W': _L3_cond_in['W'], 'L3_cond_Wr': _L3_cond_in['Wr'], 'L3_cond_A': _L3_cond_in['A'], 'L3_cond_B': _L3_cond_in['B']}

def reference(x, itok_Bx16_0_63, itok_B_207_1644, itok_B_2_6, itok_B_0_23, itok_B_0_7, L0_cond_Wq, L0_cond_Wk, L0_cond_Wv, L0_cond_Wo, L0_cond_q_norm_w, L0_cond_k_norm_w, L0_cond_k_cache, L0_cond_v_cache, L1_cond_W_gate, L1_cond_W_up, L1_cond_W_down, L1_cond_A_gate, L1_cond_B_gate, L1_cond_A_up, L1_cond_B_up, L1_cond_A_down, L1_cond_B_down, L2_cond_W, L2_cond_b, L2_cond_lora_As, L2_cond_lora_Bs, L3_cond_W, L3_cond_Wr, L3_cond_A, L3_cond_B):
    import jax
    import jax.numpy as jnp

    def _L0_cond_ref(x, Wq, Wk, Wv, Wo, q_norm_w, k_norm_w, k_cache, v_cache, block_table, cache_seqlens):
        import jax, jax.numpy as jnp
        import numpy as np
        B, S, HID = (4, 128, 512)
        D, HQ, HK = (128, 32, 8)
        PAGES, PSIZE, NPP = (64, 32, 16)
        THETA = 10000.0
        EPS = 1e-06
        SCALE = 1.0 / float(np.sqrt(D))

        def _rmsnorm(t, w):
            var = jnp.mean(t * t, axis=-1, keepdims=True)
            return t * jax.lax.rsqrt(var + EPS) * w

        def _rope(t, pos):
            inv_freq = 1.0 / THETA ** (jnp.arange(0, D, 2, dtype=jnp.float32) / D)
            freqs = pos[..., None].astype(jnp.float32) * inv_freq
            cos = jnp.cos(freqs)[:, :, None, :]
            sin = jnp.sin(freqs)[:, :, None, :]
            t1, t2 = (t[..., :D // 2], t[..., D // 2:])
            return jnp.concatenate([t1 * cos - t2 * sin, t2 * cos + t1 * sin], axis=-1)
        bsz, seqlen, _ = x.shape
        q = jnp.einsum('bsd,ed->bse', x, Wq).reshape(bsz, seqlen, HQ, D)
        k = jnp.einsum('bsd,ed->bse', x, Wk).reshape(bsz, seqlen, HK, D)
        v = jnp.einsum('bsd,ed->bse', x, Wv).reshape(bsz, seqlen, HK, D)
        q = _rmsnorm(q, q_norm_w)
        k = _rmsnorm(k, k_norm_w)
        pos = cache_seqlens[:, None] + jnp.arange(seqlen)[None, :]
        q = _rope(q, pos)
        k = _rope(k, pos)
        L = NPP * PSIZE
        kc = k_cache[block_table].reshape(bsz, L, HK, D)
        vc = v_cache[block_table].reshape(bsz, L, HK, D)
        k_all = jnp.concatenate([kc, k], axis=1)
        v_all = jnp.concatenate([vc, v], axis=1)
        valid_c = jnp.arange(L)[None, :] < cache_seqlens[:, None]
        valid = jnp.concatenate([valid_c, jnp.ones((bsz, seqlen), dtype=bool)], axis=1)
        rep = HQ // HK
        k_all = jnp.repeat(k_all, rep, axis=2)
        v_all = jnp.repeat(v_all, rep, axis=2)
        scores = jnp.einsum('bqhd,bkhd->bhqk', q, k_all) * SCALE
        scores = jnp.where(valid[:, None, None, :], scores, -1e+30)
        probs = jax.nn.softmax(scores, axis=-1)
        o = jnp.einsum('bhqk,bkhd->bqhd', probs, v_all)
        o = o.reshape(bsz, seqlen, HQ * D)
        return jnp.einsum('bse,de->bsd', o, Wo)

    def _L1_cond_ref(x, W_gate, W_up, W_down, A_gate, B_gate, A_up, B_up, A_down, B_down, lora_indices, layer_idx):
        import jax, jax.numpy as jnp
        import numpy as np
        B, N, H, F = (4, 64, 512, 1376)
        L, R, RANK = (1, 16, 16)
        SCALE = 0.5

        def lora_add(base, inp, A, B):
            Ab = A[layer_idx][lora_indices]
            Bb = B[layer_idx][lora_indices]
            t = jnp.einsum('bri,bni->bnr', Ab, inp)
            return base + jnp.einsum('bor,bnr->bno', Bb, t) * SCALE
        gate = lora_add(jnp.einsum('bnh,fh->bnf', x, W_gate), x, A_gate, B_gate)
        up = lora_add(jnp.einsum('bnh,fh->bnf', x, W_up), x, A_up, B_up)
        act = jax.nn.silu(gate) * up
        down = lora_add(jnp.einsum('bnf,hf->bnh', act, W_down), act, A_down, B_down)
        return down

    def _L2_cond_ref(x, adapter_mapping, W, b, lora_As, lora_Bs):
        import jax, jax.numpy as jnp
        import numpy as np
        R = 16
        ALPHA = 32
        SCALING = ALPHA / R
        SLOTS = 32
        IN_F = 512
        OUT_F = 512
        B, T = (8, 128)
        base_out = jnp.einsum('bti,oi->bto', x, W) + b
        A = lora_As[adapter_mapping]
        Bm = lora_Bs[adapter_mapping]
        lora_h = jnp.einsum('bti,bir->btr', x, A)
        lora_out = jnp.einsum('btr,bro->bto', lora_h, Bm)
        return base_out + lora_out * SCALING

    def _L3_cond_ref(x, language_ids, W, Wr, A, B):
        import jax, jax.numpy as jnp
        import numpy as np
        TOP_K = 2
        LANG_BIAS = 5.0
        SCALING = 32.0 / 16.0
        LANGUAGE_PAD_ID = -1
        base = jnp.einsum('btd,od->bto', x, W)
        E = Wr.shape[0]
        logits = jnp.einsum('btd,ed->bte', x.astype(jnp.float32), Wr.astype(jnp.float32))
        expert_targets = language_ids
        valid = expert_targets >= 0
        tgt = jnp.where(valid, expert_targets, 0)
        bias = jax.nn.one_hot(tgt, E, dtype=logits.dtype) * LANG_BIAS
        bias = jnp.where(valid[:, None], bias, 0.0)
        logits = logits + bias[:, None, :]
        topw, topi = jax.lax.top_k(logits, TOP_K)
        weights = jax.nn.softmax(topw, axis=-1)
        gates = jnp.sum(jax.nn.one_hot(topi, E, dtype=weights.dtype) * weights[..., None], axis=-2)
        gates = gates.astype(x.dtype)
        h = jnp.einsum('btd,erd->bter', x, A)
        lora_out = jnp.einsum('bter,bte,eor->bto', h, gates, B)
        return base + SCALING * lora_out
    x = x + _L0_cond_ref(x, L0_cond_Wq, L0_cond_Wk, L0_cond_Wv, L0_cond_Wo, L0_cond_q_norm_w, L0_cond_k_norm_w, L0_cond_k_cache, L0_cond_v_cache, itok_Bx16_0_63, itok_B_207_1644)
    x = x + _L1_cond_ref(x, L1_cond_W_gate, L1_cond_W_up, L1_cond_W_down, L1_cond_A_gate, L1_cond_B_gate, L1_cond_A_up, L1_cond_B_up, L1_cond_A_down, L1_cond_B_down, itok_B_2_6, 0)
    x = x + _L2_cond_ref(x, itok_B_0_23, L2_cond_W, L2_cond_b, L2_cond_lora_As, L2_cond_lora_Bs)
    x = x + _L3_cond_ref(x, itok_B_0_7, L3_cond_W, L3_cond_Wr, L3_cond_A, L3_cond_B)
    return x

_drawn_inputs = setup_inputs


def setup_inputs(seed=0):
    import zlib

    import numpy as np

    out = dict(_drawn_inputs(seed))
    spreads = {}
    factors = {'L0_cond_Wk': 8.0,
     'L0_cond_Wv': 7.012,
     'L0_cond_k_norm_w': 8.0,
     'L2_cond_b': 5.078,
     'L0_cond_k_cache': 3.079}
    for name, (base, spread) in spreads.items():
        noise = np.random.default_rng([zlib.crc32(name.encode()), seed]).standard_normal(out[name].shape)
        drawn = base * np.exp(spread * noise) if base else spread * noise
        out[name] = jnp.asarray(drawn.astype(out[name].dtype))
    for name, factor in factors.items():
        out[name] = (out[name] * factor).astype(out[name].dtype)
    return out
```

```python
from contextlib import ExitStack

import numpy as np

import concourse.bass as bass
from concourse import mybir
from concourse.alu_op_type import AluOpType as ALU

ACT = mybir.ActivationFunctionType
AX = mybir.AxisListType
F32 = mybir.dt.float32
I32 = mybir.dt.int32

P = 128
B, S, HID = 32, 32, 512
TOK = B * S
TILES = TOK // P
SEQ_PER_TILE = P // S
KT = HID // P
D = 128
HQ, HK = 32, 8
REP = HQ // HK
HALVES = 2
HKH = HK // HALVES
HQH = HQ // HALVES
PAGES, PSIZE, NPP = 64, 32, 16
L = PSIZE * NPP
CHUNKS = L // P
KEYS = L + P
STEPS = HALVES * TILES
PAIRS = SEQ_PER_TILE * HKH
BLOCKS = REP * HKH // 4 + 2
SCALE = 1.0 / float(np.sqrt(D))
ATT_EPS = 1e-6
NEG = -1e30
BIG = 3.0e38
F = 1376
FT = -(-F // P)
FLAST = F - (FT - 1) * P
RANK = 16
SEQ_PER_GROUP = P // RANK
GROUPS = B // SEQ_PER_GROUP
GTOK = TOK // GROUPS
E3 = 8
AR = E3 * RANK + E3
NTOK = 512

PI = 3.14159265358979
PI_SAFE = float(np.nextafter(np.float32(np.pi), np.float32(0)))
TWO_PI_1 = 6.28125
TWO_PI_2 = float(np.float32(np.floor((2 * np.pi - TWO_PI_1) * 2**21) / 2**21))
TWO_PI_3 = float(np.float32(2 * np.pi - TWO_PI_1 - TWO_PI_2))
ROUND = 12582912.0

C_IDENT = 0
C_KEY = C_IDENT + P
C_OTHER = C_KEY + L
C_FREQ = C_OTHER + SEQ_PER_TILE * P
C_STEP = C_FREQ + D // 2
C_OWN = C_STEP + 1
C_EXPERT = C_OWN + GTOK
C_FIRST = C_EXPERT + E3
C_COLS = C_FIRST + E3


def constants():
    c = np.zeros((P, C_COLS), np.float32)
    row = np.arange(P)
    c[:, C_IDENT:C_IDENT + P] = np.eye(P)
    c[:, C_KEY:C_KEY + L] = np.arange(L)
    for j in range(SEQ_PER_TILE):
        c[:, C_OTHER + j * P:C_OTHER + (j + 1) * P] = np.where(row // S == j, 0.0, NEG)[None, :]
    c[:, C_FREQ:C_FREQ + D // 2] = (1.0 / np.float32(10000.0) ** (
        np.arange(0, D, 2, dtype=np.float32) / np.float32(D))).astype(np.float32)
    c[:, C_STEP] = row % S
    c[:, C_OWN:C_OWN + GTOK] = row[:, None] // RANK == np.arange(GTOK)[None, :] // S
    c[:, C_EXPERT:C_EXPERT + E3] = np.arange(E3)
    c[:, C_FIRST:C_FIRST + E3] = E3 - np.arange(E3)
    return c


BANK_ORDER = [("block", 0), ("block", 1), ("block", 2), ("turn", 0), ("block", 3), ("turn", 1),
              ("block", 4), ("turn", 2), ("block", 5), ("turn", 3), ("turn", 4), ("out", 0)]
PROLOGUE_USES = 11
MM_BANKS = 3


def bank_use(what, n, tile=None, step=None, last=False):
    i = BANK_ORDER.index((what, n))
    if last:
        u = PROLOGUE_USES + len(BANK_ORDER) * (STEPS - 1)
        return u % MM_BANKS, u // MM_BANKS
    if tile is not None and isinstance(tile, int) and tile == 0:
        return i % MM_BANKS, i // MM_BANKS
    if step is None:
        step = tile - 1
    u = PROLOGUE_USES + i
    return u % MM_BANKS, u // MM_BANKS + (len(BANK_ORDER) // MM_BANKS) * step


def block_slots(n):
    return (2 * n, 2 * n + 1)


def turn_slot(m):
    return 2 * m + 5


def build(nc, t):
    with ExitStack() as whole:
        def sem(name):
            return whole.enter_context(nc.semaphore(name))

        def sb(scope, name, shape, dt=F32):
            return scope.enter_context(nc.sbuf_tensor(name, shape, dt))

        def ps(scope, name, shape, dt=F32):
            return scope.enter_context(nc.psum_tensor(name, shape, dt))

        ident = sb(whole, "ident", [P, P])
        own = sb(whole, "own", [P, GTOK])
        small = sb(whole, "small", [P, 2 * E3])
        y = sb(whole, "y", [P, TILES, HID])

        att = ExitStack()
        wqkv = sb(att, "wqkv", [P, BLOCKS, KT, 512])
        wo = sb(att, "wo", [P, HQH, HID])
        xt = sb(att, "xt", [P, KT, P])
        qT = sb(att, "qT", [P, 2, HKH, SEQ_PER_TILE, P])
        kTn = sb(att, "kTn", [P, 2, HKH, P])
        vN = sb(att, "vN", [P, 2, HKH, D])
        kc = sb(att, "kc", [P, 2, NPP, HKH * PSIZE])
        vc = sb(att, "vc", [P, 2, CHUNKS, HKH * D])
        probs = sb(att, "probs", [P, 2, KEYS])
        pT = sb(att, "pT", [P, 2, KEYS])
        oT = sb(att, "oT", [P, HQH, P])
        mask = sb(att, "mask", [P, 2, KEYS])
        keyno = sb(att, "keyno", [P, L])
        other = sb(att, "other", [P, SEQ_PER_TILE, P])
        cosq = sb(att, "cosq", [P, TILES, D])
        sinq = sb(att, "sinq", [P, TILES, D])
        cosk = sb(att, "cosk", [P, TILES, D])
        sink = sb(att, "sink", [P, TILES, D])
        sq = sb(att, "sq", [P, 512])
        tq = sb(att, "tq", [P, 512])
        rc = sb(att, "rc", [P, 512])
        rs = sb(att, "rs", [P, 512])
        qn = sb(att, "qn", [P, 512])
        rows = sb(att, "rows", [P, 80])
        seqlen_i = rows[:, 0:B].bitcast(I32)
        seqlen = rows[:, B:2 * B]
        minv, psum_, rinv = rows[:, 64:66], rows[:, 66:68], rows[:, 68:70]
        ss, var, rstd, halfs = rows[:, 70:74], None, None, None
        rows2 = sb(att, "rows2", [P, 12])
        var, rstd, halfs = rows2[:, 0:4], rows2[:, 4:8], rows2[:, 8:12]
        table = sb(att, "table", [B, NPP], I32)
        sc = ps(att, "sc", [P, 1024])
        pt_ps = ps(att, "pt_ps", [P, 1024])
        o_ps = ps(att, "o_ps", [P, 512])
        mm = ps(att, "mm", [P, MM_BANKS, 512])
        seqtok_i = sq[:, 0:TILES].bitcast(I32)
        pos = sq[:, TILES:2 * TILES]
        freq = sq[:, 64:128]
        step_ = sq[:, 128:129]
        wq_row, wk_row = sq[:, 129:129 + D], sq[:, 129 + D:129 + 2 * D]
        ang, turns, red, trig = tq, rc, rs, qn
        sin_t, cos_t = probs[:, 0, 0:512], probs[:, 1, 0:512]
        att.close()

        rest = ExitStack()
        xA = sb(rest, "xA", [P, KT, TOK])
        act_t = sb(rest, "act_t", [P, FT, TOK])
        n_a = 2 * B * KT * RANK
        a_gu_raw = act_t[:].rearrange("p f t -> p (f t)")[:, 0:n_a].rearrange("p (w b c) -> p w b c", w=2, b=B)
        a_gu = act_t[:].rearrange("p f t -> p (f t)")[:, n_a:2 * n_a].rearrange(
            "p (w g k c) -> p w g k c", w=2, g=GROUPS, k=KT)
        b_gu = sb(rest, "b_gu", [P, 2, GROUPS, F])
        a_d = sb(rest, "a_d", [P, GROUPS, FT, SEQ_PER_GROUP * RANK])
        b_d = sb(rest, "b_d", [P, GROUPS, HID])
        w_d = sb(rest, "w_d", [P, FT, HID])
        low = sb(rest, "low", [P, 2, TOK])
        w_f = sb(rest, "w_f", [P, 2, 2, KT, P])
        b_f = sb(rest, "b_f", [P, 2, 2, GROUPS, P])
        gated = sb(rest, "gated", [P, 2, NTOK])
        ids = sb(rest, "ids", [1, 2 * B], I32)
        bank = ps(rest, "bank", [P, 8, 512])
        rest.close()
        xB = y[:].rearrange("p t h -> p (t h)").rearrange("p (k t) -> p k t", k=KT)
        a_d_raw = y[:].rearrange("p t h -> p (t h)")[:, 0:B // 2 * FT * RANK].rearrange("p (b c) -> p b c", b=B // 2)
        a2_raw = w_f[:].rearrange("p j w k m -> p (j w k m)").rearrange("p (b c) -> p b c", b=B)
        off = [0]
        pool_ = b_gu[:].rearrange("p w g f -> p (w g f)")

        def carve(n):
            a = off[0]
            off[0] += n
            return pool_[:, a:a + n]

        w2 = carve(KT * HID).rearrange("p (k h) -> p k h", k=KT)
        a2 = carve(B * KT * RANK).rearrange("p (g k c) -> p g k c", g=GROUPS, k=KT)
        b2 = carve(GROUPS * HID).rearrange("p (g h) -> p g h", g=GROUPS)
        bias2 = carve(KT)
        w3 = carve(KT * HID).rearrange("p (k h) -> p k h", k=KT)
        ar3 = carve(KT * AR).rearrange("p (k c) -> p k c", k=KT)
        b3 = carve(HID)
        lang_i = carve(TILES).bitcast(I32)
        assert off[0] <= 2 * GROUPS * F
        off[0] = 0
        pool_ = act_t[:].rearrange("p f t -> p (f t)")
        lang = carve(TILES)
        route = [carve(TILES * E3).rearrange("p (t e) -> p t e", t=TILES) for _ in range(8)]
        route1 = [carve(TILES) for _ in range(8)]
        hg = carve(TILES * P).rearrange("p (t c) -> p t c", t=TILES)
        hgT = carve(TILES * P).rearrange("p (t c) -> p t c", t=TILES)
        xnat = carve(TILES * HID).rearrange("p (t h) -> p t h", t=TILES)
        res = carve(TILES * HID).rearrange("p (t h) -> p t h", t=TILES)

        const_in = sem("const_in")
        setup_in = sem("setup_in")
        table_in = sem("table_in")
        xt_in = sem("xt_in")
        y_in = sem("y_in")
        w_in = [sem(f"w_in{n}") for n in range(BLOCKS)]
        wo_in = sem("wo_in")
        kv_in = [sem(f"kv_in{j}") for j in range(2)]
        setup_v = sem("setup_v")
        setup_a = sem("setup_a")
        tables_made = sem("tables_made")
        block_done = sem("block_done")
        squared = sem("squared")
        summed = sem("summed")
        var_made = sem("var_made")
        rstd_made = sem("rstd_made")
        scaled = sem("scaled")
        cos_done = sem("cos_done")
        sin_done = sem("sin_done")
        roped = sem("roped")
        turned = sem("turned")
        turn_read = sem("turn_read")
        v_read = sem("v_read")
        bank_free = [sem(f"bank_free{j}") for j in range(MM_BANKS)]
        scored = sem("scored")
        new_masked = sem("new_masked")
        mask_made = sem("mask_made")
        masked = sem("masked")
        exped = sem("exped")
        inverted = sem("inverted")
        normed = sem("normed")
        probs_turned = sem("probs_turned")
        vector_went_on = sem("vector_went_on")
        pool_went_on = sem("pool_went_on")
        pt_read = sem("pt_read")
        pv_done = sem("pv_done")
        o_free = sem("o_free")
        out_done = sem("out_done")
        oT_free = sem("oT_free")
        y_added = sem("y_added")

        ad_in = sem("ad_in")
        bd_in = sem("bd_in")
        a2_in = sem("a2_in")
        agu_spread = sem("agu_spread")
        ad_spread = sem("ad_spread")
        a2_spread = sem("a2_spread")
        bgu_in = sem("bgu_in")
        agu_in = sem("agu_in")
        wd_in = sem("wd_in")
        wf_in = [sem(f"wf_in{j}") for j in range(2)]
        bf_in = [sem(f"bf_in{j}") for j in range(2)]
        l23_in = sem("l23_in")
        ids_in = sem("ids_in")
        y_turned = sem("y_turned")
        xa_made = sem("xa_made")
        low_done = sem("low_done")
        low_made = sem("low_made")
        gu_done = sem("gu_done")
        silu_done = sem("silu_done")
        act_made = sem("act_made")
        down_done = sem("down_done")
        xb_made = sem("xb_made")
        low2_done = sem("low2_done")
        low2_made = sem("low2_made")
        lin2_done = sem("lin2_done")
        x2_made = sem("x2_made")
        hr_done = sem("hr_done")
        rv = sem("rv")
        ratio_done = sem("ratio_done")
        hg_made = sem("hg_made")
        hg_turned = sem("hg_turned")
        hgt_made = sem("hgt_made")
        x_turned = sem("x_turned")
        xnat_made = sem("xnat_made")
        lin3_done = sem("lin3_done")
        res_made = sem("res_made")
        out_sent = sem("out_sent")

        def spread_group(raw, group, g, n):
            return (group.rearrange("p k (b r) -> p k b r", b=SEQ_PER_GROUP),
                    raw[:, SEQ_PER_GROUP * g:SEQ_PER_GROUP * (g + 1)].rearrange("p b (k r) -> p k b r", k=n))

        block = whole.enter_context(nc.Block())

        @block.sync
        def _(sp):
            def load_w(n, half):
                sp.dma_start(wqkv[:, n], t["wqkv"][half, n]).then_inc(w_in[n], 16)

            def load_wo(half):
                sp.dma_start(wo[:], t["wo"][half]).then_inc(wo_in, 16)

            def gather(b, half, parity):
                for j in range(NPP):
                    page = sp.value_load(bass.at_runtime_partition(table[0:1, j:j + 1], b),
                                         min_val=0, max_val=PAGES - 1)
                    sp.dma_start(kc[:, parity, j, :],
                                 t["kcache"][half, bass.ds(page, 1)].rearrange("o d k -> (o d) k")
                                 ).then_inc(kv_in[parity], 16)
                    sp.dma_start(vc[PSIZE * (j % 4):PSIZE * (j % 4) + PSIZE, parity, j // 4, :],
                                 t["vcache"][half, bass.ds(page, 1)].rearrange("o k d -> (o k) d")
                                 ).then_inc(kv_in[parity], 16)

            def gather_when_free(b, half, parity):
                sp.wait_ge(pv_done, HKH * (B * half + b - 1))
                gather(b, half, parity)

            sp.dma_start(table[:], t["table"]).then_inc(table_in, 16)
            sp.dma_start(xt[:], t["xt"][0]).then_inc(xt_in, 16)
            load_w(0, 0)
            sp.dma_start(ident[:], t["const"][:, C_IDENT:C_IDENT + P]).then_inc(const_in, 16)
            sp.dma_start(keyno[:], t["const"][:, C_KEY:C_KEY + L]).then_inc(const_in, 16)
            sp.dma_start(other[:].rearrange("p a b -> p (a b)"),
                         t["const"][:, C_OTHER:C_OTHER + SEQ_PER_TILE * P]).then_inc(const_in, 16)
            for n in range(1, BLOCKS):
                load_w(n, 0)
            sp.wait_ge(table_in, 16)
            gather(0, 0, 0)
            load_wo(0)
            sp.dma_start(own[:], t["const"][:, C_OWN:C_OWN + GTOK]).then_inc(const_in, 16)
            sp.dma_start(small[:], t["const"][:, C_EXPERT:C_EXPERT + 2 * E3]).then_inc(const_in, 16)
            sp.dma_start(y[:], t["x"]).then_inc(y_in, 16)
            gather(1, 0, 1)
            with sp.Fori(1, 14) as pair:
                for j in range(2):
                    gather_when_free(2 * pair + j, 0, j)
            for n in range(BLOCKS):
                if n == 4:
                    gather_when_free(28, 0, 0)
                sp.wait_ge(block_done, BLOCKS * (TILES - 1) + n + 1)
                load_w(n, 1)
            for b in range(29, B):
                gather_when_free(b, 0, b % 2)
            for b in range(2):
                gather_when_free(b, 1, b)
            sp.wait_ge(out_done, TILES)
            load_wo(1)
            with sp.Fori(1, B // 2) as pair:
                for j in range(2):
                    gather_when_free(2 * pair + j, 1, j)

            sp.wait_ge(out_done, STEPS)
            sp.wait_ge(y_added, STEPS)
            sp.wait_ge(o_free, STEPS * PAIRS + 1)
            sp.wait_ge(roped, 5 * STEPS)
            sp.dma_start(ids[:], t["ids"]).then_inc(ids_in, 16)
            sp.wait_ge(ids_in, 16)
            id1 = t["a_gu"]
            with sp.Fori(0, B) as b:
                r = sp.value_load(ids[0:1, bass.ds(b, 1)], min_val=0, max_val=15)
                for w in range(2):
                    sp.dma_start(a_gu_raw[:, w, bass.ds(b, 1)].rearrange("p o c -> p (o c)"),
                                 id1[w, bass.ds(r, 1)].rearrange("o p c -> (o p) c")
                                 ).then_inc(agu_in, 16)
            with sp.Fori(0, GROUPS) as g:
                for j in range(SEQ_PER_GROUP):
                    r = sp.value_load(ids[0:1, bass.ds(g * SEQ_PER_GROUP + j, 1)], min_val=0, max_val=15)
                    for w in range(2):
                        sp.dma_start(b_gu[RANK * j:RANK * j + RANK, w, bass.ds(g, 1)].rearrange("p o f -> p (o f)"),
                                     t["b_gu"][w, bass.ds(r, 1)].rearrange("o p c -> (o p) c")
                                     ).then_inc(bgu_in, 16)

            def load_f(f, j, m):
                for w in range(2):
                    sp.dma_start(w_f[:, j, w], t["w_gu"][w, bass.ds(f, 1)].rearrange("o p k m -> (o p) k m")
                                 ).then_inc(wf_in[j], 16)

            def spread_f(f, j, m):
                for w in range(2):
                    sp.dma_start(b_f[:, j, w, :, 0:m], b_gu[:, w, :, bass.ds(f * P, m)]).then_inc(bf_in[j], 16)

            load_f(0, 0, P)
            load_f(1, 1, P)
            sp.wait_ge(bgu_in, 16 * 2 * B)
            spread_f(0, 0, P)
            spread_f(1, 1, P)
            sp.dma_start(w_d[:], t["w_d"]).then_inc(wd_in, 16)
            for h in range(2):
                if h == 0:
                    sp.wait_ge(y_turned, TILES)
                else:
                    sp.wait_ge(ad_spread, GROUPS // 2)
                with sp.Fori(0, B // 2) as b:
                    r = sp.value_load(ids[0:1, bass.ds(b + h * (B // 2), 1)], min_val=0, max_val=15)
                    sp.dma_start(a_d_raw[:, bass.ds(b, 1)].rearrange("p o c -> p (o c)"),
                                 t["a_d"][bass.ds(r, 1)].rearrange("o p c -> (o p) c")).then_inc(ad_in, 16)
            with sp.Fori(0, GROUPS) as g:
                for j in range(SEQ_PER_GROUP):
                    r = sp.value_load(ids[0:1, bass.ds(g * SEQ_PER_GROUP + j, 1)], min_val=0, max_val=15)
                    sp.dma_start(b_d[RANK * j:RANK * j + RANK, bass.ds(g, 1)].rearrange("p o f -> p (o f)"),
                                 t["b_d"][bass.ds(r, 1)].rearrange("o p c -> (o p) c")).then_inc(bd_in, 16)
            with sp.Fori(1, FT // 2) as i:
                for j in range(2):
                    sp.wait_ge(gu_done, 4 * (2 * i + j - 1))
                    load_f(2 * i + j, j, P)
                    spread_f(2 * i + j, j, P)
            sp.wait_ge(gu_done, 4 * (FT - 2))
            load_f(FT - 1, 0, FLAST)
            spread_f(FT - 1, 0, FLAST)
            for j in range(2):
                sp.wait_ge(bf_in[j], 32 * ((FT + 1 - j) // 2))
            sp.dma_start(w2, t["w2"]).then_inc(l23_in, 16)
            sp.dma_start(bias2, t["bias2"]).then_inc(l23_in, 16)
            sp.dma_start(w3, t["w3"]).then_inc(l23_in, 16)
            sp.dma_start(ar3, t["ar3"]).then_inc(l23_in, 16)
            sp.dma_start(b3, t["b3"]).then_inc(l23_in, 16)
            sp.dma_start(lang_i, t["lang"]).then_inc(l23_in, 16)
            sp.wait_ge(gu_done, 4 * FT)
            with sp.Fori(0, B) as b:
                r = sp.value_load(ids[0:1, bass.ds(b + B, 1)], min_val=0, max_val=31)
                sp.dma_start(a2_raw[:, bass.ds(b, 1)].rearrange("p o c -> p (o c)"),
                             t["a2"][bass.ds(r, 1)].rearrange("o p c -> (o p) c")).then_inc(a2_in, 16)
            with sp.Fori(0, GROUPS) as g:
                for j in range(SEQ_PER_GROUP):
                    r = sp.value_load(ids[0:1, bass.ds(g * SEQ_PER_GROUP + j + B, 1)], min_val=0, max_val=31)
                    sp.dma_start(b2[RANK * j:RANK * j + RANK, bass.ds(g, 1)].rearrange("p o f -> p (o f)"),
                                 t["b2"][bass.ds(r, 1)].rearrange("o p c -> (o p) c")).then_inc(l23_in, 16)
            for tile in range(TILES):
                sp.wait_ge(res_made, tile + 1)
                sp.dma_start(t["out"][:, tile, :], res[:, tile, :]).then_inc(out_sent, 16)
            sp.wait_ge(out_sent, 16 * TILES)

        L23_ALL = 16 * (6 + B)

        @block.tensor
        def _(pe):
            def project(n, part, tile, half1):
                b, before = bank_use("block", n, tile=tile)
                if part == 0:
                    if n == 0:
                        pe.wait_ge(xt_in, 16 * (tile + 1))
                    pe.wait_ge(w_in[n], half1)
                    if not isinstance(before, int) or before > 0:
                        pe.wait_ge(bank_free[b], before)
                for k in (2 * part, 2 * part + 1):
                    last = nc.tensor.matmul(mm[:, b], xt[:, k], wqkv[:, n, k], start=(k == 0), stop=(k == KT - 1))
                if part == 1:
                    last.then_inc(block_done, 1)

            def turn(m, tile):
                b, before = bank_use("turn", m, tile=tile)
                pe.wait_ge(roped, 5 * tile + m + 1)
                pe.wait_ge(bank_free[b], before)
                for h in range(4):
                    last = nc.tensor.transpose(mm[:, b, h * P:(h + 1) * P], qn[:, h * P:(h + 1) * P], ident[:])
                last.then_inc(turned, 1)

            def scores(s, k, par):
                b, g = k // HKH, k % HKH
                pe.wait_ge(masked, PAIRS * s + k)
                if k == 0:
                    pe.wait_ge(turn_read, 5 * (s + 1))
                if g == 0:
                    pe.wait_ge(kv_in[b % 2], 16 * 2 * NPP * (2 * s + b // 2 + 1))
                q = qT[:, par, g, b, :]
                nc.tensor.matmul(sc[:, 0:L], q, kc[:, b % 2, :, PSIZE * g:PSIZE * g + PSIZE], start=True, stop=True)
                nc.tensor.matmul(sc[:, L:KEYS], q, kTn[:, par, g, :], start=True, stop=True).then_inc(scored, 1)

            def turn_probs(s, k):
                pe.wait_ge(normed, PAIRS * s + k + 1)
                pe.wait_ge(pt_read, PAIRS * s + k)
                for c in range(KEYS // P):
                    last = nc.tensor.transpose(pt_ps[:, c * P:(c + 1) * P], probs[:, k % 2, c * P:(c + 1) * P], ident[:])
                last.then_inc(probs_turned, 1)

            def values(s, k, par):
                b, g = k // HKH, k % HKH
                pe.wait_ge(pt_read, PAIRS * s + k + 1)
                pe.wait_ge(o_free, PAIRS * s + k + 1)
                for c in range(CHUNKS):
                    nc.tensor.matmul(o_ps[:, 0:P], vc[:, b % 2, c, D * g:D * g + D],
                                     pT[:, k % 2, c * P:(c + 1) * P], start=(c == 0), stop=False)
                if k == 0:
                    pe.wait_ge(v_read, s + 1)
                nc.tensor.matmul(o_ps[:, 0:P], vN[:, par, g, :], pT[:, k % 2, L:KEYS],
                                 start=False, stop=True).then_inc(pv_done, 1)

            def output(s, half1, last):
                b, before = bank_use("out", 0, step=s, last=last)
                pe.wait_ge(o_free, PAIRS * (s + 1) + 1)
                pe.wait_ge(wo_in, half1)
                pe.wait_ge(bank_free[b], before)
                for h in range(HQH):
                    mmul = nc.tensor.matmul(mm[:, b], oT[:, h, :], wo[:, h, :], start=(h == 0), stop=(h == HQH - 1))
                mmul.then_inc(out_done, 1)

            def step(s, par, last=False):
                for k in range(PAIRS):
                    if not last:
                        w_half = 16 * (1 + (s + 1) // TILES)
                        for m in range(5):
                            if turn_slot(m) == k:
                                turn(m, s + 1)
                        for n in range(BLOCKS):
                            if k in block_slots(n):
                                project(n, k - 2 * n, s + 1, w_half)
                    if k + 2 < PAIRS:
                        scores(s, k + 2, par)
                    elif not last:
                        scores(s + 1, k + 2 - PAIRS, 1 - par)
                    values(s, k, par)
                    if k + 1 < PAIRS:
                        turn_probs(s, k + 1)
                    elif not last:
                        turn_probs(s + 1, 0)
                output(s, 16 * (1 + s // TILES), last)

            pe.sem_inc(probs_turned, 2)
            pe.wait_ge(const_in, 16 * 5)
            for what, n in BANK_ORDER[:PROLOGUE_USES]:
                if what == "block":
                    project(n, 0, 0, 16)
                    project(n, 1, 0, 16)
                else:
                    turn(n, 0)
            scores(0, 0, 0)
            scores(0, 1, 0)
            turn_probs(0, 0)
            with pe.Fori(0, STEPS // 2 - 1) as i:
                step(2 * i, 0)
                step(2 * i + 1, 1)
            step(STEPS - 2, 0)
            step(STEPS - 1, 1, last=True)

            pe.wait_ge(y_added, STEPS)
            for tile in range(TILES):
                for k in range(KT):
                    last = nc.tensor.transpose(bank[:, tile, k * P:(k + 1) * P], y[:, tile, k * P:(k + 1) * P], ident[:])
                last.then_inc(y_turned, 1)

            pe.wait_ge(agu_spread, 2 * GROUPS)
            pe.wait_ge(xa_made, TILES)
            for w in range(2):
                for g in range(GROUPS):
                    o = bank[:, 2 * w + g // 2, GTOK * (g % 2):GTOK * (g % 2) + GTOK]
                    for k in range(KT):
                        last = nc.tensor.matmul(o, a_gu[:, w, g, k, :],
                                                xA[:, k, GTOK * g:GTOK * (g + 1)], start=(k == 0), stop=(k == KT - 1))
                    if g % 2 == 1:
                        last.then_inc(low_done, 1)

            def gate_up(f, j, m):
                pe.wait_ge(wf_in[j], 32 * ((f + 2 - j) // 2) if isinstance(f, int) else 16 * (f + 2 - j))
                pe.wait_ge(bf_in[j], 32 * ((f + 2 - j) // 2) if isinstance(f, int) else 16 * (f + 2 - j))
                for n in range(2):
                    for w in range(2):
                        o = bank[0:m, 4 * j + 2 * w + n, :]
                        if not isinstance(f, int) or f >= 2:
                            pe.wait_ge(act_made, 2 * (f - 2) + n + 1)
                        for k in range(KT):
                            nc.tensor.matmul(o, w_f[:, j, w, k, 0:m], xA[:, k, NTOK * n:NTOK * (n + 1)],
                                             start=(k == 0), stop=False)
                        for g in range(2 * n, 2 * n + 2):
                            last = nc.tensor.matmul(o[:, GTOK * (g % 2):GTOK * (g % 2) + GTOK], b_f[:, j, w, g, 0:m],
                                                    low[:, w, GTOK * g:GTOK * (g + 1)], start=False, stop=(g == 2 * n + 1))
                        last.then_inc(gu_done, 1)

            pe.wait_ge(low_made, 4)
            for f in range(2):
                gate_up(f, f, P)
            with pe.Fori(1, FT // 2) as i:
                gate_up(2 * i, 0, P)
                gate_up(2 * i + 1, 1, P)
            gate_up(FT - 1, 0, FLAST)

            pe.wait_ge(act_made, 2 * FT)
            pe.wait_ge(ad_spread, GROUPS)
            for g in range(GROUPS):
                for f in range(FT):
                    m = P if f < FT - 1 else FLAST
                    last = nc.tensor.matmul(bank[:, g // 2, GTOK * (g % 2):GTOK * (g % 2) + GTOK],
                                            a_d[0:m, g, f, :],
                                            act_t[0:m, f, GTOK * g:GTOK * (g + 1)], start=(f == 0), stop=(f == FT - 1))
                if g % 2 == 1:
                    last.then_inc(low_done, 1)
            pe.wait_ge(wd_in, 16)
            pe.wait_ge(bd_in, 16 * B)
            for c in range(KT):
                for n in range(2):
                    i = 2 * c + n
                    o = bank[:, (i + 2) % 8, :]
                    if i >= 6:
                        pe.wait_ge(low_made, 4 + i - 6 + 1)
                    for f in range(FT):
                        m = P if f < FT - 1 else FLAST
                        nc.tensor.matmul(o, w_d[0:m, f, c * P:(c + 1) * P], act_t[0:m, f, NTOK * n:NTOK * (n + 1)],
                                         start=(f == 0), stop=False)
                    pe.wait_ge(low_made, 6)
                    for g in range(2 * n, 2 * n + 2):
                        last = nc.tensor.matmul(o[:, GTOK * (g % 2):GTOK * (g % 2) + GTOK], b_d[:, g, c * P:(c + 1) * P],
                                                low[:, 0, GTOK * g:GTOK * (g + 1)], start=False, stop=(g == 2 * n + 1))
                    last.then_inc(down_done, 1)

            pe.wait_ge(l23_in, L23_ALL)
            pe.wait_ge(a2_spread, GROUPS)
            pe.wait_ge(xb_made, 2 * KT)
            for g in range(GROUPS):
                for k in range(KT):
                    last = nc.tensor.matmul(bank[:, g // 2, GTOK * (g % 2):GTOK * (g % 2) + GTOK],
                                            a2[:, g, k, :],
                                            xB[:, k, GTOK * g:GTOK * (g + 1)], start=(k == 0), stop=(k == KT - 1))
                if g % 2 == 1:
                    last.then_inc(low2_done, 1)
            for c in range(KT):
                for n in range(2):
                    i = 2 * c + n
                    o = bank[:, (i + 2) % 8, :]
                    if i >= 6:
                        pe.wait_ge(low2_made, i - 6 + 1)
                    for k in range(KT):
                        nc.tensor.matmul(o, w2[:, k, c * P:(c + 1) * P], xB[:, k, NTOK * n:NTOK * (n + 1)],
                                         start=(k == 0), stop=False)
                    pe.wait_ge(low2_made, 2)
                    for g in range(2 * n, 2 * n + 2):
                        last = nc.tensor.matmul(o[:, GTOK * (g % 2):GTOK * (g % 2) + GTOK], b2[:, g, c * P:(c + 1) * P],
                                                low[:, 1, GTOK * g:GTOK * (g + 1)], start=False, stop=(g == 2 * n + 1))
                    last.then_inc(lin2_done, 1)

            pe.wait_ge(x2_made, 2 * KT)
            for tile in range(TILES):
                o = bank[:, tile // 3, AR * (tile % 3):AR * (tile % 3) + AR]
                for k in range(KT):
                    last = nc.tensor.matmul(o, xA[:, k, tile * P:(tile + 1) * P], ar3[:, k, :],
                                            start=(k == 0), stop=(k == KT - 1))
            last.then_inc(hr_done, 1)
            for tile in range(TILES):
                if tile >= 2:
                    pe.wait_ge(xnat_made, tile - 1)
                for k in range(KT):
                    last = nc.tensor.transpose(bank[:, 3 + tile % 2, k * P:(k + 1) * P], xA[:, k, tile * P:(tile + 1) * P], ident[:])
                last.then_inc(x_turned, 1)
            for h in range(2):
                pe.wait_ge(hg_made, 4 * (h + 1))
                if h == 0:
                    pe.wait_ge(xnat_made, TILES)
                for tile in range(4 * h, 4 * h + 4):
                    last = nc.tensor.transpose(bank[:, 3 + h, P * (tile % 4):P * (tile % 4) + P], hg[:, tile, :], ident[:])
                last.then_inc(hg_turned, 1)
            for tile in range(TILES):
                o = bank[:, 5 + tile % 3, :]
                if tile >= 3:
                    pe.wait_ge(res_made, tile - 2)
                for k in range(KT):
                    nc.tensor.matmul(o, xA[:, k, tile * P:(tile + 1) * P], w3[:, k, :], start=(k == 0), stop=False)
                pe.wait_ge(hgt_made, tile // 4 + 1)
                nc.tensor.matmul(o, hgT[:, tile, :], b3, start=False, stop=True).then_inc(lin3_done, 1)

        @block.scalar
        def _(act):
            def square(n, tile):
                b, _ = bank_use("block", n, tile=tile)
                act.wait_ge(block_done, BLOCKS * tile + n + 1)
                i = 5 * tile + n
                act.wait_ge(summed, i)
                nc.scalar.activation(sq[:], mm[:, b], ACT.Square).then_inc(squared, 1)

            def read_v(tile, par):
                b, _ = bank_use("block", 5, tile=tile)
                act.wait_ge(block_done, BLOCKS * tile + 6)
                r = nc.scalar.copy(vN[:, par].rearrange("p g d -> p (g d)"), mm[:, b])
                r.then_inc(v_read, 1)
                act.wait_ge(v_read, tile + 1)
                act.sem_inc(bank_free[b], 1)

            def read_turned(m, tile, par):
                b, _ = bank_use("turn", m, tile=tile)
                act.wait_ge(turned, 5 * tile + m + 1)
                if m < 4:
                    nc.scalar.copy(qT[:, par, m].rearrange("p b (h t) -> p b h t", h=REP),
                                   mm[:, b].rearrange("p (h b t) -> p b h t", h=REP, b=SEQ_PER_TILE)
                                   ).then_inc(turn_read, 1)
                else:
                    nc.scalar.copy(kTn[:, par].rearrange("p h t -> p (h t)"), mm[:, b]).then_inc(turn_read, 1)
                act.wait_ge(turn_read, 5 * tile + m + 1)
                act.sem_inc(bank_free[b], 1)

            def exps(s, k):
                act.wait_ge(masked, PAIRS * s + k + 1)
                nc.scalar.activation(probs[:, k % 2], probs[:, k % 2], ACT.Exp, bias=minv[:, k % 2:k % 2 + 1],
                                     scale=-1.0, accum_out=psum_[:, k % 2:k % 2 + 1]).then_inc(exped, 1)

            def read_o(s, k):
                b, g = k // HKH, k % HKH
                act.wait_ge(pv_done, PAIRS * s + k + 1)
                if k == 0:
                    act.wait_ge(oT_free, s + 1)
                nc.scalar.copy(oT[:, REP * g:REP * g + REP, S * b:S * b + S],
                               o_ps[:, 0:P].rearrange("p (h t) -> p h t", h=REP)).then_inc(o_free, 1)

            def read_pt(s, k):
                act.wait_ge(probs_turned, 2 + PAIRS * s + k + 1)
                nc.scalar.copy(pT[:, k % 2], pt_ps[:, 0:KEYS]).then_inc(pt_read, 1)

            def load_xt(tile):
                act.wait_ge(block_done, BLOCKS * tile)
                act.dma_start(xt[:], t["xt"][bass.ds(tile % TILES, 1)].rearrange("o p k t -> (o p) k t")
                              ).then_inc(xt_in, 16)

            def step(s, par, last=False, load=True):
                for k in range(PAIRS):
                    if not last:
                        for m in range(5):
                            if turn_slot(m) == k:
                                read_turned(m, s + 1, 1 - par)
                        for n in range(BLOCKS):
                            if k == block_slots(n)[1]:
                                if n < 5:
                                    square(n, s + 1)
                                else:
                                    read_v(s + 1, 1 - par)
                    if k + 2 < PAIRS:
                        exps(s, k + 2)
                    elif not last:
                        exps(s + 1, k + 2 - PAIRS)
                    read_o(s, k)
                    if k + 1 < PAIRS:
                        read_pt(s, k + 1)
                    elif not last:
                        read_pt(s + 1, 0)
                    if k == 12 and load:
                        load_xt(s + 2)

            act.sem_inc(o_free, 1)
            act.sem_inc(oT_free, 1)
            act.dma_start(seqlen_i, t["seqlen"]).then_inc(setup_in, 16)
            act.dma_start(seqtok_i, t["seqtok"]).then_inc(setup_in, 16)
            act.dma_start(sq[:, 64:64 + D // 2 + 1], t["const"][:, C_FREQ:C_FREQ + D // 2 + 1]).then_inc(setup_in, 16)
            act.dma_start(wq_row, t["qnorm"]).then_inc(setup_in, 16)
            act.dma_start(wk_row, t["knorm"]).then_inc(setup_in, 16)
            act.wait_ge(setup_v, 11)
            nc.scalar.activation(sin_t, red[:], ACT.Sin).then_inc(setup_a, 1)
            act.wait_ge(setup_v, 18)
            nc.scalar.activation(cos_t, trig[:], ACT.Sin).then_inc(setup_a, 1)
            act.wait_ge(tables_made, 1)
            for what, n in BANK_ORDER[:PROLOGUE_USES]:
                if what == "turn":
                    read_turned(n, 0, 0)
                elif n < 5:
                    square(n, 0)
                else:
                    read_v(0, 0)
            load_xt(1)
            exps(0, 0)
            exps(0, 1)
            read_pt(0, 0)
            with act.Fori(0, STEPS // 2 - 1) as i:
                step(2 * i, 0)
                step(2 * i + 1, 1)
            step(STEPS - 2, 0, load=False)
            step(STEPS - 1, 1, last=True, load=False)

            act.wait_ge(agu_in, 16 * 2 * B)
            for g in range(GROUPS):
                nc.scalar.copy(*spread_group(a_gu_raw[:, 1], a_gu[:, 1, g], g, KT)).then_inc(agu_spread, 1)

            for tile in range(0, TILES, 2):
                act.wait_ge(y_turned, tile + 1)
                nc.scalar.copy(xA[:, :, tile * P:(tile + 1) * P],
                               bank[:, tile].rearrange("p (k t) -> p k t", k=KT)).then_inc(xa_made, 1)

            def silu(f, j, m):
                for n in range(2):
                    act.wait_ge(gu_done, 4 * f + 2 * n + 1)
                    i = 2 * f + n
                    if not isinstance(f, int) or i >= 2:
                        act.wait_ge(act_made, i - 1)
                    nc.scalar.activation(gated[0:m, n, :], bank[0:m, 4 * j + n, :], ACT.Silu).then_inc(silu_done, 1)

            silu(0, 0, P)
            silu(1, 1, P)
            with act.Fori(1, FT // 2) as i:
                silu(2 * i, 0, P)
                silu(2 * i + 1, 1, P)
            silu(FT - 1, 0, FLAST)

            for tile in range(TILES):
                act.wait_ge(x_turned, tile + 1)
                nc.scalar.copy(xnat[:, tile, :], bank[:, 3 + tile % 2, :]).then_inc(xnat_made, 1)
            act.wait_ge(rv, 12)
            nc.scalar.activation(route1[3], route1[2], ACT.Exp).then_inc(ratio_done, 1)
            for h in range(2):
                act.wait_ge(hg_turned, h + 1)
                nc.scalar.copy(hgT[:, 4 * h:4 * h + 4, :], bank[:, 3 + h].rearrange("p (t c) -> p t c", t=4)).then_inc(hgt_made, 1)

        @block.vector
        def _(dve):
            def norm_rows(n, tile):
                b, _ = bank_use("block", n, tile=tile)
                i = 5 * tile + n
                dve.wait_ge(squared, i + 1)
                nc.vector.tensor_reduce(ss, sq[:].rearrange("p (h d) -> p h d", h=4), AX.X, ALU.add).then_inc(summed, 1)
                dve.wait_ge(summed, i + 1)
                nc.vector.tensor_scalar(var, ss, 1.0 / D, ATT_EPS, ALU.mult, ALU.add).then_inc(var_made, 1)

            def scale_rows(n, tile):
                b, _ = bank_use("block", n, tile=tile)
                i = 5 * tile + n
                dve.wait_ge(rstd_made, i + 1)
                dve.wait_ge(sin_done, i)
                dve.wait_ge(cos_done, i)
                nc.vector.tensor_tensor(tq[:].rearrange("p (h d) -> p h d", h=4),
                                        mm[:, b].rearrange("p (h d) -> p h d", h=4),
                                        rstd.unsqueeze(2).to_broadcast([P, 4, D]), ALU.mult).then_inc(scaled, 1)
                dve.wait_ge(scaled, i + 1)
                dve.sem_inc(bank_free[b], 1)

            def rope_cos(n, tile):
                i = 5 * tile + n
                dve.wait_ge(roped, i)
                tab = (cosq if n < 4 else cosk)[:, bass.ds(tile % TILES, 1), :].to_broadcast([P, 4, D])
                nc.vector.tensor_tensor(rc[:].rearrange("p (h d) -> p h d", h=4),
                                        tq[:].rearrange("p (h d) -> p h d", h=4), tab, ALU.mult).then_inc(cos_done, 1)

            def make_mask(tile, b):
                i = SEQ_PER_TILE * tile + b
                col = seqlen[:, bass.ds((SEQ_PER_TILE * tile + b) % B, 1)]
                nc.vector.tensor_scalar(mask[:, b % 2, 0:L], keyno[:], col, NEG, ALU.is_ge, ALU.mult).then_inc(mask_made, 1)
                nc.vector.tensor_copy(mask[:, b % 2, L:KEYS], other[:, b, :]).then_inc(mask_made, 1)

            def mask_scores(s, k):
                b = k // HKH
                dve.wait_ge(scored, PAIRS * s + k + 1)
                if k % HKH == 0:
                    dve.wait_ge(mask_made, 2 * (SEQ_PER_TILE * s + b + 1))
                dve.wait_ge(probs_turned, PAIRS * s + k + 1)
                dve.sem_inc(vector_went_on, 1)
                nc.vector.tensor_tensor_reduce(out=probs[:, k % 2], in0=sc[:, 0:KEYS], in1=mask[:, b % 2],
                                               scale=-SCALE, scalar=BIG, op0=ALU.add, op1=ALU.min,
                                               accum_out=minv[:, k % 2:k % 2 + 1]).then_inc(masked, 1)

            def norm_probs(s, k):
                dve.wait_ge(exped, PAIRS * s + k + 1)
                nc.vector.reciprocal(rinv[:, k % 2:k % 2 + 1], psum_[:, k % 2:k % 2 + 1]).then_inc(inverted, 1)
                dve.wait_ge(inverted, PAIRS * s + k + 1)
                nc.vector.tensor_scalar(probs[:, k % 2], probs[:, k % 2], rinv[:, k % 2:k % 2 + 1], None,
                                        ALU.mult).then_inc(normed, 1)

            def add_y(s, last):
                b, _ = bank_use("out", 0, step=s, last=last)
                dve.wait_ge(out_done, s + 1)
                dve.sem_inc(oT_free, 1)
                yt = y[:, bass.ds(s % TILES, 1), :].rearrange("p o h -> p (o h)")
                nc.vector.tensor_tensor(yt, mm[:, b], yt, ALU.add).then_inc(y_added, 1)
                dve.wait_ge(y_added, s + 1)
                dve.sem_inc(bank_free[b], 1)

            def step(s, par, last=False, first=False):
                for k in range(PAIRS):
                    if k + 1 < PAIRS:
                        norm_probs(s, k + 1)
                    elif not last:
                        norm_probs(s + 1, 0)
                    if k + 2 < PAIRS:
                        mask_scores(s, k + 2)
                    elif not last:
                        mask_scores(s + 1, k + 2 - PAIRS)
                    if not last:
                        for n in range(5):
                            if k == 2 * n + 2:
                                norm_rows(n, s + 1)
                                scale_rows(n, s + 1)
                            if k == 2 * n + 3:
                                rope_cos(n, s + 1)
                    if (k + 2) % HKH == 0:
                        b = (k + 2) // HKH + 1
                        if b < SEQ_PER_TILE:
                            dve.wait_ge(masked, PAIRS * s + k + 2)
                            make_mask(s, b)
                        elif not last:
                            dve.wait_ge(masked, PAIRS * s + k + 2)
                            make_mask(s + 1, b - SEQ_PER_TILE)
                add_y(s, last)

            n_setup = [0]

            def chain(ins):
                n_setup[0] += 1
                ins.then_inc(setup_v, 1)
                dve.wait_ge(setup_v, n_setup[0])

            dve.wait_ge(setup_in, 16 * 5)
            chain(nc.vector.tensor_copy(seqlen, seqlen_i))
            chain(nc.vector.tensor_copy(pos, seqtok_i))
            chain(nc.vector.tensor_scalar(pos, pos, step_, None, ALU.add))
            halfd = D // 2
            a3, t3 = (x[:].rearrange("p (t f) -> p t f", t=TILES) for x in (ang, turns))
            chain(nc.vector.tensor_tensor(a3, pos.unsqueeze(2).to_broadcast([P, TILES, halfd]),
                                          freq.unsqueeze(1).to_broadcast([P, TILES, halfd]), ALU.mult))

            def reduce_angle(dst, quarter):
                chain(nc.vector.tensor_scalar(turns[:], ang[:], 1.0 / (2.0 * PI), quarter, ALU.mult, ALU.add))
                chain(nc.vector.tensor_scalar(turns[:], turns[:], ROUND, -ROUND, ALU.add, ALU.add))
                src = ang
                for part in (TWO_PI_1, TWO_PI_2, TWO_PI_3):
                    chain(nc.vector.scalar_tensor_tensor(out=dst[:], in0=turns[:], scalar=-part, in1=src[:],
                                                         op0=ALU.mult, op1=ALU.add))
                    src = dst
                chain(nc.vector.tensor_scalar(dst[:], dst[:], 2 * PI * quarter, PI_SAFE, ALU.add, ALU.min))
                chain(nc.vector.tensor_scalar(dst[:], dst[:], -PI_SAFE, None, ALU.max))

            reduce_angle(red, 0.0)
            reduce_angle(trig, 0.25)
            assert n_setup[0] == 18
            dve.wait_ge(setup_a, 2)
            s3, c3 = (x.rearrange("p (t f) -> p t f", t=TILES) for x in (sin_t, cos_t))
            for ctab, stab, w in ((cosq, sinq, wq_row), (cosk, sink, wk_row)):
                lo = w[:, 0:halfd].unsqueeze(1).to_broadcast([P, TILES, halfd])
                hi = w[:, halfd:D].unsqueeze(1).to_broadcast([P, TILES, halfd])
                chain(nc.vector.tensor_tensor(ctab[:, :, 0:halfd], c3, lo, ALU.mult))
                chain(nc.vector.tensor_tensor(ctab[:, :, halfd:D], c3, hi, ALU.mult))
                chain(nc.vector.scalar_tensor_tensor(out=stab[:, :, 0:halfd], in0=s3, scalar=-1.0, in1=hi,
                                                     op0=ALU.mult, op1=ALU.mult))
                chain(nc.vector.tensor_tensor(stab[:, :, halfd:D], s3, lo, ALU.mult))
            chain(nc.vector.memset(halfs, -0.5))
            dve.sem_inc(tables_made, 1)

            dve.wait_ge(const_in, 16 * 5)
            dve.wait_ge(y_in, 16)
            make_mask(0, 0)
            make_mask(0, 1)
            for n in range(5):
                norm_rows(n, 0)
                scale_rows(n, 0)
                rope_cos(n, 0)
            mask_scores(0, 0)
            norm_probs(0, 0)
            mask_scores(0, 1)
            with dve.Fori(0, STEPS // 2 - 1) as i:
                step(2 * i, 0)
                step(2 * i + 1, 1)
            step(STEPS - 2, 0)
            step(STEPS - 1, 1, last=True)

            dve.wait_ge(agu_in, 16 * 2 * B)
            for g in range(GROUPS):
                nc.vector.tensor_copy(*spread_group(a_gu_raw[:, 0], a_gu[:, 0, g], g, KT)).then_inc(agu_spread, 1)

            for tile in range(1, TILES, 2):
                dve.wait_ge(y_turned, tile + 1)
                nc.vector.tensor_copy(xA[:, :, tile * P:(tile + 1) * P],
                                      bank[:, tile].rearrange("p (k t) -> p k t", k=KT)).then_inc(xa_made, 1)

            own2 = own[:].unsqueeze(1).to_broadcast([P, 2, GTOK])

            def keep_own(i, src, dst, scale, done, made):
                dve.wait_ge(done, i)
                nc.vector.scalar_tensor_tensor(out=dst.rearrange("p (g t) -> p g t", g=2),
                                               in0=src.rearrange("p (g t) -> p g t", g=2), scalar=scale, in1=own2,
                                               op0=ALU.mult, op1=ALU.mult).then_inc(made, 1)

            for w in range(2):
                for h in range(2):
                    keep_own(2 * w + h + 1, bank[:, 2 * w + h, :], low[:, w, NTOK * h:NTOK * (h + 1)], 0.5,
                             low_done, low_made)

            def gate_times_up(f, j, m):
                for n in range(2):
                    dve.wait_ge(gu_done, 4 * f + 2 * n + 2)
                    dve.wait_ge(silu_done, 2 * f + n + 1)
                    nc.vector.tensor_tensor(act_t[0:m, bass.ds(f, 1), NTOK * n:NTOK * (n + 1)].rearrange("p o t -> p (o t)"),
                                            gated[0:m, n, :], bank[0:m, 4 * j + 2 + n, :], ALU.mult).then_inc(act_made, 1)

            gate_times_up(0, 0, P)
            gate_times_up(1, 1, P)
            with dve.Fori(1, FT // 2) as i:
                gate_times_up(2 * i, 0, P)
                gate_times_up(2 * i + 1, 1, P)
            gate_times_up(FT - 1, 0, FLAST)

            for h in range(2):
                keep_own(4 + h + 1, bank[:, h, :], low[:, 0, NTOK * h:NTOK * (h + 1)], 0.5, low_done, low_made)
            for c in range(KT):
                for n in range(2):
                    i = 2 * c + n
                    dve.wait_ge(down_done, i + 1)
                    nc.vector.tensor_tensor(xB[:, c, NTOK * n:NTOK * (n + 1)], bank[:, (i + 2) % 8, :],
                                            xA[:, c, NTOK * n:NTOK * (n + 1)], ALU.add).then_inc(xb_made, 1)
            for h in range(2):
                keep_own(h + 1, bank[:, h, :], low[:, 1, NTOK * h:NTOK * (h + 1)], 2.0, low2_done, low2_made)
            dve.wait_ge(l23_in, L23_ALL)
            for c in range(KT):
                for n in range(2):
                    i = 2 * c + n
                    dve.wait_ge(lin2_done, i + 1)
                    if i == 0:
                        dve.wait_ge(xb_made, 2 * KT)
                    nc.vector.scalar_tensor_tensor(out=xA[:, c, NTOK * n:NTOK * (n + 1)], in0=bank[:, (i + 2) % 8, :],
                                                   scalar=bias2[:, c:c + 1], in1=xB[:, c, NTOK * n:NTOK * (n + 1)],
                                                   op0=ALU.add, op1=ALU.add).then_inc(x2_made, 1)

            n_rv = [0]

            def link(ins):
                n_rv[0] += 1
                ins.then_inc(rv, 1)
                dve.wait_ge(rv, n_rv[0])

            def over_e(v):
                return v.unsqueeze(2).to_broadcast([P, TILES, E3])

            def over_t(v):
                return v.unsqueeze(1).to_broadcast([P, TILES, E3])

            logits, bias, eq, pick1, rest_, pick2, gates, tmp = route
            m1, m2, diff, ratio, den, w1, w2_, first = route1
            expert, firstness = small[:, 0:E3], small[:, E3:2 * E3]
            link(nc.vector.tensor_copy(lang, lang_i))
            link(nc.vector.tensor_tensor(bias, over_t(expert), over_e(lang), ALU.is_equal))
            dve.wait_ge(hr_done, 1)
            for tile in range(TILES):
                c0 = AR * (tile % 3) + E3 * RANK
                ins = nc.vector.scalar_tensor_tensor(out=logits[:, tile, :], in0=bias[:, tile, :], scalar=5.0,
                                                     in1=bank[:, tile // 3, c0:c0 + E3], op0=ALU.mult, op1=ALU.add)
            link(ins)
            link(nc.vector.tensor_reduce(m1, logits, AX.X, ALU.max))

            def pick(out, values_, top):
                link(nc.vector.tensor_tensor(eq, values_, over_e(top), ALU.is_equal))
                link(nc.vector.tensor_tensor(eq, eq, over_t(firstness), ALU.mult))
                link(nc.vector.tensor_reduce(first, eq, AX.X, ALU.max))
                link(nc.vector.tensor_tensor(out, eq, over_e(first), ALU.is_equal))

            pick(pick1, logits, m1)
            link(nc.vector.scalar_tensor_tensor(out=rest_, in0=pick1, scalar=NEG, in1=logits, op0=ALU.mult, op1=ALU.add))
            link(nc.vector.tensor_reduce(m2, rest_, AX.X, ALU.max))
            link(nc.vector.tensor_tensor(diff, m2, m1, ALU.subtract))
            assert n_rv[0] == 11
            dve.sem_inc(rv, 1)
            n_rv[0] += 1
            pick(pick2, rest_, m2)
            dve.wait_ge(ratio_done, 1)
            link(nc.vector.tensor_scalar(den, ratio, 1.0, None, ALU.add))
            link(nc.vector.reciprocal(w1, den))
            link(nc.vector.tensor_scalar(w1, w1, 2.0, None, ALU.mult))
            link(nc.vector.tensor_tensor(w2_, w1, ratio, ALU.mult))
            link(nc.vector.tensor_tensor(gates, pick1, over_e(w1), ALU.mult))
            link(nc.vector.tensor_tensor(tmp, pick2, over_e(w2_), ALU.mult))
            link(nc.vector.tensor_tensor(gates, gates, tmp, ALU.add))
            for tile in range(TILES):
                c0 = AR * (tile % 3)
                nc.vector.tensor_tensor(hg[:, tile, :].rearrange("p (e r) -> p e r", e=E3),
                                        bank[:, tile // 3, c0:c0 + E3 * RANK].rearrange("p (e r) -> p e r", e=E3),
                                        gates[:, tile, :].unsqueeze(2).to_broadcast([P, E3, RANK]), ALU.mult
                                        ).then_inc(hg_made, 1)
            for tile in range(TILES):
                dve.wait_ge(lin3_done, tile + 1)
                dve.wait_ge(xnat_made, tile + 1)
                nc.vector.tensor_tensor(res[:, tile, :], bank[:, 5 + tile % 3, :], xnat[:, tile, :], ALU.add).then_inc(res_made, 1)

        @block.gpsimd
        def _(pool):
            def root(i):
                pool.wait_ge(var_made, i + 1)
                nc.gpsimd.tensor_tensor(rstd, var, halfs, ALU.pow).then_inc(rstd_made, 1)

            def rope_sin(n, tile):
                i = 5 * tile + n
                half = D // 2
                pool.wait_ge(scaled, i + 1)
                pool.wait_ge(roped, i)
                pool.sem_inc(pool_went_on, 1)
                stab = sinq if n < 4 else sink
                t3 = tq[:].rearrange("p (h d) -> p h d", h=4)
                r3 = rs[:].rearrange("p (h d) -> p h d", h=4)
                tab = stab[:, bass.ds(tile % TILES, 1), :]
                nc.gpsimd.tensor_tensor(r3[:, :, 0:half], t3[:, :, half:D],
                                        tab[:, :, 0:half].to_broadcast([P, 4, half]), ALU.mult)
                nc.gpsimd.tensor_tensor(r3[:, :, half:D], t3[:, :, 0:half],
                                        tab[:, :, half:D].to_broadcast([P, 4, half]), ALU.mult).then_inc(sin_done, 1)
                pool.wait_ge(sin_done, i + 1)
                pool.wait_ge(cos_done, i + 1)
                pool.wait_ge(turned, i)
                nc.gpsimd.tensor_tensor(qn[:], rc[:], rs[:], ALU.add).then_inc(roped, 1)

            pool.wait_ge(tables_made, 1)
            for n in range(5):
                root(n)
                rope_sin(n, 0)
            with pool.Fori(1, STEPS) as tile:
                for n in range(5):
                    root(5 * tile + n)
                    rope_sin(n, tile)

            for h in range(2):
                pool.wait_ge(ad_in, 16 * (B // 2) * (h + 1))
                for g in range(GROUPS // 2):
                    nc.gpsimd.tensor_copy(*spread_group(a_d_raw, a_d[:, h * GROUPS // 2 + g], g, FT)).then_inc(ad_spread, 1)
            pool.wait_ge(a2_in, 16 * B)
            for g in range(GROUPS):
                nc.gpsimd.tensor_copy(*spread_group(a2_raw, a2[:, g], g, KT)).then_inc(a2_spread, 1)


def kernel(**inputs):
    import numpy as _np
    import concourse.bacc as _bacc
    from concourse import mybir as _mybir
    from concourse.bass_utils import run_bass_kernel_spmd as _run

    a = {k: _np.asarray(v) for k, v in inputs.items()}
    x = a["x"].reshape(TOK, HID)

    def by_k(w):
        return w.T.reshape(-1, P, w.shape[0]).transpose(1, 0, 2)

    wq, wk, wv, wo = (a["L0_cond_" + n] for n in ("Wq", "Wk", "Wv", "Wo"))
    wqkv = _np.stack([_np.stack(
        [by_k(wq[h * HQH * D + n * 512:h * HQH * D + (n + 1) * 512]) for n in range(4)]
        + [by_k(w[h * HKH * D:(h + 1) * HKH * D]) for w in (wk, wv)]) for h in range(HALVES)])
    f_pad = FT * P - F

    def rows_f(w):
        w = _np.pad(w, ((0, f_pad), (0, 0)))
        return w.reshape(FT, P, KT, P).transpose(0, 3, 2, 1)

    def low_rank(w, n):
        return w.reshape(w.shape[0], RANK, n, P).transpose(0, 3, 2, 1).reshape(w.shape[0], P, n * RANK)

    l1 = {k[len("L1_cond_"):]: v for k, v in a.items() if k.startswith("L1_cond_")}
    seq = a["itok_B_207_1644"]
    arrays = {
        "x": x.reshape(TILES, P, HID).transpose(1, 0, 2),
        "xt": x.reshape(TILES, P, KT, P).transpose(0, 3, 2, 1),
        "wqkv": wqkv,
        "wo": wo.T.reshape(HALVES, HQH, D, HID).transpose(0, 2, 1, 3),
        "kcache": a["L0_cond_k_cache"].reshape(PAGES, PSIZE, HALVES, HKH, D).transpose(2, 0, 4, 3, 1).reshape(
            HALVES, PAGES, D, HKH * PSIZE),
        "vcache": a["L0_cond_v_cache"].reshape(PAGES, PSIZE, HALVES, HKH * D).transpose(2, 0, 1, 3),
        "table": a["itok_Bx16_0_63"],
        "seqlen": _np.broadcast_to(seq[None, :], (P, B)),
        "seqtok": _np.repeat(seq, S).reshape(TILES, P).T,
        "qnorm": _np.broadcast_to(a["L0_cond_q_norm_w"][None, :], (P, D)),
        "knorm": _np.broadcast_to(a["L0_cond_k_norm_w"][None, :], (P, D)),
        "const": constants(),
        "ids": _np.concatenate([a["itok_B_2_6"], a["itok_B_0_23"]])[None, :],
        "w_gu": _np.stack([rows_f(l1["W_gate"]), rows_f(l1["W_up"])]),
        "a_gu": _np.stack([low_rank(l1["A_gate"][0], KT), low_rank(l1["A_up"][0], KT)]),
        "b_gu": _np.stack([l1["B_gate"][0].transpose(0, 2, 1), l1["B_up"][0].transpose(0, 2, 1)]),
        "w_d": _np.pad(l1["W_down"].T, ((0, f_pad), (0, 0))).reshape(FT, P, HID).transpose(1, 0, 2),
        "a_d": low_rank(_np.pad(l1["A_down"][0], ((0, 0), (0, 0), (0, f_pad))), FT),
        "b_d": l1["B_down"][0].transpose(0, 2, 1),
        "w2": by_k(a["L2_cond_W"]),
        "bias2": a["L2_cond_b"].reshape(KT, P).T,
        "a2": a["L2_cond_lora_As"].reshape(B, KT, P, RANK).transpose(0, 2, 1, 3).reshape(B, P, KT * RANK),
        "b2": a["L2_cond_lora_Bs"],
        "w3": by_k(a["L3_cond_W"]),
        "ar3": by_k(_np.concatenate([a["L3_cond_A"].reshape(E3 * RANK, HID), a["L3_cond_Wr"]])),
        "b3": a["L3_cond_B"].transpose(0, 2, 1).reshape(E3 * RANK, HID),
        "lang": _np.repeat(a["itok_B_0_7"], S).reshape(TILES, P).T,
    }
    arrays = {f"in_{k}": _np.ascontiguousarray(v) for k, v in arrays.items()}
    nc = _bacc.Bacc("TRN2", target_bir_lowering=False, num_devices=1, dynamic_dma_scratch_size=1024)
    t = {k[3:]: nc.dram_tensor(k, v.shape, _mybir.dt.from_np(v.dtype), kind="ExternalInput").ap()
         for k, v in arrays.items()}
    t["out"] = nc.dram_tensor("out", (P, TILES, HID), F32, kind="ExternalOutput").ap()
    build(nc, t)
    r = _run(nc, [arrays], core_ids=[0])
    return r.results[0]["out"].transpose(1, 0, 2).reshape(B, S, HID)
```

```python
from contextlib import ExitStack

import numpy as np

import concourse.bass as bass
from concourse import mybir
from concourse.alu_op_type import AluOpType as ALU

ACT = mybir.ActivationFunctionType
AX = mybir.AxisListType
F32 = mybir.dt.float32
I32 = mybir.dt.int32

P = 128
B, S, HID = 32, 32, 512
TOK = B * S
TILES = TOK // P
SEQ_PER_TILE = P // S
KT = HID // P
D = 128
HQ, HK = 32, 8
REP = HQ // HK
HALVES = 2
HKH = HK // HALVES
HQH = HQ // HALVES
PAGES, PSIZE, NPP = 64, 32, 16
L = PSIZE * NPP
CHUNKS = L // P
KEYS = L + S
STEPS = HALVES * TILES
PAIRS = SEQ_PER_TILE * HKH
BLOCKS = REP * HKH // 4 + 2
SCALE = 1.0 / float(np.sqrt(D))
ATT_EPS = 1e-6
NEG = -1e30
BIG = 3.0e38
F = 1376
FT = -(-F // P)
FLAST = F - (FT - 1) * P
RANK = 16
SEQ_PER_GROUP = P // RANK
GROUPS = B // SEQ_PER_GROUP
GTOK = TOK // GROUPS
E3 = 8
AR = E3 * RANK + E3
NTOK = 512

PI = 3.14159265358979
PI_SAFE = float(np.nextafter(np.float32(np.pi), np.float32(0)))
TWO_PI_1 = 6.28125
TWO_PI_2 = float(np.float32(np.floor((2 * np.pi - TWO_PI_1) * 2**21) / 2**21))
TWO_PI_3 = float(np.float32(2 * np.pi - TWO_PI_1 - TWO_PI_2))
ROUND = 12582912.0

C_IDENT = 0
C_KEY = C_IDENT + P
C_FREQ = C_KEY + L
C_STEP = C_FREQ + D // 2
C_OWN = C_STEP + 1
C_EXPERT = C_OWN + GTOK
C_FIRST = C_EXPERT + E3
C_COLS = C_FIRST + E3


def constants():
    c = np.zeros((P, C_COLS), np.float32)
    row = np.arange(P)
    c[:, C_IDENT:C_IDENT + P] = np.eye(P)
    c[:, C_KEY:C_KEY + L] = np.arange(L)
    c[:, C_FREQ:C_FREQ + D // 2] = (1.0 / np.float32(10000.0) ** (
        np.arange(0, D, 2, dtype=np.float32) / np.float32(D))).astype(np.float32)
    c[:, C_STEP] = row % S
    c[:, C_OWN:C_OWN + GTOK] = row[:, None] // RANK == np.arange(GTOK)[None, :] // S
    c[:, C_EXPERT:C_EXPERT + E3] = np.arange(E3)
    c[:, C_FIRST:C_FIRST + E3] = E3 - np.arange(E3)
    return c


BANK_ORDER = [("block", 0), ("block", 1), ("block", 2), ("turn", 0), ("block", 3), ("turn", 1),
              ("block", 4), ("turn", 2), ("block", 5), ("turn", 3), ("turn", 4), ("out", 0)]
PROLOGUE_USES = 11
SC0 = 512 - L // 2
MM_BANKS = 3


def bank_use(what, n, tile=None, step=None, last=False):
    i = BANK_ORDER.index((what, n))
    if last:
        u = PROLOGUE_USES + len(BANK_ORDER) * (STEPS - 1)
        return u % MM_BANKS, u // MM_BANKS
    if tile is not None and isinstance(tile, int) and tile == 0:
        return i % MM_BANKS, i // MM_BANKS
    if step is None:
        step = tile - 1
    u = PROLOGUE_USES + i
    return u % MM_BANKS, u // MM_BANKS + (len(BANK_ORDER) // MM_BANKS) * step


def block_slots(n):
    return (2 * n, 2 * n + 1)


def turn_slot(m):
    return 2 * m + 5


def build(nc, t):
    with ExitStack() as whole:
        def sem(name):
            return whole.enter_context(nc.semaphore(name))

        def sb(scope, name, shape, dt=F32):
            return scope.enter_context(nc.sbuf_tensor(name, shape, dt))

        def ps(scope, name, shape, dt=F32):
            return scope.enter_context(nc.psum_tensor(name, shape, dt))

        ident = sb(whole, "ident", [P, P])
        own = sb(whole, "own", [P, GTOK])
        small = sb(whole, "small", [P, 2 * E3])
        ids = sb(whole, "ids", [1, 2 * B], I32)
        y = sb(whole, "y", [P, TILES, HID])

        att = ExitStack()
        wqkv = sb(att, "wqkv", [P, BLOCKS, KT, 512])
        wo = sb(att, "wo", [P, HQH, HID])
        xt = sb(att, "xt", [P, KT, P])
        qT = sb(att, "qT", [P, 2, HKH, SEQ_PER_TILE, P])
        kTn = sb(att, "kTn", [P, SEQ_PER_TILE, HKH * S])
        vN = sb(att, "vN", [P, 2, HKH, D])
        kc = sb(att, "kc", [P, 2, NPP + 1, HKH * PSIZE])
        vc = sb(att, "vc", [P, 2, CHUNKS, HKH * D])
        probs = sb(att, "probs", [P, 2, L + P])
        pT = sb(att, "pT", [P, 2, L])
        pT_own = sb(att, "pT_own", [P, SEQ_PER_TILE, 2, P])
        oT = sb(att, "oT", [P, HQH, P])
        mask = sb(att, "mask", [P, 2, KEYS])
        keyno = sb(att, "keyno", [P, L])
        rows = sb(att, "rows", [P, 80])
        seqlen_i = rows[:, 0:B].bitcast(I32)
        seqlen = rows[:, B:2 * B]
        minv, psum_, rinv = rows[:, 64:66], rows[:, 66:68], rows[:, 68:70]
        rows2 = sb(att, "rows2", [P, 16])
        ss, var, rstd, halfs = (rows2[:, 4 * j:4 * j + 4] for j in range(4))
        table = sb(att, "table", [B, NPP], I32)
        vrow = sb(att, "vrow", [P, HALVES * B, CHUNKS], I32)
        vrow_now = sb(att, "vrow_now", [P, 2, CHUNKS], I32)
        cosq = sb(att, "cosq", [P, TILES, D])
        sinq = sb(att, "sinq", [P, TILES, D])
        cosk = sb(att, "cosk", [P, TILES, D])
        sink = sb(att, "sink", [P, TILES, D])
        sq = sb(att, "sq", [P, 512])
        tq = sb(att, "tq", [P, 512])
        rc = sb(att, "rc", [P, 512])
        rs = sb(att, "rs", [P, 512])
        qn = sb(att, "qn", [P, 512])
        sc = ps(att, "sc", [P, 1024])
        pt_ps = ps(att, "pt_ps", [P, 1024])
        o_ps = ps(att, "o_ps", [P, 512])
        mm = ps(att, "mm", [P, MM_BANKS, 512])
        seqtok_i = sq[:, 0:TILES].bitcast(I32)
        pos = sq[:, TILES:2 * TILES]
        freq = sq[:, 64:128]
        step_ = sq[:, 128:129]
        wq_row, wk_row = sq[:, 129:129 + D], sq[:, 129 + D:129 + 2 * D]
        vpage_i = pT[:, 0, 0:B * CHUNKS].bitcast(I32)
        vpage = pT[:, 1, 0:B * CHUNKS]
        ang, turns, red, trig = tq, rc, rs, qn
        sin_t, cos_t = probs[:, 0, 0:512], probs[:, 1, 0:512]
        att.close()

        rest = ExitStack()
        b_gu = sb(rest, "b_gu", [P, GROUPS, 2, F])
        w_f0 = sb(rest, "w_f0", [P, 2, KT, P])
        sb(rest, "gap0", [P, 256])
        xA = sb(rest, "xA", [P, KT, TOK])
        act_t = sb(rest, "act_t", [P, FT, TOK])
        a_d = sb(rest, "a_d", [P, GROUPS, FT, SEQ_PER_GROUP * RANK])
        w_d = sb(rest, "w_d", [P, FT, HID])
        low = sb(rest, "low", [P, 2, TOK])
        sb(rest, "gap1", [P, 1664])
        a_gu = sb(rest, "a_gu", [P, 2, GROUPS, KT, SEQ_PER_GROUP * RANK])
        a_gu_raw = sb(rest, "a_gu_raw", [P, B, 2, KT * RANK])
        w_f1 = sb(rest, "w_f1", [P, 2, KT, P])
        w_f = (w_f0, w_f1)
        bank = ps(rest, "bank", [P, 8, 512])
        rest.close()
        xB = y[:].rearrange("p t h -> p (t h)").rearrange("p (k t) -> p k t", k=KT)
        a_d_raw = y[:].rearrange("p t h -> p (t h)")[:, 0:B // 2 * FT * RANK].rearrange("p (b c) -> p b c", b=B // 2)
        flat = a_gu[:].rearrange("p w g k c -> p (w g k c)")
        b_d = flat[:, 0:GROUPS * HID].rearrange("p (g h) -> p g h", g=GROUPS)
        a2_raw = flat[:, GROUPS * HID:GROUPS * HID + B * KT * RANK].rearrange("p (b c) -> p b c", b=B)
        flat = a_gu_raw[:].rearrange("p b w c -> p (b w c)")
        b_f = flat[:, 0:4 * GROUPS * P].rearrange("p (j g w m) -> p j g w m", j=2, g=GROUPS, w=2)
        gated = flat[:, 4 * GROUPS * P:4 * GROUPS * P + 2 * NTOK].rearrange("p (n t) -> p n t", n=2)
        off = [0]
        pool_ = b_gu[:].rearrange("p g w f -> p (g w f)")

        def carve(n):
            a = off[0]
            off[0] += n
            return pool_[:, a:a + n]

        w2 = carve(KT * HID).rearrange("p (k h) -> p k h", k=KT)
        a2 = carve(B * KT * RANK).rearrange("p (g k c) -> p g k c", g=GROUPS, k=KT)
        b2 = carve(GROUPS * HID).rearrange("p (g h) -> p g h", g=GROUPS)
        bias2 = carve(KT)
        w3 = carve(KT * HID).rearrange("p (k h) -> p k h", k=KT)
        ar3 = carve(KT * AR).rearrange("p (k c) -> p k c", k=KT)
        b3 = carve(HID)
        lang_i = carve(TILES).bitcast(I32)
        assert off[0] <= 2 * GROUPS * F
        off[0] = 0
        pool_ = act_t[:].rearrange("p f t -> p (f t)")
        lang = carve(TILES)
        route = [carve(TILES * E3).rearrange("p (t e) -> p t e", t=TILES) for _ in range(8)]
        route1 = [carve(TILES) for _ in range(8)]
        hg = carve(TILES * P).rearrange("p (t c) -> p t c", t=TILES)
        hgT = carve(TILES * P).rearrange("p (t c) -> p t c", t=TILES)
        xnat = carve(TILES * HID).rearrange("p (t h) -> p t h", t=TILES)
        res = carve(TILES * HID).rearrange("p (t h) -> p t h", t=TILES)

        ident_in = sem("ident_in")
        keyno_in = sem("keyno_in")
        const_in = sem("const_in")
        setup_in = sem("setup_in")
        table_in = sem("table_in")
        xt_in = sem("xt_in")
        y_in = sem("y_in")
        w_in = [sem(f"w_in{n}") for n in range(BLOCKS)]
        wo_in = sem("wo_in")
        k_in = [sem(f"k_in{j}") for j in range(2)]
        v_in = [sem(f"v_in{j}") for j in range(2)]
        vrow_made = sem("vrow_made")
        zeroed = sem("zeroed")
        vrow_ready = sem("vrow_ready")
        setup_v = sem("setup_v")
        setup_a = sem("setup_a")
        tables_made = sem("tables_made")
        block_done = sem("block_done")
        squared = sem("squared")
        summed = sem("summed")
        var_made = sem("var_made")
        rstd_made = sem("rstd_made")
        scaled = sem("scaled")
        cos_done = sem("cos_done")
        sin_done = sem("sin_done")
        roped = sem("roped")
        turned = sem("turned")
        turn_read = sem("turn_read")
        own_k_in = sem("own_k_in")
        v_read = sem("v_read")
        bank_free = [sem(f"bank_free{j}") for j in range(MM_BANKS)]
        scored = sem("scored")
        new_masked = sem("new_masked")
        mask_made = sem("mask_made")
        masked = sem("masked")
        exped = sem("exped")
        inverted = sem("inverted")
        normed = sem("normed")
        probs_turned = sem("probs_turned")
        vector_went_on = sem("vector_went_on")
        pool_went_on = sem("pool_went_on")
        pt_read = sem("pt_read")
        pv_done = sem("pv_done")
        o_free = sem("o_free")
        out_done = sem("out_done")
        oT_free = sem("oT_free")
        y_added = sem("y_added")

        ad_in = sem("ad_in")
        bd_in = sem("bd_in")
        a2_in = sem("a2_in")
        agu_spread = sem("agu_spread")
        ad_spread = sem("ad_spread")
        a2_spread = sem("a2_spread")
        bgu_in = sem("bgu_in")
        agu_in = sem("agu_in")
        wd_in = sem("wd_in")
        wf_in = [sem(f"wf_in{j}") for j in range(2)]
        bf_in = [sem(f"bf_in{j}") for j in range(2)]
        l23_in = sem("l23_in")
        ids_in = sem("ids_in")
        y_turned = sem("y_turned")
        xa_made = sem("xa_made")
        low_done = sem("low_done")
        low_made = sem("low_made")
        gu_done = sem("gu_done")
        silu_done = sem("silu_done")
        act_made = sem("act_made")
        down_done = sem("down_done")
        xb_made = sem("xb_made")
        low2_done = sem("low2_done")
        low2_made = sem("low2_made")
        lin2_done = sem("lin2_done")
        x2_made = sem("x2_made")
        hr_done = sem("hr_done")
        rv = sem("rv")
        ratio_done = sem("ratio_done")
        hg_made = sem("hg_made")
        hg_turned = sem("hg_turned")
        hgt_made = sem("hgt_made")
        x_turned = sem("x_turned")
        xnat_made = sem("xnat_made")
        lin3_done = sem("lin3_done")
        res_made = sem("res_made")
        out_sent = sem("out_sent")

        def spread_group(raw, group, g, n):
            return (group.rearrange("p k (b r) -> p k b r", b=SEQ_PER_GROUP),
                    raw[:, SEQ_PER_GROUP * g:SEQ_PER_GROUP * (g + 1)].rearrange("p b (k r) -> p k b r", k=n))

        block = whole.enter_context(nc.Block())

        @block.sync
        def _(sp):
            def load_w(n, half):
                sp.dma_start(wqkv[:, n], t["wqkv"][half, n]).then_inc(w_in[n], 16)

            def load_wo(half):
                sp.dma_start(wo[:], t["wo"][half]).then_inc(wo_in, 16)

            def gather(b, half, parity):
                _, pages = nc.values_load_multi_w_load_instructions(
                    bass.at_runtime_partition(table[0:1, :], b), engines=(mybir.EngineType.SP,),
                    min_val=0, max_val=PAGES - 1,
                    skip_runtime_bounds_check_because="block tables hold page numbers")
                for j, page in enumerate(pages):
                    sp.dma_start(kc[:, parity, j, :],
                                 t["kcache"][half, bass.ds(page, 1)].rearrange("o d k -> (o d) k")
                                 ).then_inc(k_in[parity], 16)

            def gather_when_free(b, half, parity):
                sp.wait_ge(scored, HKH * (B * half + b - 1))
                gather(b, half, parity)

            def adapters(first, count, most):
                _, found = nc.values_load_multi_w_load_instructions(
                    ids[0:1, bass.ds(first, count)], engines=(mybir.EngineType.SP,), min_val=0, max_val=most,
                    skip_runtime_bounds_check_because="adapter numbers are below the adapters' count")
                return found

            sp.dma_start(table[:], t["table"]).then_inc(table_in, 16)
            sp.dma_start(xt[:], t["xt"][0]).then_inc(xt_in, 16)
            load_w(0, 0)
            sp.dma_start(ident[:], t["const"][:, C_IDENT:C_IDENT + P]).then_inc(ident_in, 16)
            sp.dma_start(keyno[:], t["const"][:, C_KEY:C_KEY + L]).then_inc(keyno_in, 16)
            for n in range(1, BLOCKS):
                load_w(n, 0)
            sp.wait_ge(table_in, 16)
            gather(0, 0, 0)
            load_wo(0)
            sp.dma_start(ids[:], t["ids"]).then_inc(ids_in, 16)
            sp.wait_ge(ids_in, 16)
            sp.dma_start(own[:], t["const"][:, C_OWN:C_OWN + GTOK]).then_inc(const_in, 16)
            sp.dma_start(small[:], t["const"][:, C_EXPERT:C_EXPERT + 2 * E3]).then_inc(const_in, 16)
            sp.dma_start(y[:], t["x"]).then_inc(y_in, 16)
            gather(1, 0, 1)
            with sp.Fori(1, 14) as pair:
                for j in range(2):
                    gather_when_free(2 * pair + j, 0, j)
            for n in range(BLOCKS):
                if n == 4:
                    gather_when_free(28, 0, 0)
                sp.wait_ge(block_done, BLOCKS * (TILES - 1) + n + 1)
                load_w(n, 1)
            for b in range(29, B):
                gather_when_free(b, 0, b % 2)
            for b in range(2):
                gather_when_free(b, 1, b)
            sp.wait_ge(out_done, TILES)
            load_wo(1)
            with sp.Fori(1, B // 2 - 1) as pair:
                for j in range(2):
                    gather_when_free(2 * pair + j, 1, j)

            sp.wait_ge(turned, 5 * STEPS)
            with sp.Fori(0, GROUPS) as g:
                for j, r in enumerate(adapters(g * SEQ_PER_GROUP, SEQ_PER_GROUP, 15)):
                    sp.dma_start(a_gu_raw[:, bass.ds(g * SEQ_PER_GROUP + j, 1)].rearrange("p o w c -> p (o w c)"),
                                 t["a_gu"][bass.ds(r, 1)].rearrange("o p c -> (o p) c")).then_inc(agu_in, 16)
            for b in range(B - 2, B):
                gather_when_free(b, 1, b % 2)

            def load_f(f, j):
                sp.dma_start(w_f[j][:].rearrange("p w k m -> p (w k m)"),
                             t["w_gu"][bass.ds(f, 1)].rearrange("o p c -> (o p) c")).then_inc(wf_in[j], 16)

            def spread_f(f, j, m):
                sp.dma_start(b_f[:, j, :, :, 0:m].rearrange("p g w m -> p (g w) m"),
                             b_gu[:, :, :, bass.ds(f * P, m)].rearrange("p g w m -> p (g w) m")
                             ).then_inc(bf_in[j], 16)

            sp.wait_ge(block_done, BLOCKS * STEPS)
            load_f(0, 0)
            load_f(1, 1)
            with sp.Fori(0, GROUPS) as g:
                for j, r in enumerate(adapters(g * SEQ_PER_GROUP, SEQ_PER_GROUP, 15)):
                    sp.dma_start(b_gu[RANK * j:RANK * j + RANK, bass.ds(g, 1)].rearrange("p o w f -> p (o w f)"),
                                 t["b_gu"][bass.ds(r, 1)].rearrange("o p c -> (o p) c")).then_inc(bgu_in, 16)
            sp.wait_ge(bgu_in, 16 * B)
            sp.wait_ge(agu_spread, 2 * GROUPS)
            spread_f(0, 0, P)
            spread_f(1, 1, P)
            sp.wait_ge(out_done, STEPS)
            sp.wait_ge(y_added, STEPS)
            sp.wait_ge(o_free, STEPS * PAIRS + 1)
            sp.dma_start(w_d[:], t["w_d"]).then_inc(wd_in, 16)

            def load_a_d(h):
                with sp.Fori(0, GROUPS // 2) as g:
                    for j, r in enumerate(adapters(g * SEQ_PER_GROUP + h * (B // 2), SEQ_PER_GROUP, 15)):
                        sp.dma_start(a_d_raw[:, bass.ds(g * SEQ_PER_GROUP + j, 1)].rearrange("p o c -> p (o c)"),
                                     t["a_d"][bass.ds(r, 1)].rearrange("o p c -> (o p) c")).then_inc(ad_in, 16)

            sp.wait_ge(y_turned, TILES)
            load_a_d(0)
            sp.wait_ge(low_done, 4)
            with sp.Fori(0, GROUPS) as g:
                for j, r in enumerate(adapters(g * SEQ_PER_GROUP, SEQ_PER_GROUP, 15)):
                    sp.dma_start(b_d[RANK * j:RANK * j + RANK, bass.ds(g, 1)].rearrange("p o f -> p (o f)"),
                                 t["b_d"][bass.ds(r, 1)].rearrange("o p c -> (o p) c")).then_inc(bd_in, 16)

            def next_f(f, j, m):
                sp.wait_ge(gu_done, 4 * (f - 1))
                load_f(f, j)
                spread_f(f, j, m)

            next_f(2, 0, P)
            next_f(3, 1, P)
            sp.wait_ge(ad_spread, GROUPS // 2)
            load_a_d(1)
            with sp.Fori(0, GROUPS) as g:
                for j, r in enumerate(adapters(g * SEQ_PER_GROUP + B, SEQ_PER_GROUP, 31)):
                    sp.dma_start(a2_raw[:, bass.ds(g * SEQ_PER_GROUP + j, 1)].rearrange("p o c -> p (o c)"),
                                 t["a2"][bass.ds(r, 1)].rearrange("o p c -> (o p) c")).then_inc(a2_in, 16)
            with sp.Fori(2, FT // 2) as i:
                next_f(2 * i, 0, P)
                next_f(2 * i + 1, 1, P)
            next_f(FT - 1, 0, FLAST)
            for j in range(2):
                sp.wait_ge(bf_in[j], 16 * ((FT + 1 - j) // 2))
            sp.dma_start(w2, t["w2"]).then_inc(l23_in, 16)
            sp.dma_start(bias2, t["bias2"]).then_inc(l23_in, 16)
            with sp.Fori(0, GROUPS) as g:
                for j, r in enumerate(adapters(g * SEQ_PER_GROUP + B, SEQ_PER_GROUP, 31)):
                    sp.dma_start(b2[RANK * j:RANK * j + RANK, bass.ds(g, 1)].rearrange("p o f -> p (o f)"),
                                 t["b2"][bass.ds(r, 1)].rearrange("o p c -> (o p) c")).then_inc(l23_in, 16)
            sp.dma_start(w3, t["w3"]).then_inc(l23_in, 16)
            sp.dma_start(ar3, t["ar3"]).then_inc(l23_in, 16)
            sp.dma_start(b3, t["b3"]).then_inc(l23_in, 16)
            sp.dma_start(lang_i, t["lang"]).then_inc(l23_in, 16)
            for tile in range(TILES):
                sp.wait_ge(res_made, tile + 1)
                sp.dma_start(t["out"][:, tile, :], res[:, tile, :]).then_inc(out_sent, 16)
            sp.wait_ge(out_sent, 16 * TILES)

        L23_ALL = 16 * (6 + B)

        @block.tensor
        def _(pe):
            def project(n, part, tile, half1):
                b, before = bank_use("block", n, tile=tile)
                if part == 0:
                    if n == 0:
                        pe.wait_ge(xt_in, 16 * (tile + 1))
                    pe.wait_ge(w_in[n], half1)
                    if not isinstance(before, int) or before > 0:
                        pe.wait_ge(bank_free[b], before)
                for k in (2 * part, 2 * part + 1):
                    last = nc.tensor.matmul(mm[:, b], xt[:, k], wqkv[:, n, k], start=(k == 0), stop=(k == KT - 1))
                if part == 1:
                    last.then_inc(block_done, 1)

            def turn(m, tile):
                b, before = bank_use("turn", m, tile=tile)
                pe.wait_ge(roped, 5 * tile + m + 1)
                pe.wait_ge(bank_free[b], before)
                for h in range(4):
                    last = nc.tensor.transpose(mm[:, b, h * P:(h + 1) * P], qn[:, h * P:(h + 1) * P], ident[:])
                last.then_inc(turned, 1)

            def scores(s, k, par):
                b, g = k // HKH, k % HKH
                pe.wait_ge(masked, PAIRS * s + k)
                if k == 0:
                    pe.wait_ge(turn_read, 5 * (s + 1))
                if g == 0:
                    pe.wait_ge(k_in[b % 2], 16 * NPP * (2 * s + b // 2 + 1))
                    pe.wait_ge(own_k_in, SEQ_PER_TILE * s + b + 1)
                q = qT[:, par, g, b, :]
                nc.tensor.matmul(sc[:, SC0:512], q, kc[:, b % 2, 0:NPP // 2, PSIZE * g:PSIZE * g + PSIZE],
                                 start=True, stop=True)
                nc.tensor.matmul(sc[:, 512:SC0 + KEYS], q, kc[:, b % 2, NPP // 2:NPP + 1, PSIZE * g:PSIZE * g + PSIZE],
                                 start=True, stop=True).then_inc(scored, 1)

            def turn_probs(s, k):
                pe.wait_ge(normed, PAIRS * s + k + 1)
                pe.wait_ge(pt_read, 2 * (PAIRS * s + k))
                for c in range(CHUNKS):
                    nc.tensor.transpose(pt_ps[:, c * P:(c + 1) * P], probs[:, k % 2, c * P:(c + 1) * P], ident[:])
                c0 = L - S * (k // HKH)
                nc.tensor.transpose(pt_ps[:, L:L + P], probs[:, k % 2, c0:c0 + P], ident[:]).then_inc(probs_turned, 1)

            def values(s, k, par):
                b, g = k // HKH, k % HKH
                pe.wait_ge(pt_read, 2 * (PAIRS * s + k + 1))
                pe.wait_ge(o_free, PAIRS * s + k + 1)
                if g == 0:
                    pe.wait_ge(v_in[b % 2], 16 * CHUNKS * (2 * s + b // 2 + 1))
                for c in range(CHUNKS):
                    nc.tensor.matmul(o_ps[:, 0:P], vc[:, b % 2, c, D * g:D * g + D],
                                     pT[:, k % 2, c * P:(c + 1) * P], start=(c == 0), stop=False)
                if k == 0:
                    pe.wait_ge(v_read, s + 1)
                nc.tensor.matmul(o_ps[:, 0:P], vN[:, par, g, :], pT_own[:, b, k % 2, :],
                                 start=False, stop=True).then_inc(pv_done, 1)

            def output(s, half1, last):
                b, before = bank_use("out", 0, step=s, last=last)
                pe.wait_ge(o_free, PAIRS * (s + 1) + 1)
                pe.wait_ge(wo_in, half1)
                pe.wait_ge(bank_free[b], before)
                for h in range(HQH):
                    mmul = nc.tensor.matmul(mm[:, b], oT[:, h, :], wo[:, h, :], start=(h == 0), stop=(h == HQH - 1))
                mmul.then_inc(out_done, 1)

            def step(s, par, last=False):
                for k in range(PAIRS):
                    if not last:
                        w_half = 16 * (1 + (s + 1) // TILES)
                        for m in range(5):
                            if turn_slot(m) == k:
                                turn(m, s + 1)
                        for n in range(BLOCKS):
                            if k in block_slots(n):
                                project(n, k - 2 * n, s + 1, w_half)
                    if k + 2 < PAIRS:
                        scores(s, k + 2, par)
                    elif not last:
                        scores(s + 1, k + 2 - PAIRS, 1 - par)
                    values(s, k, par)
                    if k + 1 < PAIRS:
                        turn_probs(s, k + 1)
                    elif not last:
                        turn_probs(s + 1, 0)
                output(s, 16 * (1 + s // TILES), last)

            pe.sem_inc(probs_turned, 2)
            pe.wait_ge(ident_in, 16)
            for what, n in BANK_ORDER[:PROLOGUE_USES]:
                if what == "block":
                    project(n, 0, 0, 16)
                    project(n, 1, 0, 16)
                else:
                    turn(n, 0)
            scores(0, 0, 0)
            scores(0, 1, 0)
            turn_probs(0, 0)
            with pe.Fori(0, STEPS // 2 - 1) as i:
                step(2 * i, 0)
                step(2 * i + 1, 1)
            step(STEPS - 2, 0)
            step(STEPS - 1, 1, last=True)

            pe.wait_ge(y_added, STEPS)
            for tile in range(TILES):
                for k in range(KT):
                    last = nc.tensor.transpose(bank[:, tile, k * P:(k + 1) * P], y[:, tile, k * P:(k + 1) * P], ident[:])
                last.then_inc(y_turned, 1)

            pe.wait_ge(agu_spread, 2 * GROUPS)
            pe.wait_ge(xa_made, TILES)
            for w in range(2):
                for g in range(GROUPS):
                    o = bank[:, 2 * w + g // 2, GTOK * (g % 2):GTOK * (g % 2) + GTOK]
                    for k in range(KT):
                        last = nc.tensor.matmul(o, a_gu[:, w, g, k, :],
                                                xA[:, k, GTOK * g:GTOK * (g + 1)], start=(k == 0), stop=(k == KT - 1))
                    if g % 2 == 1:
                        last.then_inc(low_done, 1)

            def gate_up(pair, j, m):
                pe.wait_ge(wf_in[j], 16 * (pair + 1))
                pe.wait_ge(bf_in[j], 16 * (pair + 1))
                f = 2 * pair + j
                for n in range(2):
                    for w in range(2):
                        o = bank[0:m, 4 * j + 2 * w + n, :]
                        if not isinstance(pair, int) or pair >= 1:
                            pe.wait_ge(act_made, 2 * (f - 2) + n + 1)
                        for k in range(KT):
                            nc.tensor.matmul(o, w_f[j][:, w, k, 0:m], xA[:, k, NTOK * n:NTOK * (n + 1)],
                                             start=(k == 0), stop=False)
                        for g in range(2 * n, 2 * n + 2):
                            last = nc.tensor.matmul(o[:, GTOK * (g % 2):GTOK * (g % 2) + GTOK], b_f[:, j, g, w, 0:m],
                                                    low[:, w, GTOK * g:GTOK * (g + 1)], start=False, stop=(g == 2 * n + 1))
                        last.then_inc(gu_done, 1)

            pe.wait_ge(low_made, 4)
            gate_up(0, 0, P)
            gate_up(0, 1, P)
            with pe.Fori(1, FT // 2) as i:
                gate_up(i, 0, P)
                gate_up(i, 1, P)
            gate_up(FT // 2, 0, FLAST)

            pe.wait_ge(act_made, 2 * FT)
            pe.wait_ge(ad_spread, GROUPS)
            for g in range(GROUPS):
                for f in range(FT):
                    m = P if f < FT - 1 else FLAST
                    last = nc.tensor.matmul(bank[:, g // 2, GTOK * (g % 2):GTOK * (g % 2) + GTOK],
                                            a_d[0:m, g, f, :],
                                            act_t[0:m, f, GTOK * g:GTOK * (g + 1)], start=(f == 0), stop=(f == FT - 1))
                if g % 2 == 1:
                    last.then_inc(low_done, 1)
            pe.wait_ge(wd_in, 16)
            pe.wait_ge(bd_in, 16 * B)
            for c in range(KT):
                for n in range(2):
                    i = 2 * c + n
                    o = bank[:, (i + 2) % 8, :]
                    if i >= 6:
                        pe.wait_ge(low_made, 4 + i - 6 + 1)
                    for f in range(FT):
                        m = P if f < FT - 1 else FLAST
                        nc.tensor.matmul(o, w_d[0:m, f, c * P:(c + 1) * P], act_t[0:m, f, NTOK * n:NTOK * (n + 1)],
                                         start=(f == 0), stop=False)
                    pe.wait_ge(low_made, 6)
                    for g in range(2 * n, 2 * n + 2):
                        last = nc.tensor.matmul(o[:, GTOK * (g % 2):GTOK * (g % 2) + GTOK], b_d[:, g, c * P:(c + 1) * P],
                                                low[:, 0, GTOK * g:GTOK * (g + 1)], start=False, stop=(g == 2 * n + 1))
                    last.then_inc(down_done, 1)

            pe.wait_ge(l23_in, L23_ALL)
            pe.wait_ge(a2_spread, GROUPS)
            pe.wait_ge(xb_made, 2 * KT)
            for g in range(GROUPS):
                for k in range(KT):
                    last = nc.tensor.matmul(bank[:, g // 2, GTOK * (g % 2):GTOK * (g % 2) + GTOK],
                                            a2[:, g, k, :],
                                            xB[:, k, GTOK * g:GTOK * (g + 1)], start=(k == 0), stop=(k == KT - 1))
                if g % 2 == 1:
                    last.then_inc(low2_done, 1)
            for c in range(KT):
                for n in range(2):
                    i = 2 * c + n
                    o = bank[:, (i + 2) % 8, :]
                    if i >= 6:
                        pe.wait_ge(low2_made, i - 6 + 1)
                    for k in range(KT):
                        nc.tensor.matmul(o, w2[:, k, c * P:(c + 1) * P], xB[:, k, NTOK * n:NTOK * (n + 1)],
                                         start=(k == 0), stop=False)
                    pe.wait_ge(low2_made, 2)
                    for g in range(2 * n, 2 * n + 2):
                        last = nc.tensor.matmul(o[:, GTOK * (g % 2):GTOK * (g % 2) + GTOK], b2[:, g, c * P:(c + 1) * P],
                                                low[:, 1, GTOK * g:GTOK * (g + 1)], start=False, stop=(g == 2 * n + 1))
                    last.then_inc(lin2_done, 1)

            pe.wait_ge(x2_made, 2 * KT)
            for tile in range(TILES):
                o = bank[:, tile // 3, AR * (tile % 3):AR * (tile % 3) + AR]
                for k in range(KT):
                    last = nc.tensor.matmul(o, xA[:, k, tile * P:(tile + 1) * P], ar3[:, k, :],
                                            start=(k == 0), stop=(k == KT - 1))
            last.then_inc(hr_done, 1)
            for tile in range(TILES):
                if tile >= 2:
                    pe.wait_ge(xnat_made, tile - 1)
                for k in range(KT):
                    last = nc.tensor.transpose(bank[:, 3 + tile % 2, k * P:(k + 1) * P], xA[:, k, tile * P:(tile + 1) * P], ident[:])
                last.then_inc(x_turned, 1)
            for h in range(2):
                pe.wait_ge(hg_made, 4 * (h + 1))
                if h == 0:
                    pe.wait_ge(xnat_made, TILES)
                for tile in range(4 * h, 4 * h + 4):
                    last = nc.tensor.transpose(bank[:, 3 + h, P * (tile % 4):P * (tile % 4) + P], hg[:, tile, :], ident[:])
                last.then_inc(hg_turned, 1)
            for tile in range(TILES):
                o = bank[:, 5 + tile % 3, :]
                if tile >= 3:
                    pe.wait_ge(res_made, tile - 2)
                for k in range(KT):
                    nc.tensor.matmul(o, xA[:, k, tile * P:(tile + 1) * P], w3[:, k, :], start=(k == 0), stop=False)
                pe.wait_ge(hgt_made, tile // 4 + 1)
                nc.tensor.matmul(o, hgT[:, tile, :], b3, start=False, stop=True).then_inc(lin3_done, 1)

        @block.scalar
        def _(act):
            def square(n, tile):
                b, _ = bank_use("block", n, tile=tile)
                act.wait_ge(block_done, BLOCKS * tile + n + 1)
                i = 5 * tile + n
                act.wait_ge(summed, i)
                nc.scalar.activation(sq[:], mm[:, b], ACT.Square).then_inc(squared, 1)

            def read_v(tile, par):
                b, _ = bank_use("block", 5, tile=tile)
                act.wait_ge(block_done, BLOCKS * tile + 6)
                r = nc.scalar.copy(vN[:, par].rearrange("p g d -> p (g d)"), mm[:, b])
                r.then_inc(v_read, 1)
                act.wait_ge(v_read, tile + 1)
                act.sem_inc(bank_free[b], 1)

            def read_turned(m, tile, par):
                b, _ = bank_use("turn", m, tile=tile)
                act.wait_ge(turned, 5 * tile + m + 1)
                if m < 4:
                    nc.scalar.copy(qT[:, par, m].rearrange("p b (h t) -> p b h t", h=REP),
                                   mm[:, b].rearrange("p (h b t) -> p b h t", h=REP, b=SEQ_PER_TILE)
                                   ).then_inc(turn_read, 1)
                else:
                    if not isinstance(tile, int) or tile > 0:
                        act.wait_ge(own_k_in, SEQ_PER_TILE * tile)
                    nc.scalar.copy(kTn[:].rearrange("p b (g t) -> p b g t", g=HKH),
                                   mm[:, b].rearrange("p (g b t) -> p b g t", g=HKH, b=SEQ_PER_TILE)
                                   ).then_inc(turn_read, 1)
                act.wait_ge(turn_read, 5 * tile + m + 1)
                act.sem_inc(bank_free[b], 1)

            def place_own_keys(tile, b):
                if b == 0:
                    act.wait_ge(turn_read, 5 * tile + 5)
                if not (isinstance(tile, int) and tile == 0 and b < 2):
                    act.wait_ge(scored, HKH * (SEQ_PER_TILE * tile + b - 1))
                nc.scalar.copy(kc[:, b % 2, NPP, :], kTn[:, b]).then_inc(own_k_in, 1)

            def exps(s, k):
                act.wait_ge(masked, PAIRS * s + k + 1)
                nc.scalar.activation(probs[:, k % 2, 0:KEYS], probs[:, k % 2, 0:KEYS], ACT.Exp, bias=minv[:, k % 2:k % 2 + 1],
                                     scale=-1.0, accum_out=psum_[:, k % 2:k % 2 + 1]).then_inc(exped, 1)

            def read_o(s, k):
                b, g = k // HKH, k % HKH
                act.wait_ge(pv_done, PAIRS * s + k + 1)
                if k == 0:
                    act.wait_ge(oT_free, s + 1)
                nc.scalar.copy(oT[:, REP * g:REP * g + REP, S * b:S * b + S],
                               o_ps[:, 0:P].rearrange("p (h t) -> p h t", h=REP)).then_inc(o_free, 1)

            def read_pt(s, k):
                act.wait_ge(probs_turned, 2 + PAIRS * s + k + 1)
                b = k // HKH
                nc.scalar.copy(pT_own[S * b:S * b + S, b, k % 2, :], pt_ps[S * b:S * b + S, L:L + P]).then_inc(pt_read, 1)
                nc.scalar.copy(pT[:, k % 2], pt_ps[:, 0:L]).then_inc(pt_read, 1)

            def load_xt(tile):
                act.wait_ge(block_done, BLOCKS * tile)
                act.dma_start(xt[:], t["xt"][bass.ds(tile % TILES, 1)].rearrange("o p k t -> (o p) k t")
                              ).then_inc(xt_in, 16)

            def step(s, par, last=False, load=True):
                for k in range(PAIRS):
                    if not last:
                        for m in range(5):
                            if turn_slot(m) == k:
                                read_turned(m, s + 1, 1 - par)
                        for n in range(BLOCKS):
                            if k == block_slots(n)[1]:
                                if n < 5:
                                    square(n, s + 1)
                                else:
                                    read_v(s + 1, 1 - par)
                    if k in (2, 6):
                        place_own_keys(s, 2 + k // 6)
                    if k in (13, 15) and not last:
                        place_own_keys(s + 1, k // 15)
                    if k + 2 < PAIRS:
                        exps(s, k + 2)
                    elif not last:
                        exps(s + 1, k + 2 - PAIRS)
                    read_o(s, k)
                    if k + 1 < PAIRS:
                        read_pt(s, k + 1)
                    elif not last:
                        read_pt(s + 1, 0)
                    if k == 12 and load:
                        load_xt(s + 2)

            act.sem_inc(o_free, 1)
            act.sem_inc(oT_free, 1)
            act.dma_start(seqlen_i, t["seqlen"]).then_inc(setup_in, 16)
            act.dma_start(seqtok_i, t["seqtok"]).then_inc(setup_in, 16)
            act.dma_start(sq[:, 64:64 + D // 2 + 1], t["const"][:, C_FREQ:C_FREQ + D // 2 + 1]).then_inc(setup_in, 16)
            act.dma_start(vpage_i, t["vpages"]).then_inc(setup_in, 16)
            act.dma_start(wq_row, t["qnorm"]).then_inc(setup_in, 16)
            act.dma_start(wk_row, t["knorm"]).then_inc(setup_in, 16)
            act.wait_ge(setup_v, 15)
            nc.scalar.activation(sin_t, red[:], ACT.Sin).then_inc(setup_a, 1)
            act.wait_ge(setup_v, 22)
            nc.scalar.activation(cos_t, trig[:], ACT.Sin).then_inc(setup_a, 1)
            act.wait_ge(zeroed, 3)
            act.wait_ge(tables_made, 1)
            for what, n in BANK_ORDER[:PROLOGUE_USES]:
                if what == "turn":
                    read_turned(n, 0, 0)
                elif n < 5:
                    square(n, 0)
                else:
                    read_v(0, 0)
            place_own_keys(0, 0)
            place_own_keys(0, 1)
            load_xt(1)
            exps(0, 0)
            exps(0, 1)
            read_pt(0, 0)
            with act.Fori(0, STEPS // 2 - 1) as i:
                step(2 * i, 0)
                step(2 * i + 1, 1)
            step(STEPS - 2, 0, load=False)
            step(STEPS - 1, 1, last=True, load=False)

            for tile in range(0, TILES, 2):
                act.wait_ge(y_turned, tile + 1)
                nc.scalar.copy(xA[:, :, tile * P:(tile + 1) * P],
                               bank[:, tile].rearrange("p (k t) -> p k t", k=KT)).then_inc(xa_made, 1)

            def silu(f, j, m):
                for n in range(2):
                    act.wait_ge(gu_done, 4 * f + 2 * n + 1)
                    i = 2 * f + n
                    if not isinstance(f, int) or i >= 2:
                        act.wait_ge(act_made, i - 1)
                    nc.scalar.activation(gated[0:m, n, :], bank[0:m, 4 * j + n, :], ACT.Silu).then_inc(silu_done, 1)

            silu(0, 0, P)
            silu(1, 1, P)
            with act.Fori(1, FT // 2) as i:
                silu(2 * i, 0, P)
                silu(2 * i + 1, 1, P)
            silu(FT - 1, 0, FLAST)

            for tile in range(TILES):
                act.wait_ge(x_turned, tile + 1)
                nc.scalar.copy(xnat[:, tile, :], bank[:, 3 + tile % 2, :]).then_inc(xnat_made, 1)
            act.wait_ge(rv, 12)
            nc.scalar.activation(route1[3], route1[2], ACT.Exp).then_inc(ratio_done, 1)
            for h in range(2):
                act.wait_ge(hg_turned, h + 1)
                nc.scalar.copy(hgT[:, 4 * h:4 * h + 4, :], bank[:, 3 + h].rearrange("p (t c) -> p t c", t=4)).then_inc(hgt_made, 1)

        @block.vector
        def _(dve):
            def norm_rows(n, tile):
                b, _ = bank_use("block", n, tile=tile)
                i = 5 * tile + n
                dve.wait_ge(squared, i + 1)
                nc.vector.tensor_reduce(ss, sq[:].rearrange("p (h d) -> p h d", h=4), AX.X, ALU.add).then_inc(summed, 1)
                dve.wait_ge(summed, i + 1)
                nc.vector.tensor_scalar(var, ss, 1.0 / D, ATT_EPS, ALU.mult, ALU.add).then_inc(var_made, 1)

            def scale_rows(n, tile):
                b, _ = bank_use("block", n, tile=tile)
                i = 5 * tile + n
                dve.wait_ge(rstd_made, i + 1)
                dve.wait_ge(sin_done, i)
                dve.wait_ge(cos_done, i)
                nc.vector.tensor_tensor(tq[:].rearrange("p (h d) -> p h d", h=4),
                                        mm[:, b].rearrange("p (h d) -> p h d", h=4),
                                        rstd.unsqueeze(2).to_broadcast([P, 4, D]), ALU.mult).then_inc(scaled, 1)
                dve.wait_ge(scaled, i + 1)
                dve.sem_inc(bank_free[b], 1)

            def rope_cos(n, tile):
                i = 5 * tile + n
                dve.wait_ge(roped, i)
                tab = (cosq if n < 4 else cosk)[:, bass.ds(tile % TILES, 1), :].to_broadcast([P, 4, D])
                nc.vector.tensor_tensor(rc[:].rearrange("p (h d) -> p h d", h=4),
                                        tq[:].rearrange("p (h d) -> p h d", h=4), tab, ALU.mult).then_inc(cos_done, 1)

            def make_mask(tile, b):
                i = SEQ_PER_TILE * tile + b
                col = seqlen[:, bass.ds((SEQ_PER_TILE * tile + b) % B, 1)]
                nc.vector.tensor_scalar(mask[:, b % 2, 0:L], keyno[:], col, NEG, ALU.is_ge, ALU.mult).then_inc(mask_made, 1)

            def mask_scores(s, k):
                b = k // HKH
                dve.wait_ge(scored, PAIRS * s + k + 1)
                if k % HKH == 0:
                    dve.wait_ge(mask_made, SEQ_PER_TILE * s + b + 1)
                dve.wait_ge(probs_turned, PAIRS * s + k + 1)
                dve.sem_inc(vector_went_on, 1)
                nc.vector.tensor_tensor_reduce(out=probs[:, k % 2, 0:KEYS], in0=sc[:, SC0:SC0 + KEYS], in1=mask[:, b % 2],
                                               scale=-SCALE, scalar=BIG, op0=ALU.add, op1=ALU.min,
                                               accum_out=minv[:, k % 2:k % 2 + 1]).then_inc(masked, 1)

            def norm_probs(s, k):
                dve.wait_ge(exped, PAIRS * s + k + 1)
                nc.vector.reciprocal(rinv[:, k % 2:k % 2 + 1], psum_[:, k % 2:k % 2 + 1]).then_inc(inverted, 1)
                dve.wait_ge(inverted, PAIRS * s + k + 1)
                nc.vector.tensor_scalar(probs[:, k % 2, 0:KEYS], probs[:, k % 2, 0:KEYS], rinv[:, k % 2:k % 2 + 1], None,
                                        ALU.mult).then_inc(normed, 1)

            def add_y(s, last):
                b, _ = bank_use("out", 0, step=s, last=last)
                dve.wait_ge(out_done, s + 1)
                dve.sem_inc(oT_free, 1)
                yt = y[:, bass.ds(s % TILES, 1), :].rearrange("p o h -> p (o h)")
                nc.vector.tensor_tensor(yt, mm[:, b], yt, ALU.add).then_inc(y_added, 1)
                dve.wait_ge(y_added, s + 1)
                dve.sem_inc(bank_free[b], 1)

            def step(s, par, last=False, first=False):
                for k in range(PAIRS):
                    if k + 1 < PAIRS:
                        norm_probs(s, k + 1)
                    elif not last:
                        norm_probs(s + 1, 0)
                    if k + 2 < PAIRS:
                        mask_scores(s, k + 2)
                    elif not last:
                        mask_scores(s + 1, k + 2 - PAIRS)
                    if not last:
                        for n in range(5):
                            if k == 2 * n + 1:
                                norm_rows(n, s + 1)
                            if k == 2 * n + 2:
                                scale_rows(n, s + 1)
                                rope_cos(n, s + 1)
                    if (k + 2) % HKH == 0:
                        b = (k + 2) // HKH + 1
                        if b < SEQ_PER_TILE:
                            dve.wait_ge(masked, PAIRS * s + k + 2)
                            make_mask(s, b)
                        elif not last:
                            dve.wait_ge(masked, PAIRS * s + k + 2)
                            make_mask(s + 1, b - SEQ_PER_TILE)
                add_y(s, last)

            n_setup = [0]

            def chain(ins):
                n_setup[0] += 1
                ins.then_inc(setup_v, 1)
                dve.wait_ge(setup_v, n_setup[0])

            dve.wait_ge(setup_in, 16 * 6)
            chain(nc.vector.tensor_copy(vpage, vpage_i))
            chain(nc.vector.tensor_scalar(vpage, vpage, float(PSIZE), step_, ALU.mult, ALU.add))
            for half in range(HALVES):
                chain(nc.vector.tensor_scalar(vrow[:, B * half:B * (half + 1)].rearrange("p b c -> p (b c)"), vpage,
                                              float(half * PAGES * PSIZE), None, ALU.add))
            dve.sem_inc(vrow_made, 1)
            chain(nc.vector.tensor_copy(seqlen, seqlen_i))
            chain(nc.vector.tensor_copy(pos, seqtok_i))
            chain(nc.vector.tensor_scalar(pos, pos, step_, None, ALU.add))
            halfd = D // 2
            a3, t3 = (x[:].rearrange("p (t f) -> p t f", t=TILES) for x in (ang, turns))
            chain(nc.vector.tensor_tensor(a3, pos.unsqueeze(2).to_broadcast([P, TILES, halfd]),
                                          freq.unsqueeze(1).to_broadcast([P, TILES, halfd]), ALU.mult))

            def reduce_angle(dst, quarter):
                chain(nc.vector.tensor_scalar(turns[:], ang[:], 1.0 / (2.0 * PI), quarter, ALU.mult, ALU.add))
                chain(nc.vector.tensor_scalar(turns[:], turns[:], ROUND, -ROUND, ALU.add, ALU.add))
                src = ang
                for part in (TWO_PI_1, TWO_PI_2, TWO_PI_3):
                    chain(nc.vector.scalar_tensor_tensor(out=dst[:], in0=turns[:], scalar=-part, in1=src[:],
                                                         op0=ALU.mult, op1=ALU.add))
                    src = dst
                chain(nc.vector.tensor_scalar(dst[:], dst[:], 2 * PI * quarter, PI_SAFE, ALU.add, ALU.min))
                chain(nc.vector.tensor_scalar(dst[:], dst[:], -PI_SAFE, None, ALU.max))

            reduce_angle(red, 0.0)
            reduce_angle(trig, 0.25)
            assert n_setup[0] == 22
            dve.wait_ge(setup_a, 2)
            s3, c3 = (x.rearrange("p (t f) -> p t f", t=TILES) for x in (sin_t, cos_t))
            for ctab, stab, w in ((cosq, sinq, wq_row), (cosk, sink, wk_row)):
                lo = w[:, 0:halfd].unsqueeze(1).to_broadcast([P, TILES, halfd])
                hi = w[:, halfd:D].unsqueeze(1).to_broadcast([P, TILES, halfd])
                chain(nc.vector.tensor_tensor(ctab[:, :, 0:halfd], c3, lo, ALU.mult))
                chain(nc.vector.tensor_tensor(ctab[:, :, halfd:D], c3, hi, ALU.mult))
                chain(nc.vector.scalar_tensor_tensor(out=stab[:, :, 0:halfd], in0=s3, scalar=-1.0, in1=hi,
                                                     op0=ALU.mult, op1=ALU.mult))
                chain(nc.vector.tensor_tensor(stab[:, :, halfd:D], s3, lo, ALU.mult))
            chain(nc.vector.memset(halfs, -0.5))
            dve.sem_inc(tables_made, 1)

            dve.wait_ge(keyno_in, 16)
            dve.wait_ge(zeroed, 3)
            make_mask(0, 0)
            make_mask(0, 1)
            for n in range(5):
                norm_rows(n, 0)
                scale_rows(n, 0)
                rope_cos(n, 0)
            mask_scores(0, 0)
            norm_probs(0, 0)
            mask_scores(0, 1)
            dve.wait_ge(const_in, 16 * 2)
            dve.wait_ge(y_in, 16)
            with dve.Fori(0, STEPS // 2 - 1) as i:
                step(2 * i, 0)
                step(2 * i + 1, 1)
            step(STEPS - 2, 0)
            step(STEPS - 1, 1, last=True)

            for tile in range(1, TILES, 2):
                dve.wait_ge(y_turned, tile + 1)
                nc.vector.tensor_copy(xA[:, :, tile * P:(tile + 1) * P],
                                      bank[:, tile].rearrange("p (k t) -> p k t", k=KT)).then_inc(xa_made, 1)

            own2 = own[:].unsqueeze(1).to_broadcast([P, 2, GTOK])

            def keep_own(i, src, dst, scale, done, made):
                dve.wait_ge(done, i)
                nc.vector.scalar_tensor_tensor(out=dst.rearrange("p (g t) -> p g t", g=2),
                                               in0=src.rearrange("p (g t) -> p g t", g=2), scalar=scale, in1=own2,
                                               op0=ALU.mult, op1=ALU.mult).then_inc(made, 1)

            for w in range(2):
                for h in range(2):
                    keep_own(2 * w + h + 1, bank[:, 2 * w + h, :], low[:, w, NTOK * h:NTOK * (h + 1)], 0.5,
                             low_done, low_made)

            def gate_times_up(f, j, m):
                for n in range(2):
                    dve.wait_ge(gu_done, 4 * f + 2 * n + 2)
                    dve.wait_ge(silu_done, 2 * f + n + 1)
                    nc.vector.tensor_tensor(act_t[0:m, bass.ds(f, 1), NTOK * n:NTOK * (n + 1)].rearrange("p o t -> p (o t)"),
                                            gated[0:m, n, :], bank[0:m, 4 * j + 2 + n, :], ALU.mult).then_inc(act_made, 1)

            gate_times_up(0, 0, P)
            gate_times_up(1, 1, P)
            with dve.Fori(1, FT // 2) as i:
                gate_times_up(2 * i, 0, P)
                gate_times_up(2 * i + 1, 1, P)
            gate_times_up(FT - 1, 0, FLAST)

            for h in range(2):
                keep_own(4 + h + 1, bank[:, h, :], low[:, 0, NTOK * h:NTOK * (h + 1)], 0.5, low_done, low_made)
            for c in range(KT):
                for n in range(2):
                    i = 2 * c + n
                    dve.wait_ge(down_done, i + 1)
                    nc.vector.tensor_tensor(xB[:, c, NTOK * n:NTOK * (n + 1)], bank[:, (i + 2) % 8, :],
                                            xA[:, c, NTOK * n:NTOK * (n + 1)], ALU.add).then_inc(xb_made, 1)
            for h in range(2):
                keep_own(h + 1, bank[:, h, :], low[:, 1, NTOK * h:NTOK * (h + 1)], 2.0, low2_done, low2_made)
            dve.wait_ge(l23_in, L23_ALL)
            for c in range(KT):
                for n in range(2):
                    i = 2 * c + n
                    dve.wait_ge(lin2_done, i + 1)
                    if i == 0:
                        dve.wait_ge(xb_made, 2 * KT)
                    nc.vector.scalar_tensor_tensor(out=xA[:, c, NTOK * n:NTOK * (n + 1)], in0=bank[:, (i + 2) % 8, :],
                                                   scalar=bias2[:, c:c + 1], in1=xB[:, c, NTOK * n:NTOK * (n + 1)],
                                                   op0=ALU.add, op1=ALU.add).then_inc(x2_made, 1)

            n_rv = [0]

            def link(ins):
                n_rv[0] += 1
                ins.then_inc(rv, 1)
                dve.wait_ge(rv, n_rv[0])

            def over_e(v):
                return v.unsqueeze(2).to_broadcast([P, TILES, E3])

            def over_t(v):
                return v.unsqueeze(1).to_broadcast([P, TILES, E3])

            logits, bias, eq, pick1, rest_, pick2, gates, tmp = route
            m1, m2, diff, ratio, den, w1, w2_, first = route1
            expert, firstness = small[:, 0:E3], small[:, E3:2 * E3]
            link(nc.vector.tensor_copy(lang, lang_i))
            link(nc.vector.tensor_tensor(bias, over_t(expert), over_e(lang), ALU.is_equal))
            dve.wait_ge(hr_done, 1)
            for tile in range(TILES):
                c0 = AR * (tile % 3) + E3 * RANK
                ins = nc.vector.scalar_tensor_tensor(out=logits[:, tile, :], in0=bias[:, tile, :], scalar=5.0,
                                                     in1=bank[:, tile // 3, c0:c0 + E3], op0=ALU.mult, op1=ALU.add)
            link(ins)
            link(nc.vector.tensor_reduce(m1, logits, AX.X, ALU.max))

            def pick(out, values_, top):
                link(nc.vector.tensor_tensor(eq, values_, over_e(top), ALU.is_equal))
                link(nc.vector.tensor_tensor(eq, eq, over_t(firstness), ALU.mult))
                link(nc.vector.tensor_reduce(first, eq, AX.X, ALU.max))
                link(nc.vector.tensor_tensor(out, eq, over_e(first), ALU.is_equal))

            pick(pick1, logits, m1)
            link(nc.vector.scalar_tensor_tensor(out=rest_, in0=pick1, scalar=NEG, in1=logits, op0=ALU.mult, op1=ALU.add))
            link(nc.vector.tensor_reduce(m2, rest_, AX.X, ALU.max))
            link(nc.vector.tensor_tensor(diff, m2, m1, ALU.subtract))
            assert n_rv[0] == 11
            dve.sem_inc(rv, 1)
            n_rv[0] += 1
            pick(pick2, rest_, m2)
            dve.wait_ge(ratio_done, 1)
            link(nc.vector.tensor_scalar(den, ratio, 1.0, None, ALU.add))
            link(nc.vector.reciprocal(w1, den))
            link(nc.vector.tensor_scalar(w1, w1, 2.0, None, ALU.mult))
            link(nc.vector.tensor_tensor(w2_, w1, ratio, ALU.mult))
            link(nc.vector.tensor_tensor(gates, pick1, over_e(w1), ALU.mult))
            link(nc.vector.tensor_tensor(tmp, pick2, over_e(w2_), ALU.mult))
            link(nc.vector.tensor_tensor(gates, gates, tmp, ALU.add))
            for tile in range(TILES):
                c0 = AR * (tile % 3)
                nc.vector.tensor_tensor(hg[:, tile, :].rearrange("p (e r) -> p e r", e=E3),
                                        bank[:, tile // 3, c0:c0 + E3 * RANK].rearrange("p (e r) -> p e r", e=E3),
                                        gates[:, tile, :].unsqueeze(2).to_broadcast([P, E3, RANK]), ALU.mult
                                        ).then_inc(hg_made, 1)
            for tile in range(TILES):
                dve.wait_ge(lin3_done, tile + 1)
                dve.wait_ge(xnat_made, tile + 1)
                nc.vector.tensor_tensor(res[:, tile, :], bank[:, 5 + tile % 3, :], xnat[:, tile, :], ALU.add).then_inc(res_made, 1)

        @block.gpsimd
        def _(pool):
            def root(i):
                pool.wait_ge(var_made, i + 1)
                nc.gpsimd.tensor_tensor(rstd, var, halfs, ALU.pow).then_inc(rstd_made, 1)

            def rope_sin(n, tile):
                i = 5 * tile + n
                half = D // 2
                pool.wait_ge(scaled, i + 1)
                pool.wait_ge(roped, i)
                pool.sem_inc(pool_went_on, 1)
                stab = sinq if n < 4 else sink
                t3 = tq[:].rearrange("p (h d) -> p h d", h=4)
                r3 = rs[:].rearrange("p (h d) -> p h d", h=4)
                tab = stab[:, bass.ds(tile % TILES, 1), :]
                nc.gpsimd.tensor_tensor(r3[:, :, 0:half], t3[:, :, half:D],
                                        tab[:, :, 0:half].to_broadcast([P, 4, half]), ALU.mult)
                nc.gpsimd.tensor_tensor(r3[:, :, half:D], t3[:, :, 0:half],
                                        tab[:, :, half:D].to_broadcast([P, 4, half]), ALU.mult).then_inc(sin_done, 1)
                pool.wait_ge(sin_done, i + 1)
                pool.wait_ge(cos_done, i + 1)
                pool.wait_ge(turned, i)
                nc.gpsimd.tensor_tensor(qn[:], rc[:], rs[:], ALU.add).then_inc(roped, 1)

            def gather_v(c, parity):
                if isinstance(c, int) and c < 2:
                    nc.gpsimd.tensor_copy(vrow_now[:, parity], vrow[:, c]).then_inc(vrow_ready, 1)
                else:
                    pool.wait_ge(pv_done, HKH * (c - 1))
                    pool.wait_ge(v_in[parity], 16 * CHUNKS * ((c - parity) // 2) if isinstance(c, int) else
                                 8 * CHUNKS * (c - parity))
                    pool.sem_inc(pool_went_on, 1)
                    nc.gpsimd.tensor_copy(vrow_now[:, parity],
                                          vrow[:, bass.ds(c, 1)].rearrange("p o c -> p (o c)")).then_inc(vrow_ready, 1)
                pool.wait_ge(vrow_ready, c + 1)
                pool.sem_inc(pool_went_on, 1)
                for i in range(CHUNKS):
                    nc.gpsimd.indirect_dma_start(
                        out=vc[:, parity, i, :], out_offset=None, in_=t["vcache"],
                        in_offset=bass.IndirectOffsetOnAxis(ap=vrow_now[:, parity, i:i + 1].bitcast(mybir.dt.uint32), axis=0)
                    ).then_inc(v_in[parity], 16)

            nc.gpsimd.memset(mask[:, :, L:KEYS], 0.0).then_inc(zeroed, 1)
            nc.gpsimd.memset(probs[:, :, KEYS:L + P], 0.0).then_inc(zeroed, 1)
            nc.gpsimd.memset(pT_own[:], 0.0).then_inc(zeroed, 1)
            pool.wait_ge(vrow_made, 1)
            gather_v(0, 0)
            gather_v(1, 1)
            pool.wait_ge(tables_made, 1)
            for n in range(5):
                root(n)
                rope_sin(n, 0)
            with pool.Fori(1, STEPS) as tile:
                for n in range(5):
                    root(5 * tile + n)
                    rope_sin(n, tile)
                    if n in (1, 3):
                        gather_v(SEQ_PER_TILE * tile - 2 + n // 2, n // 2)
                for j in range(2):
                    gather_v(SEQ_PER_TILE * tile + j, j)
            for j in range(2):
                gather_v(HALVES * B - 2 + j, j)

            pool.wait_ge(agu_in, 16 * B)
            for w in range(2):
                for g in range(GROUPS):
                    nc.gpsimd.tensor_copy(*spread_group(a_gu_raw[:, :, w], a_gu[:, w, g], g, KT)).then_inc(agu_spread, 1)
            for h in range(2):
                pool.wait_ge(ad_in, 16 * (B // 2) * (h + 1))
                for g in range(GROUPS // 2):
                    nc.gpsimd.tensor_copy(*spread_group(a_d_raw, a_d[:, h * GROUPS // 2 + g], g, FT)).then_inc(ad_spread, 1)
            pool.wait_ge(a2_in, 16 * B)
            for j in range(2):
                pool.wait_ge(bf_in[j], 16 * ((FT + 1 - j) // 2))
            for g in range(GROUPS):
                nc.gpsimd.tensor_copy(*spread_group(a2_raw, a2[:, g], g, KT)).then_inc(a2_spread, 1)


def kernel(**inputs):
    import numpy as _np
    import concourse.bacc as _bacc
    from concourse import mybir as _mybir
    from concourse.bass_utils import run_bass_kernel_spmd as _run

    a = {k: _np.asarray(v) for k, v in inputs.items()}
    x = a["x"].reshape(TOK, HID)

    def by_k(w):
        return w.T.reshape(-1, P, w.shape[0]).transpose(1, 0, 2)

    wq, wk, wv, wo = (a["L0_cond_" + n] for n in ("Wq", "Wk", "Wv", "Wo"))
    wqkv = _np.stack([_np.stack(
        [by_k(wq[h * HQH * D + n * 512:h * HQH * D + (n + 1) * 512]) for n in range(4)]
        + [by_k(w[h * HKH * D:(h + 1) * HKH * D]) for w in (wk, wv)]) for h in range(HALVES)])
    f_pad = FT * P - F

    def rows_f(w):
        w = _np.pad(w, ((0, f_pad), (0, 0)))
        return w.reshape(FT, P, KT, P).transpose(0, 3, 2, 1)

    def low_rank(w, n):
        return w.reshape(w.shape[0], RANK, n, P).transpose(0, 3, 2, 1).reshape(w.shape[0], P, n * RANK)

    l1 = {k[len("L1_cond_"):]: v for k, v in a.items() if k.startswith("L1_cond_")}
    seq = a["itok_B_207_1644"]
    arrays = {
        "x": x.reshape(TILES, P, HID).transpose(1, 0, 2),
        "xt": x.reshape(TILES, P, KT, P).transpose(0, 3, 2, 1),
        "wqkv": wqkv,
        "wo": wo.T.reshape(HALVES, HQH, D, HID).transpose(0, 2, 1, 3),
        "kcache": a["L0_cond_k_cache"].reshape(PAGES, PSIZE, HALVES, HKH, D).transpose(2, 0, 4, 3, 1).reshape(
            HALVES, PAGES, D, HKH * PSIZE),
        "vcache": a["L0_cond_v_cache"].reshape(PAGES * PSIZE, HALVES, HKH * D).transpose(1, 0, 2).reshape(
            HALVES * PAGES * PSIZE, HKH * D),
        "vpages": _np.repeat(a["itok_Bx16_0_63"].reshape(B, CHUNKS, P // PSIZE), PSIZE, axis=2).transpose(2, 0, 1).reshape(
            P, B * CHUNKS),
        "table": a["itok_Bx16_0_63"],
        "seqlen": _np.broadcast_to(seq[None, :], (P, B)),
        "seqtok": _np.repeat(seq, S).reshape(TILES, P).T,
        "qnorm": _np.broadcast_to(a["L0_cond_q_norm_w"][None, :], (P, D)),
        "knorm": _np.broadcast_to(a["L0_cond_k_norm_w"][None, :], (P, D)),
        "const": constants(),
        "ids": _np.concatenate([a["itok_B_2_6"], a["itok_B_0_23"]])[None, :],
        "w_gu": _np.stack([rows_f(l1["W_gate"]), rows_f(l1["W_up"])], axis=2).reshape(FT, P, 2 * KT * P),
        "a_gu": _np.concatenate([low_rank(l1["A_gate"][0], KT), low_rank(l1["A_up"][0], KT)], axis=2),
        "b_gu": _np.concatenate([l1["B_gate"][0].transpose(0, 2, 1), l1["B_up"][0].transpose(0, 2, 1)], axis=2),
        "w_d": _np.pad(l1["W_down"].T, ((0, f_pad), (0, 0))).reshape(FT, P, HID).transpose(1, 0, 2),
        "a_d": low_rank(_np.pad(l1["A_down"][0], ((0, 0), (0, 0), (0, f_pad))), FT),
        "b_d": l1["B_down"][0].transpose(0, 2, 1),
        "w2": by_k(a["L2_cond_W"]),
        "bias2": a["L2_cond_b"].reshape(KT, P).T,
        "a2": a["L2_cond_lora_As"].reshape(B, KT, P, RANK).transpose(0, 2, 1, 3).reshape(B, P, KT * RANK),
        "b2": a["L2_cond_lora_Bs"],
        "w3": by_k(a["L3_cond_W"]),
        "ar3": by_k(_np.concatenate([a["L3_cond_A"].reshape(E3 * RANK, HID), a["L3_cond_Wr"]])),
        "b3": a["L3_cond_B"].transpose(0, 2, 1).reshape(E3 * RANK, HID),
        "lang": _np.repeat(a["itok_B_0_7"], S).reshape(TILES, P).T,
    }
    arrays = {f"in_{k}": _np.ascontiguousarray(v) for k, v in arrays.items()}
    nc = _bacc.Bacc("TRN2", target_bir_lowering=False, num_devices=1, dynamic_dma_scratch_size=3072)
    t = {k[3:]: nc.dram_tensor(k, v.shape, _mybir.dt.from_np(v.dtype), kind="ExternalInput").ap()
         for k, v in arrays.items()}
    t["out"] = nc.dram_tensor("out", (P, TILES, HID), F32, kind="ExternalOutput").ap()
    build(nc, t)
    r = _run(nc, [arrays], core_ids=[0])
    return r.results[0]["out"].transpose(1, 0, 2).reshape(B, S, HID)
```

```python
from contextlib import ExitStack

import numpy as np

import concourse.bass as bass
from concourse import mybir
from concourse.alu_op_type import AluOpType as ALU

ACT = mybir.ActivationFunctionType
AX = mybir.AxisListType
F32 = mybir.dt.float32
F32R = mybir.dt.float32r
I32 = mybir.dt.int32

P = 128
B, S, HID = 32, 32, 512
TOK = B * S
TILES = TOK // P
SEQ_PER_TILE = P // S
KT = HID // P
D = 128
HQ, HK = 32, 8
REP = HQ // HK
HALVES = 2
HKH = HK // HALVES
HQH = HQ // HALVES
PAGES, PSIZE, NPP = 64, 32, 16
L = PSIZE * NPP
CHUNKS = L // P
KEYS = L + S
STEPS = HALVES * TILES
PAIRS = SEQ_PER_TILE * HKH
BLOCKS = REP * HKH // 4 + 2
SCALE = 1.0 / float(np.sqrt(D))
ATT_EPS = 1e-6
NEG = -1e30
BIG = 3.0e38
F = 1376
FT = -(-F // P)
FLAST = F - (FT - 1) * P
RANK = 16
SEQ_PER_GROUP = P // RANK
GROUPS = B // SEQ_PER_GROUP
GTOK = TOK // GROUPS
E3 = 8
AR = E3 * RANK + E3
NTOK = 512

PI = 3.14159265358979
PI_SAFE = float(np.nextafter(np.float32(np.pi), np.float32(0)))
TWO_PI_1 = 6.28125
TWO_PI_2 = float(np.float32(np.floor((2 * np.pi - TWO_PI_1) * 2**21) / 2**21))
TWO_PI_3 = float(np.float32(2 * np.pi - TWO_PI_1 - TWO_PI_2))
ROUND = 12582912.0

C_IDENT = 0
C_KEY = C_IDENT + P
C_FREQ = C_KEY + L
C_STEP = C_FREQ + D // 2
C_OWN = C_STEP + 1
C_EXPERT = C_OWN + GTOK
C_FIRST = C_EXPERT + E3
C_COLS = C_FIRST + E3


def constants():
    c = np.zeros((P, C_COLS), np.float32)
    row = np.arange(P)
    c[:, C_IDENT:C_IDENT + P] = np.eye(P)
    c[:, C_KEY:C_KEY + L] = np.arange(L)
    c[:, C_FREQ:C_FREQ + D // 2] = (1.0 / np.float32(10000.0) ** (
        np.arange(0, D, 2, dtype=np.float32) / np.float32(D))).astype(np.float32)
    c[:, C_STEP] = row % S
    c[:, C_OWN:C_OWN + GTOK] = row[:, None] // RANK == np.arange(GTOK)[None, :] // S
    c[:, C_EXPERT:C_EXPERT + E3] = np.arange(E3)
    c[:, C_FIRST:C_FIRST + E3] = E3 - np.arange(E3)
    return c


BANK_ORDER = [("block", 0), ("block", 1), ("block", 2), ("turn", 0), ("block", 3), ("turn", 1),
              ("block", 4), ("turn", 2), ("block", 5), ("turn", 3), ("turn", 4), ("out", 0)]
PROLOGUE_USES = 11
SC0 = 512 - L // 2
MM_BANKS = 3


def bank_use(what, n, tile=None, step=None, last=False):
    i = BANK_ORDER.index((what, n))
    if last:
        u = PROLOGUE_USES + len(BANK_ORDER) * (STEPS - 1)
        return u % MM_BANKS, u // MM_BANKS
    if tile is not None and isinstance(tile, int) and tile == 0:
        return i % MM_BANKS, i // MM_BANKS
    if step is None:
        step = tile - 1
    u = PROLOGUE_USES + i
    return u % MM_BANKS, u // MM_BANKS + (len(BANK_ORDER) // MM_BANKS) * step


SPLITS = BLOCKS * KT + HQH
SPLIT_BUFS = 3
SPLIT_BUF = [j % SPLIT_BUFS for j in range(SPLITS - 1)] + [1]
USES = BLOCKS * (KT - 1) + HQH - 1


def head_split(h, last):
    return h if last else BLOCKS * KT + h


def splits_in_slot(k, last):
    if last:
        return range(3) if k == 13 else ()
    if k < 2 * BLOCKS - 1:
        return range(2 * k + SPLIT_BUFS, 2 * k + SPLIT_BUFS + 2)
    return range(k + 14, k + 15) if k < 2 * BLOCKS + 1 else ()


def product_of(s, j, last):
    if not last and j < BLOCKS * KT:
        n, k = divmod(j, KT)
        if k == KT - 1:
            return "block_done", BLOCKS * (s + 1) + n + 1
        return "w_used", USES * s + (KT - 1) * n + k + 1
    h = j - head_split(0, last)
    if h == HQH - 1:
        return "out_done", s + 1
    return "w_used", USES * s + (0 if last else BLOCKS * (KT - 1)) + h + 1


def product_before(s, j, last):
    if j >= SPLIT_BUFS:
        return product_of(s, j - (2 if j == SPLITS - 1 else SPLIT_BUFS), last)
    if isinstance(s, int) and s == 0:
        return None, 0
    return product_of(s - 1, (SPLITS - 4, SPLITS - 1, SPLITS - 2)[j], False)


def block_slots(n):
    return (2 * n, 2 * n + 1)


def turn_slot(m):
    return 2 * m + 5


def build(nc, t):
    with ExitStack() as whole:
        def sem(name):
            return whole.enter_context(nc.semaphore(name))

        def sb(scope, name, shape, dt=F32):
            return scope.enter_context(nc.sbuf_tensor(name, shape, dt))

        def ps(scope, name, shape, dt=F32):
            return scope.enter_context(nc.psum_tensor(name, shape, dt))

        ident = sb(whole, "ident", [P, P])
        ids = sb(whole, "ids", [1, 2 * B], I32)
        over_y = ExitStack()
        y = sb(over_y, "y", [P, TILES, HID])

        att = ExitStack()
        wqkv = sb(att, "wqkv", [P, BLOCKS, KT, 512])
        wo = sb(att, "wo", [P, HQH, HID])
        qT = sb(att, "qT", [P, 2, HKH, SEQ_PER_TILE, P])
        vN = sb(att, "vN", [P, 2, HKH, D])
        kc = sb(att, "kc", [P, 2, NPP + 1, HKH * PSIZE])
        vc = sb(att, "vc", [P, 2, CHUNKS, HKH * D])
        probs = sb(att, "probs", [P, 2, L + P])
        pT = sb(att, "pT", [P, 2, L])
        pT_own = sb(att, "pT_own", [P, SEQ_PER_TILE, 2, P])
        oT_hi = sb(att, "oT_hi", [P, HQH, P], F32R)
        oT_lo = sb(att, "oT_lo", [P, HQH, P], F32R)
        mask = sb(att, "mask", [P, KEYS])
        keyno = sb(att, "keyno", [P, L])
        rows = sb(att, "rows", [P, 80])
        seqlen_i = rows[:, 0:B].bitcast(I32)
        seqlen = rows[:, B:2 * B]
        minv, psum_, rinv = rows[:, 64:66], rows[:, 66:68], rows[:, 68:70]
        rows2 = sb(att, "rows2", [P, 16])
        ss, var, rstd, halfs = (rows2[:, 4 * j:4 * j + 4] for j in range(4))
        table = sb(att, "table", [B, NPP], I32)
        vrow = sb(att, "vrow", [P, HALVES * B, CHUNKS], I32)
        vrow_now = sb(att, "vrow_now", [P, 2, CHUNKS], I32)
        kTn = sb(att, "kTn", [P, SEQ_PER_TILE, HKH * S])
        xt = sb(att, "xt", [P, KT, P])
        angles = sb(att, "angles", [P, 2, TILES, D // 2])
        rope_w = sb(att, "rope_w", [P, 2, 2, D])
        tab = sb(att, "tab", [P, 2, 2, D])
        tq = sb(att, "tq", [P, 512])
        rc = sb(att, "rc", [P, 512])
        sq = rc
        rs = sb(att, "rs", [P, 512])
        qn = sb(att, "qn", [P, 512])
        xt_hi = sb(att, "xt_hi", [P, KT, P], F32R)
        xt_lo = sb(att, "xt_lo", [P, KT, P], F32R)
        w_hi = sb(att, "w_hi", [P, SPLIT_BUFS, 512], F32R)
        w_lo = sb(att, "w_lo", [P, SPLIT_BUFS, 512], F32R)
        sc = ps(att, "sc", [P, 1024])
        pt_ps = ps(att, "pt_ps", [P, 1024])
        o_ps = ps(att, "o_ps", [P, 512])
        mm = ps(att, "mm", [P, MM_BANKS, 512])
        spare = pT[:, 0, B * CHUNKS:L]
        seqtok_i = spare[:, 0:TILES].bitcast(I32)
        pos = spare[:, TILES:2 * TILES]
        freq = spare[:, 16:16 + D // 2]
        step_ = spare[:, 80:81]
        vpage_i = pT[:, 0, 0:B * CHUNKS].bitcast(I32)
        vpage = pT[:, 1, 0:B * CHUNKS]
        ang, turns, red, trig = tq, rc, rs, qn
        cos_t, sin_t = (angles[:, i].rearrange("p t f -> p (t f)") for i in range(2))
        att.close()

        rest = ExitStack()
        b_gu = sb(rest, "b_gu", [P, GROUPS, 2, F])
        w_f0 = sb(rest, "w_f0", [P, 2, KT, P])
        sb(rest, "gap0", [P, 256])
        xA = sb(rest, "xA", [P, KT, TOK])
        act_t = sb(rest, "act_t", [P, FT, TOK])
        a_d = sb(rest, "a_d", [P, GROUPS, FT, SEQ_PER_GROUP * RANK])
        w_d = sb(rest, "w_d", [P, FT, HID])
        low = sb(rest, "low", [P, 2, TOK])
        w_f1 = sb(rest, "w_f1", [P, 2, KT, P])
        own = sb(rest, "own", [P, GTOK])
        small = sb(rest, "small", [P, 2 * E3])
        w_f_hi0 = sb(rest, "w_f_hi0", [P, KT, P], F32R)
        sb(rest, "gap1", [P, 648 - KT * P])
        a_gu_raw = sb(rest, "a_gu_raw", [P, B, 2, KT * RANK])
        a_gu = sb(rest, "a_gu", [P, 2, GROUPS, KT, SEQ_PER_GROUP * RANK])
        w_f_hi = (w_f_hi0, sb(rest, "w_f_hi1", [P, KT, P], F32R))
        w_f_lo0 = sb(rest, "w_f_lo0", [P, KT, P], F32R)
        w_f = (w_f0, w_f1)
        bank = ps(rest, "bank", [P, 8, 512])
        rest.close()
        over_y.close()
        parts = ExitStack()
        x_hi = sb(parts, "x_hi", [P, KT, TOK], F32R)
        sb(parts, "gap2", [P, 2 * GROUPS * F + 2 * KT * P + 256])
        x_lo = sb(parts, "x_lo", [P, KT, TOK], F32R)
        sb(parts, "gap3", [P, FT * TOK + GROUPS * FT * P + FT * HID + 2 * TOK + 2 * KT * P + GTOK + 2 * E3
                           + 648 + 4 * GROUPS * P + 2 * NTOK])
        w_f_lo = (w_f_lo0, sb(parts, "w_f_lo1", [P, KT, P], F32R))
        parts.close()
        xB = y[:].rearrange("p t h -> p (t h)").rearrange("p (k t) -> p k t", k=KT)
        flat = a_gu[:].rearrange("p w g k c -> p (w g k c)")
        a_d_raw = flat[:, 0:B // 2 * FT * RANK].rearrange("p (b c) -> p b c", b=B // 2)
        b_d = flat[:, 0:GROUPS * HID].rearrange("p (g h) -> p g h", g=GROUPS)
        a2_raw = flat[:, GROUPS * HID:GROUPS * HID + B * KT * RANK].rearrange("p (b c) -> p b c", b=B)
        flat = a_gu_raw[:].rearrange("p b w c -> p (b w c)")
        b_f = flat[:, 0:4 * GROUPS * P].rearrange("p (j g w m) -> p j g w m", j=2, g=GROUPS, w=2)
        gated = flat[:, 4 * GROUPS * P:4 * GROUPS * P + 2 * NTOK].rearrange("p (n t) -> p n t", n=2)
        off = [0]
        pool_ = b_gu[:].rearrange("p g w f -> p (g w f)")

        def carve(n):
            a = off[0]
            off[0] += n
            return pool_[:, a:a + n]

        w2 = carve(KT * HID).rearrange("p (k h) -> p k h", k=KT)
        a2 = carve(B * KT * RANK).rearrange("p (g k c) -> p g k c", g=GROUPS, k=KT)
        b2 = carve(GROUPS * HID).rearrange("p (g h) -> p g h", g=GROUPS)
        bias2 = carve(KT)
        w3 = carve(KT * HID).rearrange("p (k h) -> p k h", k=KT)
        ar3 = carve(KT * AR).rearrange("p (k c) -> p k c", k=KT)
        b3 = carve(HID)
        lang_i = carve(TILES).bitcast(I32)
        assert off[0] <= 2 * GROUPS * F
        off[0] = 0
        pool_ = act_t[:].rearrange("p f t -> p (f t)")
        lang = carve(TILES)
        route = [carve(TILES * E3).rearrange("p (t e) -> p t e", t=TILES) for _ in range(8)]
        route1 = [carve(TILES) for _ in range(8)]
        hg = carve(TILES * P).rearrange("p (t c) -> p t c", t=TILES)
        hgT = carve(TILES * P).rearrange("p (t c) -> p t c", t=TILES)
        xnat = carve(TILES * HID).rearrange("p (t h) -> p t h", t=TILES)
        res = carve(TILES * HID).rearrange("p (t h) -> p t h", t=TILES)

        ident_in = sem("ident_in")
        keyno_in = sem("keyno_in")
        const_in = sem("const_in")
        setup_in = sem("setup_in")
        table_in = sem("table_in")
        xt_in = sem("xt_in")
        y_in = sem("y_in")
        w_in = [sem(f"w_in{n}") for n in range(BLOCKS)]
        wo_in = sem("wo_in")
        k_in = [sem(f"k_in{j}") for j in range(2)]
        v_in = [sem(f"v_in{j}") for j in range(2)]
        vrow_made = sem("vrow_made")
        zeroed = sem("zeroed")
        vrow_ready = sem("vrow_ready")
        setup_v = sem("setup_v")
        setup_a = sem("setup_a")
        tables_made = sem("tables_made")
        block_done = sem("block_done")
        xt_hi_made = sem("xt_hi_made")
        xt_lo_made = sem("xt_lo_made")
        w_hi_made = sem("w_hi_made")
        w_lo_made = sem("w_lo_made")
        w_used = sem("w_used")
        squared = sem("squared")
        summed = sem("summed")
        var_made = sem("var_made")
        rstd_made = sem("rstd_made")
        scaled = sem("scaled")
        tab_made = sem("tab_made")
        cos_done = sem("cos_done")
        sin_done = sem("sin_done")
        roped = sem("roped")
        turned = sem("turned")
        turn_read = sem("turn_read")
        own_k_in = sem("own_k_in")
        v_read = sem("v_read")
        bank_free = [sem(f"bank_free{j}") for j in range(MM_BANKS)]
        scored = sem("scored")
        mask_made = sem("mask_made")
        masked = sem("masked")
        exped = sem("exped")
        inverted = sem("inverted")
        normed = sem("normed")
        probs_turned = sem("probs_turned")
        vector_went_on = sem("vector_went_on")
        pool_went_on = sem("pool_went_on")
        pt_read = sem("pt_read")
        pv_done = sem("pv_done")
        o_hi_made = sem("o_hi_made")
        o_free = sem("o_free")
        out_done = sem("out_done")
        oT_free = sem("oT_free")
        y_added = sem("y_added")

        ad_in = sem("ad_in")
        bd_in = sem("bd_in")
        a2_in = sem("a2_in")
        ag_spread = sem("ag_spread")
        au_spread = sem("au_spread")
        ad_spread = sem("ad_spread")
        a2_spread = sem("a2_spread")
        bgu_in = sem("bgu_in")
        agu_in = sem("agu_in")
        wd_in = sem("wd_in")
        wf_in = [sem(f"wf_in{j}") for j in range(2)]
        bf_in = [sem(f"bf_in{j}") for j in range(2)]
        l23_in = sem("l23_in")
        ids_in = sem("ids_in")
        y_turned = sem("y_turned")
        xa_made = sem("xa_made")
        low_done = sem("low_done")
        low_made = sem("low_made")
        gu_done = sem("gu_done")
        x_hi_made = sem("x_hi_made")
        x_lo_made = sem("x_lo_made")
        wf_hi_made = sem("wf_hi_made")
        wf_lo_made = sem("wf_lo_made")
        x_lo_added = sem("x_lo_added")
        silu_done = sem("silu_done")
        act_made = sem("act_made")
        down_done = sem("down_done")
        xb_made = sem("xb_made")
        low2_done = sem("low2_done")
        low2_made = sem("low2_made")
        lin2_done = sem("lin2_done")
        x2_made = sem("x2_made")
        hr_done = sem("hr_done")
        rv = sem("rv")
        ratio_done = sem("ratio_done")
        hg_made = sem("hg_made")
        hg_turned = sem("hg_turned")
        hgt_made = sem("hgt_made")
        x_turned = sem("x_turned")
        xnat_made = sem("xnat_made")
        lin3_done = sem("lin3_done")
        res_made = sem("res_made")
        out_sent = sem("out_sent")

        def squares(tile):
            return probs[:, 0, 0:512] if isinstance(tile, int) and tile == 0 else sq[:]

        def spread_group(raw, group, g, n):
            return (group.rearrange("p k (b r) -> p k b r", b=SEQ_PER_GROUP),
                    raw[:, SEQ_PER_GROUP * g:SEQ_PER_GROUP * (g + 1)].rearrange("p b (k r) -> p k b r", k=n))

        block = whole.enter_context(nc.Block())

        @block.sync
        def _(sp):
            def load_w(n, half):
                sp.dma_start(wqkv[:, n], t["wqkv"][half, n]).then_inc(w_in[n], 16)

            def load_wo(half):
                sp.dma_start(wo[:], t["wo"][half]).then_inc(wo_in, 16)

            def gather(b, half, parity):
                _, pages = nc.values_load_multi_w_load_instructions(
                    bass.at_runtime_partition(table[0:1, :], b), engines=(mybir.EngineType.SP,),
                    min_val=0, max_val=PAGES - 1,
                    skip_runtime_bounds_check_because="block tables hold page numbers")
                for j, page in enumerate(pages):
                    sp.dma_start(kc[:, parity, j, :],
                                 t["kcache"][half, bass.ds(page, 1)].rearrange("o d k -> (o d) k")
                                 ).then_inc(k_in[parity], 16)

            def gather_when_free(b, half, parity):
                sp.wait_ge(scored, HKH * (B * half + b - 1))
                gather(b, half, parity)

            def adapters(first, count, most):
                _, found = nc.values_load_multi_w_load_instructions(
                    ids[0:1, bass.ds(first, count)], engines=(mybir.EngineType.SP,), min_val=0, max_val=most,
                    skip_runtime_bounds_check_because="adapter numbers are below the adapters' count")
                return found

            sp.dma_start(table[:], t["table"]).then_inc(table_in, 16)
            sp.dma_start(xt[:], t["xt"][0]).then_inc(xt_in, 16)
            load_w(0, 0)
            sp.dma_start(ident[:], t["const"][:, C_IDENT:C_IDENT + P]).then_inc(ident_in, 16)
            sp.dma_start(keyno[:], t["const"][:, C_KEY:C_KEY + L]).then_inc(keyno_in, 16)
            for n in range(1, BLOCKS):
                load_w(n, 0)
            sp.wait_ge(table_in, 16)
            gather(0, 0, 0)
            load_wo(0)
            sp.dma_start(ids[:], t["ids"]).then_inc(ids_in, 16)
            sp.wait_ge(ids_in, 16)
            sp.dma_start(y[:], t["x"]).then_inc(y_in, 16)
            gather(1, 0, 1)
            with sp.Fori(1, 14) as pair:
                for j in range(2):
                    gather_when_free(2 * pair + j, 0, j)
            for n in range(BLOCKS):
                if n == 4:
                    gather_when_free(28, 0, 0)
                sp.wait_ge(block_done, BLOCKS * (TILES - 1) + n + 1)
                load_w(n, 1)
            for b in range(29, B):
                gather_when_free(b, 0, b % 2)
            for b in range(2):
                gather_when_free(b, 1, b)
            sp.wait_ge(out_done, TILES)
            load_wo(1)
            with sp.Fori(1, B // 2 - 1) as pair:
                for j in range(2):
                    gather_when_free(2 * pair + j, 1, j)

            for b in range(B - 2, B):
                gather_when_free(b, 1, b % 2)
            sp.wait_ge(turned, 5 * STEPS)
            sp.wait_ge(own_k_in, SEQ_PER_TILE * STEPS)
            sp.wait_ge(tab_made, 4 * (STEPS + 1))
            with sp.Fori(0, GROUPS) as g:
                for j, r in enumerate(adapters(g * SEQ_PER_GROUP, SEQ_PER_GROUP, 15)):
                    sp.dma_start(a_gu_raw[:, bass.ds(g * SEQ_PER_GROUP + j, 1)].rearrange("p o w c -> p (o w c)"),
                                 t["a_gu"][bass.ds(r, 1)].rearrange("o p c -> (o p) c")).then_inc(agu_in, 16)

            def load_f(f, j):
                sp.dma_start(w_f[j][:].rearrange("p w k m -> p (w k m)"),
                             t["w_gu"][bass.ds(f, 1)].rearrange("o p c -> (o p) c")).then_inc(wf_in[j], 16)

            def spread_f(f, j, m):
                sp.dma_start(b_f[:, j, :, :, 0:m].rearrange("p g w m -> p (g w) m"),
                             b_gu[:, :, :, bass.ds(f * P, m)].rearrange("p g w m -> p (g w) m")
                             ).then_inc(bf_in[j], 16)

            sp.wait_ge(block_done, BLOCKS * STEPS)
            load_f(0, 0)
            with sp.Fori(0, GROUPS) as g:
                for j, r in enumerate(adapters(g * SEQ_PER_GROUP, SEQ_PER_GROUP, 15)):
                    sp.dma_start(b_gu[RANK * j:RANK * j + RANK, bass.ds(g, 1)].rearrange("p o w f -> p (o w f)"),
                                 t["b_gu"][bass.ds(r, 1)].rearrange("o p c -> (o p) c")).then_inc(bgu_in, 16)
            sp.wait_ge(bgu_in, 16 * B)
            sp.wait_ge(out_done, STEPS)
            sp.wait_ge(y_added, STEPS)
            sp.wait_ge(o_free, STEPS * PAIRS + 1)
            sp.dma_start(own[:], t["const"][:, C_OWN:C_OWN + GTOK]).then_inc(const_in, 16)
            sp.dma_start(small[:], t["const"][:, C_EXPERT:C_EXPERT + 2 * E3]).then_inc(const_in, 16)
            load_f(1, 1)
            sp.wait_ge(ag_spread, GROUPS)
            sp.wait_ge(au_spread, GROUPS)
            spread_f(0, 0, P)
            spread_f(1, 1, P)
            sp.dma_start(w_d[:], t["w_d"]).then_inc(wd_in, 16)

            def load_a_d(h):
                with sp.Fori(0, GROUPS // 2) as g:
                    for j, r in enumerate(adapters(g * SEQ_PER_GROUP + h * (B // 2), SEQ_PER_GROUP, 15)):
                        sp.dma_start(a_d_raw[:, bass.ds(g * SEQ_PER_GROUP + j, 1)].rearrange("p o c -> p (o c)"),
                                     t["a_d"][bass.ds(r, 1)].rearrange("o p c -> (o p) c")).then_inc(ad_in, 16)

            sp.wait_ge(low_done, 4)
            load_a_d(0)

            def next_f(f, j, m):
                sp.wait_ge(gu_done, 4 * (f - 1))
                load_f(f, j)
                spread_f(f, j, m)

            next_f(2, 0, P)
            next_f(3, 1, P)
            sp.wait_ge(ad_spread, GROUPS // 2)
            load_a_d(1)
            next_f(4, 0, P)
            next_f(5, 1, P)
            sp.wait_ge(ad_spread, GROUPS)
            with sp.Fori(0, GROUPS) as g:
                for j, r in enumerate(adapters(g * SEQ_PER_GROUP, SEQ_PER_GROUP, 15)):
                    sp.dma_start(b_d[RANK * j:RANK * j + RANK, bass.ds(g, 1)].rearrange("p o f -> p (o f)"),
                                 t["b_d"][bass.ds(r, 1)].rearrange("o p c -> (o p) c")).then_inc(bd_in, 16)
            next_f(6, 0, P)
            next_f(7, 1, P)
            with sp.Fori(0, GROUPS) as g:
                for j, r in enumerate(adapters(g * SEQ_PER_GROUP + B, SEQ_PER_GROUP, 31)):
                    sp.dma_start(a2_raw[:, bass.ds(g * SEQ_PER_GROUP + j, 1)].rearrange("p o c -> p (o c)"),
                                 t["a2"][bass.ds(r, 1)].rearrange("o p c -> (o p) c")).then_inc(a2_in, 16)
            with sp.Fori(4, FT // 2) as i:
                next_f(2 * i, 0, P)
                next_f(2 * i + 1, 1, P)
            next_f(FT - 1, 0, FLAST)
            for j in range(2):
                sp.wait_ge(bf_in[j], 16 * ((FT + 1 - j) // 2))
            sp.dma_start(w2, t["w2"]).then_inc(l23_in, 16)
            sp.dma_start(bias2, t["bias2"]).then_inc(l23_in, 16)
            with sp.Fori(0, GROUPS) as g:
                for j, r in enumerate(adapters(g * SEQ_PER_GROUP + B, SEQ_PER_GROUP, 31)):
                    sp.dma_start(b2[RANK * j:RANK * j + RANK, bass.ds(g, 1)].rearrange("p o f -> p (o f)"),
                                 t["b2"][bass.ds(r, 1)].rearrange("o p c -> (o p) c")).then_inc(l23_in, 16)
            sp.dma_start(w3, t["w3"]).then_inc(l23_in, 16)
            sp.dma_start(ar3, t["ar3"]).then_inc(l23_in, 16)
            sp.dma_start(b3, t["b3"]).then_inc(l23_in, 16)
            sp.dma_start(lang_i, t["lang"]).then_inc(l23_in, 16)
            for tile in range(TILES):
                sp.wait_ge(res_made, tile + 1)
                sp.dma_start(t["out"][:, tile, :], res[:, tile, :]).then_inc(out_sent, 16)
            sp.wait_ge(out_sent, 16 * TILES)

        L23_ALL = 16 * (6 + B)

        @block.tensor
        def _(pe):
            def project_first(n):
                b, before = bank_use("block", n, tile=0)
                if n == 0:
                    pe.wait_ge(xt_in, 16)
                pe.wait_ge(w_in[n], 16)
                if before > 0:
                    pe.wait_ge(bank_free[b], before)
                for k in range(KT):
                    last = nc.tensor.matmul(mm[:, b], xt[:, k], wqkv[:, n, k], start=(k == 0), stop=(k == KT - 1))
                last.then_inc(block_done, 1)

            def project(n, part, tile):
                b, before = bank_use("block", n, tile=tile)
                if part == 0:
                    if n == 0:
                        pe.wait_ge(xt_lo_made, tile)
                    pe.wait_ge(bank_free[b], before)
                for k in (2 * part, 2 * part + 1):
                    j = KT * n + k
                    pe.wait_ge(w_hi_made, SPLITS * (tile - 1) + j + 1)
                    nc.tensor.matmul(mm[:, b], xt_lo[:, k], w_hi[:, SPLIT_BUF[j]], start=(k == 0), stop=False)
                    nc.tensor.matmul(mm[:, b], xt_hi[:, k], w_hi[:, SPLIT_BUF[j]], start=False, stop=False)
                    pe.wait_ge(w_lo_made, SPLITS * (tile - 1) + j + 1)
                    nc.tensor.matmul(mm[:, b], xt_hi[:, k], w_lo[:, SPLIT_BUF[j]], start=False,
                                     stop=(k == KT - 1)).then_inc(block_done if k == KT - 1 else w_used, 1)

            def turn(m, tile):
                b, before = bank_use("turn", m, tile=tile)
                pe.wait_ge(roped, 5 * tile + m + 1)
                pe.wait_ge(bank_free[b], before)
                for h in range(4):
                    last = nc.tensor.transpose(mm[:, b, h * P:(h + 1) * P], qn[:, h * P:(h + 1) * P], ident[:])
                last.then_inc(turned, 1)

            def scores(s, k, par):
                b, g = k // HKH, k % HKH
                pe.wait_ge(masked, PAIRS * s + k)
                if k == 0:
                    pe.wait_ge(turn_read, 5 * (s + 1))
                if g == 0:
                    pe.wait_ge(k_in[b % 2], 16 * NPP * (2 * s + b // 2 + 1))
                    pe.wait_ge(own_k_in, SEQ_PER_TILE * s + b + 1)
                q = qT[:, par, g, b, :]
                nc.tensor.matmul(sc[:, SC0:512], q, kc[:, b % 2, 0:NPP // 2, PSIZE * g:PSIZE * g + PSIZE],
                                 start=True, stop=True)
                nc.tensor.matmul(sc[:, 512:SC0 + KEYS], q, kc[:, b % 2, NPP // 2:NPP + 1, PSIZE * g:PSIZE * g + PSIZE],
                                 start=True, stop=True).then_inc(scored, 1)

            def turn_probs(s, k):
                pe.wait_ge(normed, PAIRS * s + k + 1)
                pe.wait_ge(pt_read, 2 * (PAIRS * s + k))
                for c in range(CHUNKS):
                    nc.tensor.transpose(pt_ps[:, c * P:(c + 1) * P], probs[:, k % 2, c * P:(c + 1) * P], ident[:])
                c0 = L - S * (k // HKH)
                nc.tensor.transpose(pt_ps[:, L:L + P], probs[:, k % 2, c0:c0 + P], ident[:]).then_inc(probs_turned, 1)

            def values(s, k, par):
                b, g = k // HKH, k % HKH
                pe.wait_ge(pt_read, 2 * (PAIRS * s + k + 1))
                pe.wait_ge(o_free, PAIRS * s + k + 1)
                if g == 0:
                    pe.wait_ge(v_in[b % 2], 16 * CHUNKS * (2 * s + b // 2 + 1))
                for c in range(CHUNKS):
                    nc.tensor.matmul(o_ps[:, 0:P], vc[:, b % 2, c, D * g:D * g + D],
                                     pT[:, k % 2, c * P:(c + 1) * P], start=(c == 0), stop=False)
                if k == 0:
                    pe.wait_ge(v_read, s + 1)
                nc.tensor.matmul(o_ps[:, 0:P], vN[:, par, g, :], pT_own[:, b, k % 2, :],
                                 start=False, stop=True).then_inc(pv_done, 1)

            def output(s, last):
                b, before = bank_use("out", 0, step=s, last=last)
                pe.wait_ge(bank_free[b], before)
                for h in range(HQH):
                    if h % REP == 0:
                        pe.wait_ge(o_free, PAIRS * (s + 1) - HKH + h // REP + 2)
                    j = head_split(h, last)
                    pe.wait_ge(w_hi_made, SPLITS * s + j + 1)
                    nc.tensor.matmul(mm[:, b], oT_lo[:, h, :], w_hi[:, SPLIT_BUF[j]], start=(h == 0), stop=False)
                    nc.tensor.matmul(mm[:, b], oT_hi[:, h, :], w_hi[:, SPLIT_BUF[j]], start=False, stop=False)
                    pe.wait_ge(w_lo_made, SPLITS * s + j + 1)
                    nc.tensor.matmul(mm[:, b], oT_hi[:, h, :], w_lo[:, SPLIT_BUF[j]], start=False,
                                     stop=(h == HQH - 1)).then_inc(out_done if h == HQH - 1 else w_used, 1)

            def step(s, par, last=False):
                for k in range(PAIRS):
                    if not last and k == turn_slot(4):
                        turn(4, s + 1)
                    if not last and k > 0:
                        for n in range(BLOCKS):
                            if k in block_slots(n):
                                project(n, k - 2 * n, s + 1)
                    if k + 2 < PAIRS:
                        scores(s, k + 2, par)
                    elif not last:
                        scores(s + 1, k + 2 - PAIRS, 1 - par)
                    if not last and k == 0:
                        project(0, 0, s + 1)
                    if not last:
                        for m in range(4):
                            if turn_slot(m) == k:
                                turn(m, s + 1)
                    values(s, k, par)
                    if k + 1 < PAIRS:
                        turn_probs(s, k + 1)
                    elif not last:
                        turn_probs(s + 1, 0)
                output(s, last)

            pe.sem_inc(probs_turned, 2)
            pe.wait_ge(ident_in, 16)
            for what, n in BANK_ORDER[:PROLOGUE_USES]:
                if what == "block":
                    project_first(n)
                else:
                    turn(n, 0)
            scores(0, 0, 0)
            scores(0, 1, 0)
            turn_probs(0, 0)
            with pe.Fori(0, STEPS // 2 - 1) as i:
                step(2 * i, 0)
                step(2 * i + 1, 1)
            step(STEPS - 2, 0)
            step(STEPS - 1, 1, last=True)

            pe.wait_ge(y_added, STEPS)
            for tile in range(TILES):
                for k in range(KT):
                    last = nc.tensor.transpose(bank[:, tile, k * P:(k + 1) * P], y[:, tile, k * P:(k + 1) * P], ident[:])
                last.then_inc(y_turned, 1)

            pe.wait_ge(xa_made, TILES)
            for w in range(2):
                pe.wait_ge((ag_spread, au_spread)[w], GROUPS)
                for g in range(GROUPS):
                    o = bank[:, 2 * w + g // 2, GTOK * (g % 2):GTOK * (g % 2) + GTOK]
                    for k in range(KT):
                        last = nc.tensor.matmul(o, a_gu[:, w, g, k, :],
                                                xA[:, k, GTOK * g:GTOK * (g + 1)], start=(k == 0), stop=(k == KT - 1))
                    if g % 2 == 1:
                        last.then_inc(low_done, 1)

            def gate_up(pair, j, m):
                pe.wait_ge(wf_in[j], 16 * (pair + 1))
                f = 2 * pair + j
                for n in range(2):
                    for w in range(2):
                        o = bank[0:m, 4 * (1 - j) + 2 * w + n, :]
                        if not isinstance(pair, int) or pair >= 1:
                            pe.wait_ge(act_made, 2 * (f - 2) + n + 1)
                        cols = slice(NTOK * n, NTOK * (n + 1))
                        if n == 0:
                            pe.wait_ge(wf_hi_made, 2 * f + w + 1)
                        for k in range(KT):
                            if isinstance(pair, int) and f == 0 and w == 0:
                                pe.wait_ge(x_hi_made, KT * n + k + 1)
                            nc.tensor.matmul(o, w_f_hi[w][:, k, 0:m], x_hi[:, k, cols], start=(k == 0), stop=False)
                        if n == 0:
                            pe.wait_ge(wf_lo_made, 2 * f + w + 1)
                        for k in range(KT):
                            nc.tensor.matmul(o, w_f_lo[w][:, k, 0:m], x_hi[:, k, cols], start=False, stop=False)
                        for k in range(KT):
                            if isinstance(pair, int) and f == 0 and w == 0:
                                pe.wait_ge(x_lo_made, KT * n + k + 1)
                            nc.tensor.matmul(o, w_f_hi[w][:, k, 0:m], x_lo[:, k, cols], start=False, stop=False)
                        if n == 0 and w == 0:
                            pe.wait_ge(bf_in[j], 16 * (pair + 1))
                        if isinstance(pair, int) and f == 0:
                            pe.wait_ge(low_made, 4)
                        for g in range(2 * n, 2 * n + 2):
                            last = nc.tensor.matmul(o[:, GTOK * (g % 2):GTOK * (g % 2) + GTOK], b_f[:, j, g, w, 0:m],
                                                    low[:, w, GTOK * g:GTOK * (g + 1)], start=False, stop=(g == 2 * n + 1))
                        last.then_inc(gu_done, 1)

            gate_up(0, 0, P)
            gate_up(0, 1, P)
            with pe.Fori(1, FT // 2) as i:
                gate_up(i, 0, P)
                gate_up(i, 1, P)
            gate_up(FT // 2, 0, FLAST)

            pe.wait_ge(act_made, 2 * (FT - 1))
            pe.wait_ge(ad_spread, GROUPS)
            for g in range(GROUPS):
                for f in range(FT):
                    m = P if f < FT - 1 else FLAST
                    if g == 0 and f == FT - 1:
                        pe.wait_ge(act_made, 2 * FT)
                    last = nc.tensor.matmul(bank[:, g // 2, GTOK * (g % 2):GTOK * (g % 2) + GTOK],
                                            a_d[0:m, g, f, :],
                                            act_t[0:m, f, GTOK * g:GTOK * (g + 1)], start=(f == 0), stop=(f == FT - 1))
                if g % 2 == 1:
                    last.then_inc(low_done, 1)
            pe.wait_ge(wd_in, 16)
            pe.wait_ge(bd_in, 16 * B)
            for c in range(KT):
                for n in range(2):
                    i = 2 * c + n
                    o = bank[:, (i + 2) % 8, :]
                    if i >= 6:
                        pe.wait_ge(low_made, 4 + i - 6 + 1)
                    for f in range(FT):
                        m = P if f < FT - 1 else FLAST
                        nc.tensor.matmul(o, w_d[0:m, f, c * P:(c + 1) * P], act_t[0:m, f, NTOK * n:NTOK * (n + 1)],
                                         start=(f == 0), stop=False)
                    pe.wait_ge(low_made, 6)
                    for g in range(2 * n, 2 * n + 2):
                        last = nc.tensor.matmul(o[:, GTOK * (g % 2):GTOK * (g % 2) + GTOK], b_d[:, g, c * P:(c + 1) * P],
                                                low[:, 0, GTOK * g:GTOK * (g + 1)], start=False, stop=(g == 2 * n + 1))
                    last.then_inc(down_done, 1)

            pe.wait_ge(l23_in, L23_ALL)
            pe.wait_ge(a2_spread, GROUPS)
            pe.wait_ge(xb_made, 2 * KT)
            for g in range(GROUPS):
                for k in range(KT):
                    last = nc.tensor.matmul(bank[:, g // 2, GTOK * (g % 2):GTOK * (g % 2) + GTOK],
                                            a2[:, g, k, :],
                                            xB[:, k, GTOK * g:GTOK * (g + 1)], start=(k == 0), stop=(k == KT - 1))
                if g % 2 == 1:
                    last.then_inc(low2_done, 1)
            for c in range(KT):
                for n in range(2):
                    i = 2 * c + n
                    o = bank[:, (i + 2) % 8, :]
                    if i >= 6:
                        pe.wait_ge(low2_made, i - 6 + 1)
                    for k in range(KT):
                        nc.tensor.matmul(o, w2[:, k, c * P:(c + 1) * P], xB[:, k, NTOK * n:NTOK * (n + 1)],
                                         start=(k == 0), stop=False)
                    pe.wait_ge(low2_made, 2)
                    for g in range(2 * n, 2 * n + 2):
                        last = nc.tensor.matmul(o[:, GTOK * (g % 2):GTOK * (g % 2) + GTOK], b2[:, g, c * P:(c + 1) * P],
                                                low[:, 1, GTOK * g:GTOK * (g + 1)], start=False, stop=(g == 2 * n + 1))
                    last.then_inc(lin2_done, 1)

            pe.wait_ge(x2_made, 2 * KT)
            for tile in range(TILES):
                o = bank[:, tile // 3, AR * (tile % 3):AR * (tile % 3) + AR]
                for k in range(KT):
                    last = nc.tensor.matmul(o, xA[:, k, tile * P:(tile + 1) * P], ar3[:, k, :],
                                            start=(k == 0), stop=(k == KT - 1))
            last.then_inc(hr_done, 1)
            for tile in range(TILES):
                if tile >= 2:
                    pe.wait_ge(xnat_made, tile - 1)
                for k in range(KT):
                    last = nc.tensor.transpose(bank[:, 3 + tile % 2, k * P:(k + 1) * P], xA[:, k, tile * P:(tile + 1) * P], ident[:])
                last.then_inc(x_turned, 1)
            def last_layer(tile):
                if tile >= 3:
                    pe.wait_ge(res_made, tile - 2)
                for k in range(KT):
                    nc.tensor.matmul(bank[:, 5 + tile % 3, :], xA[:, k, tile * P:(tile + 1) * P], w3[:, k, :],
                                     start=(k == 0), stop=False)

            def last_adapters(tile):
                pe.wait_ge(hgt_made, tile // 4 + 1)
                nc.tensor.matmul(bank[:, 5 + tile % 3, :], hgT[:, tile, :], b3, start=False, stop=True).then_inc(lin3_done, 1)

            for tile in range(3):
                last_layer(tile)
            for h in range(2):
                pe.wait_ge(hg_made, 4 * (h + 1))
                if h == 0:
                    pe.wait_ge(xnat_made, TILES)
                for tile in range(4 * h, 4 * h + 4):
                    last = nc.tensor.transpose(bank[:, 3 + h, P * (tile % 4):P * (tile % 4) + P], hg[:, tile, :], ident[:])
                last.then_inc(hg_turned, 1)
            for tile in range(TILES):
                if tile >= 3:
                    last_layer(tile)
                last_adapters(tile)

        @block.scalar
        def _(act):
            def square(n, tile):
                b, _ = bank_use("block", n, tile=tile)
                act.wait_ge(block_done, BLOCKS * tile + n + 1)
                i = 5 * tile + n
                act.wait_ge(summed, i)
                if not isinstance(tile, int) or tile > 0:
                    act.wait_ge(roped, i)
                nc.scalar.activation(squares(tile), mm[:, b], ACT.Square).then_inc(squared, 1)

            def read_v(tile, par):
                b, _ = bank_use("block", 5, tile=tile)
                act.wait_ge(block_done, BLOCKS * tile + 6)
                r = nc.scalar.copy(vN[:, par].rearrange("p g d -> p (g d)"), mm[:, b])
                r.then_inc(v_read, 1)
                act.wait_ge(v_read, tile + 1)
                act.sem_inc(bank_free[b], 1)

            def read_turned(m, tile, par):
                b, _ = bank_use("turn", m, tile=tile)
                act.wait_ge(turned, 5 * tile + m + 1)
                if m < 4:
                    nc.scalar.copy(qT[:, par, m].rearrange("p b (h t) -> p b h t", h=REP),
                                   mm[:, b].rearrange("p (h b t) -> p b h t", h=REP, b=SEQ_PER_TILE)
                                   ).then_inc(turn_read, 1)
                else:
                    if not isinstance(tile, int) or tile > 0:
                        act.wait_ge(own_k_in, SEQ_PER_TILE * tile)
                    nc.scalar.copy(kTn[:].rearrange("p b (g t) -> p b g t", g=HKH),
                                   mm[:, b].rearrange("p (g b t) -> p b g t", g=HKH, b=SEQ_PER_TILE)
                                   ).then_inc(turn_read, 1)
                act.wait_ge(turn_read, 5 * tile + m + 1)
                act.sem_inc(bank_free[b], 1)

            def place_own_keys(tile, b):
                if b == 0:
                    act.wait_ge(turn_read, 5 * tile + 5)
                if not (isinstance(tile, int) and tile == 0 and b < 2):
                    act.wait_ge(scored, HKH * (SEQ_PER_TILE * tile + b - 1))
                nc.scalar.copy(kc[:, b % 2, NPP, :], kTn[:, b]).then_inc(own_k_in, 1)

            def exps(s, k):
                act.wait_ge(masked, PAIRS * s + k + 1)
                nc.scalar.activation(probs[:, k % 2, 0:KEYS], probs[:, k % 2, 0:KEYS], ACT.Exp, bias=minv[:, k % 2:k % 2 + 1],
                                     scale=-1.0, accum_out=psum_[:, k % 2:k % 2 + 1]).then_inc(exped, 1)

            def read_o(s, k):
                b, g = k // HKH, k % HKH
                act.wait_ge(pv_done, PAIRS * s + k + 1)
                if k == 0:
                    act.wait_ge(oT_free, s + 1)
                nc.scalar.copy(oT_hi[:, REP * g:REP * g + REP, S * b:S * b + S],
                               o_ps[:, 0:P].rearrange("p (h t) -> p h t", h=REP)).then_inc(o_hi_made, 1)

            def read_pt(s, k):
                act.wait_ge(probs_turned, 2 + PAIRS * s + k + 1)
                b = k // HKH
                nc.scalar.copy(pT_own[S * b:S * b + S, b, k % 2, :], pt_ps[S * b:S * b + S, L:L + P]).then_inc(pt_read, 1)
                nc.scalar.copy(pT[:, k % 2], pt_ps[:, 0:L]).then_inc(pt_read, 1)

            def load_xt(tile):
                if isinstance(tile, int) and tile == 1:
                    act.wait_ge(block_done, BLOCKS)
                else:
                    act.wait_ge(xt_lo_made, tile - 1)
                act.dma_start(xt[:], t["xt"][bass.ds(tile % TILES, 1)].rearrange("o p k t -> (o p) k t")
                              ).then_inc(xt_in, 16)

            def split_xt(tile):
                act.wait_ge(xt_in, 16 * (tile + 1))
                act.wait_ge(block_done, BLOCKS * tile)
                nc.scalar.copy(xt_hi[:].rearrange("p k t -> p (k t)"), xt[:].rearrange("p k t -> p (k t)")
                               ).then_inc(xt_hi_made, 1)

            def wait_for_buffer(s, j, last):
                signal, count = product_before(s, j, last)
                if signal == "block_done":
                    act.wait_ge(block_done, count)
                elif signal == "out_done":
                    act.wait_ge(out_done, count)
                elif signal == "w_used":
                    act.wait_ge(w_used, count)

            def split_w(j, tile):
                n, k = divmod(j, KT)
                if k == 0:
                    act.wait_ge(w_in[n], 16 * (1 + tile // TILES))
                wait_for_buffer(tile - 1, j, False)
                nc.scalar.copy(w_hi[:, SPLIT_BUF[j]], wqkv[:, n, k]).then_inc(w_hi_made, 1)

            def split_wo(h, s, last):
                if h == 0:
                    act.wait_ge(wo_in, 16 * (1 + s // TILES))
                wait_for_buffer(s, head_split(h, last), last)
                nc.scalar.copy(w_hi[:, SPLIT_BUF[head_split(h, last)]], wo[:, h]).then_inc(w_hi_made, 1)

            def step(s, par, last=False, load=True):
                for k in range(PAIRS):
                    for j in splits_in_slot(k, last):
                        if j < head_split(0, last):
                            split_w(j, s + 1)
                        else:
                            split_wo(j - head_split(0, last), s, last)
                    if load and k == 15:
                        split_xt(s + 2)
                    if not last and k == turn_slot(4):
                        read_turned(4, s + 1, 1 - par)
                    if not last:
                        for n in range(BLOCKS):
                            if k == block_slots(n)[1]:
                                if n < 5:
                                    square(n, s + 1)
                                else:
                                    read_v(s + 1, 1 - par)
                    if k in (2, 6):
                        place_own_keys(s, 2 + k // 6)
                    if k in (13, 15) and not last:
                        place_own_keys(s + 1, k // 15)
                    if k + 2 < PAIRS:
                        exps(s, k + 2)
                    elif not last:
                        exps(s + 1, k + 2 - PAIRS)
                    read_o(s, k)
                    if k + 1 < PAIRS:
                        read_pt(s, k + 1)
                    elif not last:
                        read_pt(s + 1, 0)
                    if not last:
                        for m in range(4):
                            if turn_slot(m) == k:
                                read_turned(m, s + 1, 1 - par)
                    if k == 12 and load:
                        load_xt(s + 2)
                for h in range(3, HQH):
                    split_wo(h, s, last)
                if load:
                    for j in range(SPLIT_BUFS):
                        split_w(j, s + 2)

            act.sem_inc(o_free, 1)
            act.sem_inc(oT_free, 1)
            act.dma_start(seqlen_i, t["seqlen"]).then_inc(setup_in, 16)
            act.dma_start(seqtok_i, t["seqtok"]).then_inc(setup_in, 16)
            act.dma_start(spare[:, 16:16 + D // 2 + 1], t["const"][:, C_FREQ:C_FREQ + D // 2 + 1]).then_inc(setup_in, 16)
            act.dma_start(vpage_i, t["vpages"]).then_inc(setup_in, 16)
            act.dma_start(rope_w[:, 0, 0, :], t["qnorm"]).then_inc(setup_in, 16)
            act.dma_start(rope_w[:, 1, 0, :], t["knorm"]).then_inc(setup_in, 16)
            act.wait_ge(setup_v, 15)
            nc.scalar.activation(sin_t, red[:], ACT.Sin).then_inc(setup_a, 1)
            act.wait_ge(setup_v, 22)
            nc.scalar.activation(cos_t, trig[:], ACT.Sin).then_inc(setup_a, 1)
            act.wait_ge(zeroed, 3)
            act.wait_ge(tables_made, 1)
            for what, n in BANK_ORDER[:PROLOGUE_USES]:
                if what == "turn":
                    read_turned(n, 0, 0)
                elif n < 5:
                    square(n, 0)
                else:
                    read_v(0, 0)
            place_own_keys(0, 0)
            place_own_keys(0, 1)
            load_xt(1)
            for j in range(SPLIT_BUFS):
                split_w(j, 1)
            split_xt(1)
            exps(0, 0)
            exps(0, 1)
            read_pt(0, 0)
            with act.Fori(0, STEPS // 2 - 1) as i:
                step(2 * i, 0)
                step(2 * i + 1, 1)
            step(STEPS - 2, 0, load=False)
            step(STEPS - 1, 1, last=True, load=False)

            for tile in range(0, TILES, 2):
                act.wait_ge(y_turned, tile + 1)
                nc.scalar.copy(xA[:, :, tile * P:(tile + 1) * P],
                               bank[:, tile].rearrange("p (k t) -> p k t", k=KT)).then_inc(xa_made, 1)

            act.wait_ge(agu_in, 16 * B)
            act.wait_ge(out_done, STEPS)
            for g in range(GROUPS):
                nc.scalar.copy(*spread_group(a_gu_raw[:, :, 1], a_gu[:, 1, g], g, KT)).then_inc(au_spread, 1)

            act.wait_ge(y_turned, TILES)
            act.wait_ge(xa_made, TILES)
            for n in range(2):
                for k in range(KT):
                    cols = slice(NTOK * n, NTOK * (n + 1))
                    nc.scalar.copy(x_hi[:, k, cols], xA[:, k, cols]).then_inc(x_hi_made, 1)

            def split_f(f, j, w):
                if w == 0:
                    act.wait_ge(wf_in[j], 16 * ((f - j) // 2 + 1) if isinstance(f, int) else 8 * (f - j) + 16)
                if not isinstance(f, int) or f > 0:
                    act.wait_ge(gu_done, 4 * (f - 1) + 3 + w)
                nc.scalar.copy(w_f_hi[w][:].rearrange("p k m -> p (k m)"),
                               w_f[j][:, w].rearrange("p k m -> p (k m)")).then_inc(wf_hi_made, 1)

            def silu(f, j, m, more=True):
                for n in range(2):
                    act.wait_ge(gu_done, 4 * f + 2 * n + 1)
                    i = 2 * f + n
                    if not isinstance(f, int) or i >= 2:
                        act.wait_ge(act_made, i - 1)
                    nc.scalar.activation(gated[0:m, n, :], bank[0:m, 4 * (1 - j) + n, :], ACT.Silu).then_inc(silu_done, 1)
                    if more:
                        split_f(f + 1, 1 - j, n)

            split_f(0, 0, 0)
            split_f(0, 0, 1)
            silu(0, 0, P)
            silu(1, 1, P)
            with act.Fori(1, FT // 2) as i:
                silu(2 * i, 0, P)
                silu(2 * i + 1, 1, P)
            silu(FT - 1, 0, FLAST, more=False)

            for tile in range(TILES):
                act.wait_ge(x_turned, tile + 1)
                nc.scalar.copy(xnat[:, tile, :], bank[:, 3 + tile % 2, :]).then_inc(xnat_made, 1)
            act.wait_ge(rv, 12)
            nc.scalar.activation(route1[3], route1[2], ACT.Exp).then_inc(ratio_done, 1)
            for h in range(2):
                act.wait_ge(hg_turned, h + 1)
                nc.scalar.copy(hgT[:, 4 * h:4 * h + 4, :], bank[:, 3 + h].rearrange("p (t c) -> p t c", t=4)).then_inc(hgt_made, 1)

        @block.vector
        def _(dve):
            def norm_rows(n, tile):
                b, _ = bank_use("block", n, tile=tile)
                i = 5 * tile + n
                dve.wait_ge(squared, i + 1)
                nc.vector.tensor_reduce(ss, squares(tile).rearrange("p (h d) -> p h d", h=4), AX.X, ALU.add).then_inc(summed, 1)
                dve.wait_ge(summed, i + 1)
                nc.vector.tensor_scalar(var, ss, 1.0 / D, ATT_EPS, ALU.mult, ALU.add).then_inc(var_made, 1)

            def scale_rows(n, tile):
                b, _ = bank_use("block", n, tile=tile)
                i = 5 * tile + n
                dve.wait_ge(rstd_made, i + 1)
                dve.wait_ge(sin_done, i)
                dve.wait_ge(cos_done, i)
                nc.vector.tensor_tensor(tq[:].rearrange("p (h d) -> p h d", h=4),
                                        mm[:, b].rearrange("p (h d) -> p h d", h=4),
                                        rstd.unsqueeze(2).to_broadcast([P, 4, D]), ALU.mult).then_inc(scaled, 1)
                dve.wait_ge(scaled, i + 1)
                dve.sem_inc(bank_free[b], 1)

            def rope_cos(n, tile):
                i = 5 * tile + n
                dve.wait_ge(roped, i)
                if n == 0:
                    dve.wait_ge(tab_made, 4 * (tile + 1))
                nc.vector.tensor_tensor(rc[:].rearrange("p (h d) -> p h d", h=4),
                                        tq[:].rearrange("p (h d) -> p h d", h=4),
                                        tab[:, n // 4, 0:1, :].to_broadcast([P, 4, D]), ALU.mult).then_inc(cos_done, 1)

            def make_mask(tile, b):
                i = SEQ_PER_TILE * tile + b
                col = seqlen[:, bass.ds((SEQ_PER_TILE * tile + b) % B, 1)]
                nc.vector.tensor_scalar(mask[:, 0:L], keyno[:], col, NEG, ALU.is_ge, ALU.mult).then_inc(mask_made, 1)

            def mask_scores(s, k):
                b = k // HKH
                dve.wait_ge(scored, PAIRS * s + k + 1)
                if k % HKH == 0:
                    dve.wait_ge(mask_made, SEQ_PER_TILE * s + b + 1)
                dve.wait_ge(probs_turned, PAIRS * s + k + 1)
                dve.sem_inc(vector_went_on, 1)
                nc.vector.tensor_tensor_reduce(out=probs[:, k % 2, 0:KEYS], in0=sc[:, SC0:SC0 + KEYS], in1=mask[:],
                                               scale=-SCALE, scalar=BIG, op0=ALU.add, op1=ALU.min,
                                               accum_out=minv[:, k % 2:k % 2 + 1]).then_inc(masked, 1)

            def norm_probs(s, k):
                dve.wait_ge(exped, PAIRS * s + k + 1)
                nc.vector.reciprocal(rinv[:, k % 2:k % 2 + 1], psum_[:, k % 2:k % 2 + 1]).then_inc(inverted, 1)
                dve.wait_ge(inverted, PAIRS * s + k + 1)
                nc.vector.tensor_scalar(probs[:, k % 2, 0:KEYS], probs[:, k % 2, 0:KEYS], rinv[:, k % 2:k % 2 + 1], None,
                                        ALU.mult).then_inc(normed, 1)

            def add_y(s, last):
                b, _ = bank_use("out", 0, step=s, last=last)
                dve.wait_ge(out_done, s + 1)
                dve.sem_inc(oT_free, 1)
                yt = y[:, bass.ds(s % TILES, 1), :].rearrange("p o h -> p (o h)")
                nc.vector.tensor_tensor(yt, mm[:, b], yt, ALU.add).then_inc(y_added, 1)
                dve.wait_ge(y_added, s + 1)
                dve.sem_inc(bank_free[b], 1)

            def split_xt(tile):
                dve.wait_ge(xt_hi_made, tile)
                nc.vector.tensor_tensor(xt_lo[:].rearrange("p k t -> p (k t)"), xt[:].rearrange("p k t -> p (k t)"),
                                        xt_hi[:].rearrange("p k t -> p (k t)").bitcast(F32), ALU.subtract
                                        ).then_inc(xt_lo_made, 1)

            def split_w(j, tile):
                n, k = divmod(j, KT)
                dve.wait_ge(w_hi_made, SPLITS * (tile - 1) + j + 1)
                nc.vector.tensor_tensor(w_lo[:, SPLIT_BUF[j]], wqkv[:, n, k], w_hi[:, SPLIT_BUF[j]].bitcast(F32),
                                        ALU.subtract).then_inc(w_lo_made, 1)

            def split_wo(h, s, last):
                j = head_split(h, last)
                dve.wait_ge(w_hi_made, SPLITS * s + j + 1)
                nc.vector.tensor_tensor(w_lo[:, SPLIT_BUF[j]], wo[:, h], w_hi[:, SPLIT_BUF[j]].bitcast(F32),
                                        ALU.subtract).then_inc(w_lo_made, 1)

            def split(s, j, last):
                if j < head_split(0, last):
                    split_w(j, s + 1)
                else:
                    split_wo(j - head_split(0, last), s, last)

            def split_o(s, k):
                b, g = k // HKH, k % HKH
                dve.wait_ge(o_hi_made, PAIRS * s + k + 1)
                heads = (slice(None), slice(REP * g, REP * g + REP), slice(S * b, S * b + S))
                nc.vector.tensor_tensor(oT_lo[heads], o_ps[:, 0:P].rearrange("p (h t) -> p h t", h=REP),
                                        oT_hi[heads].bitcast(F32), ALU.subtract).then_inc(o_free, 1)

            def step(s, par, last=False, load=True):
                for k in range(PAIRS):
                    if k > 0:
                        split_o(s, k - 1)
                    if k + 1 < PAIRS:
                        norm_probs(s, k + 1)
                    elif not last:
                        norm_probs(s + 1, 0)
                    if k + 2 < PAIRS:
                        mask_scores(s, k + 2)
                    elif not last:
                        mask_scores(s + 1, k + 2 - PAIRS)
                    for j in splits_in_slot(k, last)[:1]:
                        split(s, j, last)
                    for j in splits_in_slot(k, last)[1:]:
                        split(s, j, last)
                    if (k + 3) % HKH == 0 and not (last and k + 3 >= PAIRS):
                        dve.wait_ge(masked, PAIRS * s + k + 3)
                        make_mask(s + (k + 3) // PAIRS, (k + 3) % PAIRS // HKH)
                    if not last:
                        for n in range(5):
                            if k == 2 * n + 2:
                                scale_rows(n, s + 1)
                    if load and k == 15:
                        split_xt(s + 2)
                    if not last:
                        for n in range(5):
                            if k == 2 * n + 1:
                                norm_rows(n, s + 1)
                            if k == 2 * n + 2:
                                rope_cos(n, s + 1)
                split_o(s, PAIRS - 1)
                for h in range(3, HQH):
                    split_wo(h, s, last)
                if load:
                    for j in range(SPLIT_BUFS):
                        split_w(j, s + 2)
                add_y(s, last)

            n_setup = [0]

            def chain(ins):
                n_setup[0] += 1
                ins.then_inc(setup_v, 1)
                dve.wait_ge(setup_v, n_setup[0])

            dve.wait_ge(setup_in, 16 * 6)
            chain(nc.vector.tensor_copy(vpage, vpage_i))
            chain(nc.vector.tensor_scalar(vpage, vpage, float(PSIZE), step_, ALU.mult, ALU.add))
            for half in range(HALVES):
                chain(nc.vector.tensor_scalar(vrow[:, B * half:B * (half + 1)].rearrange("p b c -> p (b c)"), vpage,
                                              float(half * PAGES * PSIZE), None, ALU.add))
            dve.sem_inc(vrow_made, 1)
            chain(nc.vector.tensor_copy(seqlen, seqlen_i))
            chain(nc.vector.tensor_copy(pos, seqtok_i))
            chain(nc.vector.tensor_scalar(pos, pos, step_, None, ALU.add))
            halfd = D // 2
            a3, t3 = (x[:].rearrange("p (t f) -> p t f", t=TILES) for x in (ang, turns))
            chain(nc.vector.tensor_tensor(a3, pos.unsqueeze(2).to_broadcast([P, TILES, halfd]),
                                          freq.unsqueeze(1).to_broadcast([P, TILES, halfd]), ALU.mult))

            def reduce_angle(dst, quarter):
                chain(nc.vector.tensor_scalar(turns[:], ang[:], 1.0 / (2.0 * PI), quarter, ALU.mult, ALU.add))
                chain(nc.vector.tensor_scalar(turns[:], turns[:], ROUND, -ROUND, ALU.add, ALU.add))
                src = ang
                for part in (TWO_PI_1, TWO_PI_2, TWO_PI_3):
                    chain(nc.vector.scalar_tensor_tensor(out=dst[:], in0=turns[:], scalar=-part, in1=src[:],
                                                         op0=ALU.mult, op1=ALU.add))
                    src = dst
                chain(nc.vector.tensor_scalar(dst[:], dst[:], 2 * PI * quarter, PI_SAFE, ALU.add, ALU.min))
                chain(nc.vector.tensor_scalar(dst[:], dst[:], -PI_SAFE, None, ALU.max))

            reduce_angle(red, 0.0)
            reduce_angle(trig, 0.25)
            assert n_setup[0] == 22
            dve.wait_ge(setup_a, 2)
            chain(nc.vector.tensor_scalar(rope_w[:, :, 1, 0:halfd], rope_w[:, :, 0, halfd:D], -1.0, None, ALU.mult))
            chain(nc.vector.tensor_copy(rope_w[:, :, 1, halfd:D], rope_w[:, :, 0, 0:halfd]))
            chain(nc.vector.memset(halfs, -0.5))
            dve.sem_inc(tables_made, 1)

            dve.wait_ge(keyno_in, 16)
            dve.wait_ge(zeroed, 3)
            make_mask(0, 0)
            for n in range(5):
                norm_rows(n, 0)
                scale_rows(n, 0)
                rope_cos(n, 0)
            mask_scores(0, 0)
            norm_probs(0, 0)
            mask_scores(0, 1)
            dve.wait_ge(y_in, 16)
            for j in range(SPLIT_BUFS):
                split_w(j, 1)
            split_xt(1)
            with dve.Fori(0, STEPS // 2 - 1) as i:
                step(2 * i, 0)
                step(2 * i + 1, 1)
            step(STEPS - 2, 0, load=False)
            step(STEPS - 1, 1, last=True, load=False)

            for tile in range(1, TILES, 2):
                dve.wait_ge(y_turned, tile + 1)
                nc.vector.tensor_copy(xA[:, :, tile * P:(tile + 1) * P],
                                      bank[:, tile].rearrange("p (k t) -> p k t", k=KT)).then_inc(xa_made, 1)

            own2 = own[:].unsqueeze(1).to_broadcast([P, 2, GTOK])

            dve.wait_ge(const_in, 16 * 2)

            def keep_own(i, src, dst, scale, done, made):
                dve.wait_ge(done, i)
                nc.vector.scalar_tensor_tensor(out=dst.rearrange("p (g t) -> p g t", g=2),
                                               in0=src.rearrange("p (g t) -> p g t", g=2), scalar=scale, in1=own2,
                                               op0=ALU.mult, op1=ALU.mult).then_inc(made, 1)

            def low_part(n, k):
                cols = slice(NTOK * n, NTOK * (n + 1))
                dve.wait_ge(x_hi_made, KT * n + k + 1)
                nc.vector.tensor_tensor(x_lo[:, k, cols], xA[:, k, cols], x_hi[:, k, cols].bitcast(F32),
                                        ALU.subtract).then_inc(x_lo_made, 1)

            def split_f(f, j, w):
                dve.wait_ge(wf_hi_made, 2 * f + w + 1)
                nc.vector.tensor_tensor(w_f_lo[w][:].rearrange("p k m -> p (k m)"),
                                        w_f[j][:, w].rearrange("p k m -> p (k m)"),
                                        w_f_hi[w][:].rearrange("p k m -> p (k m)").bitcast(F32),
                                        ALU.subtract).then_inc(wf_lo_made, 1)

            dve.wait_ge(low_done, 4)
            split_f(0, 0, 0)
            for k in range(KT):
                low_part(0, k)
            split_f(0, 0, 1)
            for w in range(2):
                for h in range(2):
                    keep_own(2 * w + h + 1, bank[:, 2 * w + h, :], low[:, w, NTOK * h:NTOK * (h + 1)], 0.5,
                             low_done, low_made)

            for k in range(KT):
                low_part(1, k)

            def gate_times_up(f, j, m, more=True):
                for n in range(2):
                    dve.wait_ge(gu_done, 4 * f + 2 * n + 2)
                    dve.wait_ge(silu_done, 2 * f + n + 1)
                    nc.vector.tensor_tensor(act_t[0:m, bass.ds(f, 1), NTOK * n:NTOK * (n + 1)].rearrange("p o t -> p (o t)"),
                                            gated[0:m, n, :], bank[0:m, 4 * (1 - j) + 2 + n, :], ALU.mult).then_inc(act_made, 1)
                    if more:
                        split_f(f + 1, 1 - j, n)

            gate_times_up(0, 0, P)
            gate_times_up(1, 1, P)
            with dve.Fori(1, FT // 2) as i:
                gate_times_up(2 * i, 0, P)
                gate_times_up(2 * i + 1, 1, P)
            gate_times_up(FT - 1, 0, FLAST, more=False)

            for h in range(2):
                keep_own(4 + h + 1, bank[:, h, :], low[:, 0, NTOK * h:NTOK * (h + 1)], 0.5, low_done, low_made)
            for c in range(KT):
                for n in range(2):
                    i = 2 * c + n
                    dve.wait_ge(down_done, i + 1)
                    cols = slice(NTOK * n, NTOK * (n + 1))
                    nc.vector.tensor_tensor(xA[:, c, cols], bank[:, (i + 2) % 8, :],
                                            x_lo[:, c, cols].bitcast(F32), ALU.add).then_inc(x_lo_added, 1)
                    dve.wait_ge(x_lo_added, i + 1)
                    nc.vector.tensor_tensor(xB[:, c, cols], xA[:, c, cols],
                                            x_hi[:, c, cols].bitcast(F32), ALU.add).then_inc(xb_made, 1)
            for h in range(2):
                keep_own(h + 1, bank[:, h, :], low[:, 1, NTOK * h:NTOK * (h + 1)], 2.0, low2_done, low2_made)
            dve.wait_ge(l23_in, L23_ALL)
            for c in range(KT):
                for n in range(2):
                    i = 2 * c + n
                    dve.wait_ge(lin2_done, i + 1)
                    if i == 0:
                        dve.wait_ge(xb_made, 2 * KT)
                    nc.vector.scalar_tensor_tensor(out=xA[:, c, NTOK * n:NTOK * (n + 1)], in0=bank[:, (i + 2) % 8, :],
                                                   scalar=bias2[:, c:c + 1], in1=xB[:, c, NTOK * n:NTOK * (n + 1)],
                                                   op0=ALU.add, op1=ALU.add).then_inc(x2_made, 1)

            n_rv = [0]

            def link(ins):
                n_rv[0] += 1
                ins.then_inc(rv, 1)
                dve.wait_ge(rv, n_rv[0])

            def over_e(v):
                return v.unsqueeze(2).to_broadcast([P, TILES, E3])

            def over_t(v):
                return v.unsqueeze(1).to_broadcast([P, TILES, E3])

            logits, bias, eq, pick1, rest_, pick2, gates, tmp = route
            m1, m2, diff, ratio, den, w1, w2_, first = route1
            expert, firstness = small[:, 0:E3], small[:, E3:2 * E3]
            link(nc.vector.tensor_copy(lang, lang_i))
            link(nc.vector.tensor_tensor(bias, over_t(expert), over_e(lang), ALU.is_equal))
            dve.wait_ge(hr_done, 1)
            for tile in range(TILES):
                c0 = AR * (tile % 3) + E3 * RANK
                ins = nc.vector.scalar_tensor_tensor(out=logits[:, tile, :], in0=bias[:, tile, :], scalar=5.0,
                                                     in1=bank[:, tile // 3, c0:c0 + E3], op0=ALU.mult, op1=ALU.add)
            link(ins)
            link(nc.vector.tensor_reduce(m1, logits, AX.X, ALU.max))

            def pick(out, values_, top):
                link(nc.vector.tensor_tensor(eq, values_, over_e(top), ALU.is_equal))
                link(nc.vector.tensor_tensor(eq, eq, over_t(firstness), ALU.mult))
                link(nc.vector.tensor_reduce(first, eq, AX.X, ALU.max))
                link(nc.vector.tensor_tensor(out, eq, over_e(first), ALU.is_equal))

            pick(pick1, logits, m1)
            link(nc.vector.scalar_tensor_tensor(out=rest_, in0=pick1, scalar=NEG, in1=logits, op0=ALU.mult, op1=ALU.add))
            link(nc.vector.tensor_reduce(m2, rest_, AX.X, ALU.max))
            link(nc.vector.tensor_tensor(diff, m2, m1, ALU.subtract))
            assert n_rv[0] == 11
            dve.sem_inc(rv, 1)
            n_rv[0] += 1
            pick(pick2, rest_, m2)
            dve.wait_ge(ratio_done, 1)
            link(nc.vector.tensor_scalar(den, ratio, 1.0, None, ALU.add))
            link(nc.vector.reciprocal(w1, den))
            link(nc.vector.tensor_scalar(w1, w1, 2.0, None, ALU.mult))
            link(nc.vector.tensor_tensor(w2_, w1, ratio, ALU.mult))
            link(nc.vector.tensor_tensor(gates, pick1, over_e(w1), ALU.mult))
            link(nc.vector.tensor_tensor(tmp, pick2, over_e(w2_), ALU.mult))
            link(nc.vector.tensor_tensor(gates, gates, tmp, ALU.add))
            for tile in range(TILES):
                c0 = AR * (tile % 3)
                nc.vector.tensor_tensor(hg[:, tile, :].rearrange("p (e r) -> p e r", e=E3),
                                        bank[:, tile // 3, c0:c0 + E3 * RANK].rearrange("p (e r) -> p e r", e=E3),
                                        gates[:, tile, :].unsqueeze(2).to_broadcast([P, E3, RANK]), ALU.mult
                                        ).then_inc(hg_made, 1)
            for tile in range(TILES):
                dve.wait_ge(lin3_done, tile + 1)
                dve.wait_ge(xnat_made, tile + 1)
                nc.vector.tensor_tensor(res[:, tile, :], bank[:, 5 + tile % 3, :], xnat[:, tile, :], ALU.add).then_inc(res_made, 1)

        @block.gpsimd
        def _(pool):
            def root(i):
                pool.wait_ge(var_made, i + 1)
                nc.gpsimd.tensor_tensor(rstd, var, halfs, ALU.pow).then_inc(rstd_made, 1)

            def make_tab(tile):
                if not isinstance(tile, int) or tile > 0:
                    pool.wait_ge(roped, 5 * tile)
                pool.sem_inc(pool_went_on, 1)
                for w in range(2):
                    for c in range(2):
                        nc.gpsimd.tensor_tensor(tab[:, w, c, :].rearrange("p (h f) -> p h f", h=2),
                                                angles[:, c, bass.ds(tile % TILES, 1), :].to_broadcast([P, 2, D // 2]),
                                                rope_w[:, w, c, :].rearrange("p (h f) -> p h f", h=2),
                                                ALU.mult).then_inc(tab_made, 1)

            def rope_sin(n, tile):
                i = 5 * tile + n
                half = D // 2
                if n == 0:
                    pool.wait_ge(tab_made, 4 * (tile + 1))
                pool.wait_ge(scaled, i + 1)
                pool.wait_ge(roped, i)
                pool.sem_inc(pool_went_on, 1)
                t3 = tq[:].rearrange("p (h d) -> p h d", h=4)
                r3 = rs[:].rearrange("p (h d) -> p h d", h=4)
                stab = tab[:, n // 4, 1:2, :]
                nc.gpsimd.tensor_tensor(r3[:, :, 0:half], t3[:, :, half:D],
                                        stab[:, :, 0:half].to_broadcast([P, 4, half]), ALU.mult)
                nc.gpsimd.tensor_tensor(r3[:, :, half:D], t3[:, :, 0:half],
                                        stab[:, :, half:D].to_broadcast([P, 4, half]), ALU.mult).then_inc(sin_done, 1)
                pool.wait_ge(sin_done, i + 1)
                pool.wait_ge(cos_done, i + 1)
                pool.wait_ge(turned, i)
                nc.gpsimd.tensor_tensor(qn[:], rc[:], rs[:], ALU.add).then_inc(roped, 1)

            def gather_v(c, parity):
                ready_v(c, parity)
                gather_chunks(parity, range(CHUNKS))

            def gather_chunks(parity, chunks):
                for i in chunks:
                    nc.gpsimd.indirect_dma_start(
                        out=vc[:, parity, i, :], out_offset=None, in_=t["vcache"],
                        in_offset=bass.IndirectOffsetOnAxis(ap=vrow_now[:, parity, i:i + 1].bitcast(mybir.dt.uint32), axis=0)
                    ).then_inc(v_in[parity], 16)

            def ready_v(c, parity):
                if isinstance(c, int) and c < 2:
                    nc.gpsimd.tensor_copy(vrow_now[:, parity], vrow[:, c]).then_inc(vrow_ready, 1)
                else:
                    pool.wait_ge(pv_done, HKH * (c - 1))
                    pool.wait_ge(v_in[parity], 16 * CHUNKS * ((c - parity) // 2) if isinstance(c, int) else
                                 8 * CHUNKS * (c - parity))
                    pool.sem_inc(pool_went_on, 1)
                    nc.gpsimd.tensor_copy(vrow_now[:, parity],
                                          vrow[:, bass.ds(c, 1)].rearrange("p o c -> p (o c)")).then_inc(vrow_ready, 1)
                pool.wait_ge(vrow_ready, c + 1)
                pool.sem_inc(pool_went_on, 1)

            nc.gpsimd.memset(mask[:, L:KEYS], 0.0).then_inc(zeroed, 1)
            nc.gpsimd.memset(probs[:, :, KEYS:L + P], 0.0).then_inc(zeroed, 1)
            nc.gpsimd.memset(pT_own[:], 0.0).then_inc(zeroed, 1)
            pool.wait_ge(vrow_made, 1)
            gather_v(0, 0)
            gather_v(1, 1)
            pool.wait_ge(tables_made, 1)
            make_tab(0)
            for n in range(5):
                root(n)
                rope_sin(n, 0)
            make_tab(1)
            with pool.Fori(1, STEPS) as tile:
                for n in range(5):
                    root(5 * tile + n)
                    if n in (1, 3):
                        ready_v(SEQ_PER_TILE * tile - 2 + n // 2, n // 2)
                        gather_chunks(n // 2, range(CHUNKS // 2))
                    if n in (2, 4):
                        gather_chunks(n // 2 - 1, range(CHUNKS // 2, CHUNKS))
                    rope_sin(n, tile)
                make_tab(tile + 1)
                for j in range(2):
                    gather_v(SEQ_PER_TILE * tile + j, j)
            for j in range(2):
                gather_v(HALVES * B - 2 + j, j)

            pool.wait_ge(agu_in, 16 * B)
            for g in range(GROUPS):
                nc.gpsimd.tensor_copy(*spread_group(a_gu_raw[:, :, 0], a_gu[:, 0, g], g, KT)).then_inc(ag_spread, 1)
            for h in range(2):
                pool.wait_ge(ad_in, 16 * (B // 2) * (h + 1))
                for g in range(GROUPS // 2):
                    nc.gpsimd.tensor_copy(*spread_group(a_d_raw, a_d[:, h * GROUPS // 2 + g], g, FT)).then_inc(ad_spread, 1)
            pool.wait_ge(a2_in, 16 * B)
            for j in range(2):
                pool.wait_ge(bf_in[j], 16 * ((FT + 1 - j) // 2))
            for g in range(GROUPS):
                nc.gpsimd.tensor_copy(*spread_group(a2_raw, a2[:, g], g, KT)).then_inc(a2_spread, 1)


def kernel(**inputs):
    import numpy as _np
    import concourse.bacc as _bacc
    from concourse import mybir as _mybir
    from concourse.bass_utils import run_bass_kernel_spmd as _run

    a = {k: _np.asarray(v) for k, v in inputs.items()}
    x = a["x"].reshape(TOK, HID)

    def by_k(w):
        return w.T.reshape(-1, P, w.shape[0]).transpose(1, 0, 2)

    wq, wk, wv, wo = (a["L0_cond_" + n] for n in ("Wq", "Wk", "Wv", "Wo"))
    wqkv = _np.stack([_np.stack(
        [by_k(wq[h * HQH * D + n * 512:h * HQH * D + (n + 1) * 512]) for n in range(4)]
        + [by_k(w[h * HKH * D:(h + 1) * HKH * D]) for w in (wk, wv)]) for h in range(HALVES)])
    f_pad = FT * P - F

    def rows_f(w):
        w = _np.pad(w, ((0, f_pad), (0, 0)))
        return w.reshape(FT, P, KT, P).transpose(0, 3, 2, 1)

    def low_rank(w, n):
        return w.reshape(w.shape[0], RANK, n, P).transpose(0, 3, 2, 1).reshape(w.shape[0], P, n * RANK)

    l1 = {k[len("L1_cond_"):]: v for k, v in a.items() if k.startswith("L1_cond_")}
    seq = a["itok_B_207_1644"]
    arrays = {
        "x": x.reshape(TILES, P, HID).transpose(1, 0, 2),
        "xt": x.reshape(TILES, P, KT, P).transpose(0, 3, 2, 1),
        "wqkv": wqkv,
        "wo": wo.T.reshape(HALVES, HQH, D, HID).transpose(0, 2, 1, 3),
        "kcache": a["L0_cond_k_cache"].reshape(PAGES, PSIZE, HALVES, HKH, D).transpose(2, 0, 4, 3, 1).reshape(
            HALVES, PAGES, D, HKH * PSIZE),
        "vcache": a["L0_cond_v_cache"].reshape(PAGES * PSIZE, HALVES, HKH * D).transpose(1, 0, 2).reshape(
            HALVES * PAGES * PSIZE, HKH * D),
        "vpages": _np.repeat(a["itok_Bx16_0_63"].reshape(B, CHUNKS, P // PSIZE), PSIZE, axis=2).transpose(2, 0, 1).reshape(
            P, B * CHUNKS),
        "table": a["itok_Bx16_0_63"],
        "seqlen": _np.broadcast_to(seq[None, :], (P, B)),
        "seqtok": _np.repeat(seq, S).reshape(TILES, P).T,
        "qnorm": _np.broadcast_to(a["L0_cond_q_norm_w"][None, :], (P, D)),
        "knorm": _np.broadcast_to(a["L0_cond_k_norm_w"][None, :], (P, D)),
        "const": constants(),
        "ids": _np.concatenate([a["itok_B_2_6"], a["itok_B_0_23"]])[None, :],
        "w_gu": _np.stack([rows_f(l1["W_gate"]), rows_f(l1["W_up"])], axis=2).reshape(FT, P, 2 * KT * P),
        "a_gu": _np.concatenate([low_rank(l1["A_gate"][0], KT), low_rank(l1["A_up"][0], KT)], axis=2),
        "b_gu": _np.concatenate([l1["B_gate"][0].transpose(0, 2, 1), l1["B_up"][0].transpose(0, 2, 1)], axis=2),
        "w_d": _np.pad(l1["W_down"].T, ((0, f_pad), (0, 0))).reshape(FT, P, HID).transpose(1, 0, 2),
        "a_d": low_rank(_np.pad(l1["A_down"][0], ((0, 0), (0, 0), (0, f_pad))), FT),
        "b_d": l1["B_down"][0].transpose(0, 2, 1),
        "w2": by_k(a["L2_cond_W"]),
        "bias2": a["L2_cond_b"].reshape(KT, P).T,
        "a2": a["L2_cond_lora_As"].reshape(B, KT, P, RANK).transpose(0, 2, 1, 3).reshape(B, P, KT * RANK),
        "b2": a["L2_cond_lora_Bs"],
        "w3": by_k(a["L3_cond_W"]),
        "ar3": by_k(_np.concatenate([a["L3_cond_A"].reshape(E3 * RANK, HID), a["L3_cond_Wr"]])),
        "b3": a["L3_cond_B"].transpose(0, 2, 1).reshape(E3 * RANK, HID),
        "lang": _np.repeat(a["itok_B_0_7"], S).reshape(TILES, P).T,
    }
    arrays = {f"in_{k}": _np.ascontiguousarray(v) for k, v in arrays.items()}
    nc = _bacc.Bacc("TRN2", target_bir_lowering=False, num_devices=1, dynamic_dma_scratch_size=3072)
    t = {k[3:]: nc.dram_tensor(k, v.shape, _mybir.dt.from_np(v.dtype), kind="ExternalInput").ap()
         for k, v in arrays.items()}
    t["out"] = nc.dram_tensor("out", (P, TILES, HID), F32, kind="ExternalOutput").ap()
    build(nc, t)
    r = _run(nc, [arrays], core_ids=[0])
    return r.results[0]["out"].transpose(1, 0, 2).reshape(B, S, HID)
```
